# Optimizing a Trainium2 kernel written in Bass

```python
import numpy as np
import jax
import jax.numpy as jnp

def _softmax(x, axis=-1):
    return jax.nn.softmax(x, axis=axis)

def _gelu(x):
    return jax.nn.gelu(x, approximate=True)

def _silu(x):
    return jax.nn.silu(x)

def _sigmoid(x):
    return jax.nn.sigmoid(x)

def _layernorm(x, axis=-1, eps=1e-05):
    m = jnp.mean(x, axis=axis, keepdims=True)
    v = jnp.var(x, axis=axis, keepdims=True)
    return (x - m) / jnp.sqrt(v + eps)

def _scatter_add(tgt, idx, src, axis=0):
    return tgt.at[idx].add(src)

def _segment_sum(src, seg, n):
    return jax.ops.segment_sum(src, seg, n)
kernel_name = 'mk_gps_d2_gnn_r16_9a1049'

def setup_inputs(seed: int=0):
    np.random.seed(seed)
    _w = jnp.asarray

    def _rec_inputs():
        import jax
        import jax.numpy as jnp
        _gk = jax.random.key(seed)
        x = -0.0003713 + 1 * jax.random.normal(jax.random.fold_in(_gk, 1), (3125, 256), jnp.float32)
        src = jax.random.randint(jax.random.fold_in(_gk, 2), (100000,), 0, 3125, jnp.int32)
        dst = jnp.minimum((3125 * jax.random.uniform(jax.random.fold_in(_gk, 3), (100000,)) ** 2.0).astype(jnp.int32), 49999)
        _o = jnp.argsort(dst, stable=True)
        src = src[_o]
        dst = dst[_o]
        edge_attr_128 = -5.16925e-05 + 1.00005 * jax.random.normal(jax.random.fold_in(_gk, 12), (100000, 128), jnp.float32)
        edge_type_8 = jax.random.randint(jax.random.fold_in(_gk, 14), (100000,), 0, 8, jnp.int32)
        node_type_4 = jax.random.randint(jax.random.fold_in(_gk, 15), (3125,), 0, 4, jnp.int32)
        return (x, src, dst, edge_attr_128, edge_type_8, node_type_4)
    x, src, dst, edge_attr_128, edge_type_8, node_type_4 = _rec_inputs()

    def _L0_gnn_setup():
        import jax, jax.numpy as jnp
        import numpy as np
        N_NODES = 3125
        N_EDGES = 50000
        IN_DIM = 256
        OUT_DIM = 256
        HEADS = 1
        EDGE_DIM = 128
        NEG_SLOPE = 0.01
        key = jax.random.key(seed)
        ks = jax.random.split(key, 8)
        x = jax.random.normal(ks[0], (N_NODES, IN_DIM), dtype=jnp.float32)
        edge_index = jax.random.randint(ks[1], (2, N_EDGES), 0, N_NODES, dtype=jnp.int64)
        edge_attr = jax.random.normal(ks[2], (N_EDGES, EDGE_DIM), dtype=jnp.float32)
        hc = HEADS * OUT_DIM
        Wn = jax.random.normal(ks[3], (hc, IN_DIM), dtype=jnp.float32) / np.sqrt(IN_DIM)
        bn = jnp.zeros((hc,), dtype=jnp.float32)
        We = jax.random.normal(ks[4], (hc, EDGE_DIM), dtype=jnp.float32) / np.sqrt(EDGE_DIM)
        be = jnp.zeros((hc,), dtype=jnp.float32)
        attn = jax.random.normal(ks[5], (1, HEADS, OUT_DIM), dtype=jnp.float32) * np.sqrt(2.0 / (HEADS * OUT_DIM + 1))
        return {'x': x, 'edge_index': edge_index, 'edge_attr': edge_attr, 'Wn': Wn, 'bn': bn, 'We': We, 'be': be, 'attn': attn}
    _L0_gnn_all = _L0_gnn_setup()
    _L0_gnn_in = {k: v for k, v in _L0_gnn_all.items() if k in ('Wn', 'bn', 'We', 'be', 'attn')}
    del _L0_gnn_all

    def _L0_mix_setup():
        import jax, jax.numpy as jnp
        import numpy as np
        C_CURV = 1.0
        MIN_NORM = 1e-15
        BALL_EPS = 1e-05
        ATT_EPS = 1e-15
        DIM = 32

        def _norm(x):
            return jnp.clip(jnp.linalg.norm(x, axis=-1, keepdims=True), MIN_NORM)

        def proj(x, c):
            maxnorm = (1.0 - BALL_EPS) / jnp.sqrt(c)
            n = _norm(x)
            return jnp.where(n > maxnorm, x / n * maxnorm, x)

        def expmap0(u, c):
            sc = jnp.sqrt(c)
            n = _norm(u)
            return jnp.tanh(sc * n) * u / (sc * n)

        def logmap0(p, c):
            sc = jnp.sqrt(c)
            n = _norm(p)
            return jnp.arctanh(jnp.clip(sc * n, -1.0 + 1e-07, 1.0 - 1e-07)) * p / (sc * n)

        def mobius_add(x, y, c):
            x2 = jnp.sum(x * x, -1, keepdims=True)
            y2 = jnp.sum(y * y, -1, keepdims=True)
            xy = jnp.sum(x * y, -1, keepdims=True)
            num = (1 + 2 * c * xy + c * y2) * x + (1 - c * x2) * y
            den = 1 + 2 * c * xy + c * c * x2 * y2
            return num / jnp.clip(den, MIN_NORM)

        def conv1d(x, w, pad, groups=1):
            return jax.lax.conv_general_dilated(x, w, (1,), [(pad, pad)], dimension_numbers=('NCH', 'OIH', 'NCH'), feature_group_count=groups)

        def batchnorm(x, gamma, beta):
            mean = jnp.mean(x, axis=(0, 2), keepdims=True)
            var = jnp.var(x, axis=(0, 2), keepdims=True)
            xn = (x - mean) * jax.lax.rsqrt(var + 1e-05)
            return gamma[None, :, None] * xn + beta[None, :, None]

        def _reference_tuple_inner(x, w_qkv, bn_gamma, bn_beta, w_dw, w_pw, w_res, b_res):
            c = C_CURV
            h = logmap0(proj(x, c), c)
            h = jnp.transpose(h, (1, 2, 0))
            h = conv1d(h, w_qkv, pad=2)
            h = batchnorm(h, bn_gamma, bn_beta)
            h = jax.nn.relu(jnp.transpose(h, (2, 0, 1)))
            qkv = proj(expmap0(h, c), c)
            t = jnp.transpose(logmap0(proj(qkv, c), c), (1, 2, 0))
            s = conv1d(t, w_dw, pad=2, groups=t.shape[1])
            s = conv1d(s, w_pw, pad=0, groups=t.shape[1] // DIM)
            cat = jnp.concatenate([t, s], axis=1)
            ai = proj(expmap0(jnp.transpose(cat, (2, 0, 1)), c), c)
            t2 = logmap0(proj(ai, c), c)
            L, N, C2 = t2.shape
            g = C2 // (3 * DIM)
            qkv3 = jnp.transpose(t2, (1, 2, 0)).reshape(N, g, 3 * DIM, L)
            q, k, v = jnp.split(qkv3, 3, axis=2)
            q = jax.nn.relu(q)
            k = jax.nn.relu(k)
            vk = jnp.einsum('ngdl,ngel->ngde', v, k)
            out = jnp.einsum('ngde,ngdl->ngdl', vk, q)
            out = out / (jnp.sum(v, -1, keepdims=True) + ATT_EPS)
            out = jnp.transpose(out.reshape(N, g * DIM, L), (2, 0, 1))
            fx_h = proj(expmap0(out, c), c)
            ft = jnp.transpose(logmap0(proj(fx_h, c), c), (1, 2, 0))
            ft = conv1d(ft, w_res, pad=0) + b_res[None, :, None]
            fx = proj(expmap0(jnp.transpose(ft, (2, 0, 1)), c), c)
            residual = mobius_add(fx, x, c)
            return (fx, residual)
        key = jax.random.key(seed)
        ks = jax.random.split(key, 6)
        L, N, C, TD = (128, 16, 256, 256)
        x = jax.random.normal(ks[0], (L, N, C), jnp.float32) * 0.05
        w_qkv = jax.random.normal(ks[1], (3 * TD, C, 5), jnp.float32) / np.sqrt(C * 5)
        bn_gamma = jnp.ones((3 * TD,), jnp.float32)
        bn_beta = jnp.zeros((3 * TD,), jnp.float32)
        w_dw = jax.random.normal(ks[2], (3 * TD, 1, 5), jnp.float32) / np.sqrt(5.0)
        w_pw = jax.random.normal(ks[3], (3 * TD, DIM, 1), jnp.float32) / np.sqrt(DIM)
        w_res = jax.random.normal(ks[4], (C, 2 * TD, 1), jnp.float32) / np.sqrt(2 * TD)
        b_res = jnp.zeros((C,), jnp.float32)
        return {'x': x, 'w_qkv': w_qkv, 'bn_gamma': bn_gamma, 'bn_beta': bn_beta, 'w_dw': w_dw, 'w_pw': w_pw, 'w_res': w_res, 'b_res': b_res}
    _L0_mix_all = _L0_mix_setup()
    _L0_mix_in = {k: v for k, v in _L0_mix_all.items() if k in ('w_qkv', 'bn_gamma', 'bn_beta', 'w_dw', 'w_pw', 'w_res', 'b_res')}
    del _L0_mix_all

    def _L0_ffn_setup():
        import jax, jax.numpy as jnp
        import numpy as np
        B, S, H, F, E, K = (8, 256, 256, 512, 16, 2)
        EPS = 1e-05
        key = jax.random.key(seed)
        ks = jax.random.split(key, 9)
        sc = 0.02
        return {'x': jax.random.normal(ks[0], (B, S, H), dtype=jnp.float32), 'gate_w': jax.random.normal(ks[1], (H, E), dtype=jnp.float32) * sc, 'gate_b': jnp.zeros((E,), dtype=jnp.float32), 'w1': jax.random.normal(ks[2], (E, H, F), dtype=jnp.float32) * sc, 'b1': jnp.zeros((E, F), dtype=jnp.float32), 'w2': jax.random.normal(ks[3], (E, F, H), dtype=jnp.float32) * sc, 'b2': jnp.zeros((E, H), dtype=jnp.float32), 'gamma': jnp.ones((H,), dtype=jnp.float32), 'beta': jnp.zeros((H,), dtype=jnp.float32)}
    _L0_ffn_all = _L0_ffn_setup()
    _L0_ffn_in = {k: v for k, v in _L0_ffn_all.items() if k in ('gate_w', 'gate_b', 'w1', 'b1', 'w2', 'b2', 'gamma', 'beta')}
    del _L0_ffn_all

    def _L1_gnn_setup():
        import jax, jax.numpy as jnp
        import numpy as np
        N_NODES = 1250
        N_EDGES = 20000
        IN_DIM = 256
        OUT_DIM = 256
        N_HEADS = 4
        D_K = OUT_DIM // N_HEADS
        N_NTYPES = 4
        N_RELS = 8
        SQRT_DK = float(np.sqrt(D_K))

        def _typed_matmul(x, W, node_type):
            all_t = jnp.einsum('ni,tio->tno', x, W)
            return all_t[node_type, jnp.arange(x.shape[0])]
        key = jax.random.key(seed)
        ks = jax.random.split(key, 12)
        xav = lambda k, shape, fan: jax.random.normal(k, shape, jnp.float32) * (1.0 / np.sqrt(fan))
        return {'h': jax.random.normal(ks[0], (N_NODES, IN_DIM), jnp.float32), 'k_linears': xav(ks[1], (N_NTYPES, IN_DIM, OUT_DIM), IN_DIM), 'q_linears': xav(ks[2], (N_NTYPES, IN_DIM, OUT_DIM), IN_DIM), 'v_linears': xav(ks[3], (N_NTYPES, IN_DIM, OUT_DIM), IN_DIM), 'a_linears': xav(ks[4], (N_NTYPES, OUT_DIM, OUT_DIM), OUT_DIM), 'relation_att': xav(ks[5], (N_RELS, N_HEADS, D_K, D_K), D_K), 'relation_msg': xav(ks[6], (N_RELS, N_HEADS, D_K, D_K), D_K), 'relation_pri': jnp.ones((N_RELS, N_HEADS), jnp.float32), 'skip': jnp.ones((N_NTYPES,), jnp.float32), 'node_type': jax.random.randint(ks[7], (N_NODES,), 0, N_NTYPES), 'etype': jnp.sort(jax.random.randint(ks[8], (N_EDGES,), 0, N_RELS)), 'row_idx': jax.random.randint(ks[9], (N_EDGES,), 0, N_NODES), 'col_idx': jax.random.randint(ks[10], (N_EDGES,), 0, N_NODES)}
    _L1_gnn_all = _L1_gnn_setup()
    _L1_gnn_in = {k: v for k, v in _L1_gnn_all.items() if k in ('k_linears', 'q_linears', 'v_linears', 'a_linears', 'relation_att', 'relation_msg', 'relation_pri', 'skip')}
    del _L1_gnn_all

    def _L1_mix_setup():
        import jax, jax.numpy as jnp
        import numpy as np
        EPS_NORM = 1e-06
        EPS_ATTN = 1e-06
        HEADS = 8

        def rmsnorm(x, w):
            ms = jnp.mean(x * x, axis=-1, keepdims=True)
            return w * (x * jax.lax.rsqrt(ms + EPS_NORM))

        def linear_attention(x, w_qkv, w_out, b_out):
            B, N, D = x.shape
            hd = D // HEADS
            qkv = (x @ w_qkv).reshape(B, N, 3, HEADS, hd)
            q, k, v = (qkv[:, :, 0], qkv[:, :, 1], qkv[:, :, 2])
            q = jax.nn.elu(q) + 1.0
            k = jax.nn.elu(k) + 1.0
            kv = jnp.einsum('bnhd,bnhm->bhdm', k, v)
            z = 1.0 / (jnp.einsum('bnhd,bhd->bnh', q, k.sum(axis=1)) + EPS_ATTN)
            out = jnp.einsum('bnhd,bhdm,bnh->bnhm', q, kv, z)
            out = out.reshape(B, N, D)
            return out @ w_out + b_out
        key = jax.random.key(seed)
        ks = jax.random.split(key, 4)
        B, N, D = (16, 512, 256)
        x = jax.random.normal(ks[0], (B, N, D), dtype=jnp.float32)
        w_norm1 = jnp.ones((D,), dtype=jnp.float32)
        w_qkv = jax.random.normal(ks[1], (D, 3 * D), dtype=jnp.float32) * 0.02
        w_out = jax.random.normal(ks[2], (D, D), dtype=jnp.float32) * 0.02
        b_out = jnp.zeros((D,), dtype=jnp.float32)
        w_norm2 = jnp.ones((D,), dtype=jnp.float32)
        return {'x': x, 'w_norm1': w_norm1, 'w_qkv': w_qkv, 'w_out': w_out, 'b_out': b_out, 'w_norm2': w_norm2}
    _L1_mix_all = _L1_mix_setup()
    _L1_mix_in = {k: v for k, v in _L1_mix_all.items() if k in ('w_norm1', 'w_qkv', 'w_out', 'b_out', 'w_norm2')}
    del _L1_mix_all

    def _L1_ffn_setup():
        import jax, jax.numpy as jnp
        import numpy as np
        B, S, D, E, H, K = (4, 256, 256, 8, 512, 2)
        key = jax.random.key(seed)
        ks = jax.random.split(key, 6)
        x = jax.random.normal(ks[0], (B, S, D), jnp.float32)
        Wg = jax.random.normal(ks[1], (D, E), jnp.float32) * 0.02
        bg = jnp.zeros((E,), jnp.float32)
        W1 = jax.random.normal(ks[2], (E, D, H), jnp.float32) * 0.02
        b1 = jnp.zeros((E, H), jnp.float32)
        W2 = jax.random.normal(ks[3], (E, H, D), jnp.float32) * 0.02
        b2 = jnp.zeros((E, D), jnp.float32)
        return {'x': x, 'Wg': Wg, 'bg': bg, 'W1': W1, 'b1': b1, 'W2': W2, 'b2': b2}
    _L1_ffn_all = _L1_ffn_setup()
    _L1_ffn_in = {k: v for k, v in _L1_ffn_all.items() if k in ('Wg', 'bg', 'W1', 'b1', 'W2', 'b2')}
    del _L1_ffn_all
    return {'x': x, 'src': src, 'dst': dst, 'edge_attr_128': edge_attr_128, 'edge_type_8': edge_type_8, 'node_type_4': node_type_4, 'L0_gnn_Wn': _L0_gnn_in['Wn'], 'L0_gnn_bn': _L0_gnn_in['bn'], 'L0_gnn_We': _L0_gnn_in['We'], 'L0_gnn_be': _L0_gnn_in['be'], 'L0_gnn_attn': _L0_gnn_in['attn'], 'L0_mix_w_qkv': _L0_mix_in['w_qkv'], 'L0_mix_bn_gamma': _L0_mix_in['bn_gamma'], 'L0_mix_bn_beta': _L0_mix_in['bn_beta'], 'L0_mix_w_dw': _L0_mix_in['w_dw'], 'L0_mix_w_pw': _L0_mix_in['w_pw'], 'L0_mix_w_res': _L0_mix_in['w_res'], 'L0_mix_b_res': _L0_mix_in['b_res'], 'L0_ffn_gate_w': _L0_ffn_in['gate_w'], 'L0_ffn_gate_b': _L0_ffn_in['gate_b'], 'L0_ffn_w1': _L0_ffn_in['w1'], 'L0_ffn_b1': _L0_ffn_in['b1'], 'L0_ffn_w2': _L0_ffn_in['w2'], 'L0_ffn_b2': _L0_ffn_in['b2'], 'L0_ffn_gamma': _L0_ffn_in['gamma'], 'L0_ffn_beta': _L0_ffn_in['beta'], 'L1_gnn_k_linears': _L1_gnn_in['k_linears'], 'L1_gnn_q_linears': _L1_gnn_in['q_linears'], 'L1_gnn_v_linears': _L1_gnn_in['v_linears'], 'L1_gnn_a_linears': _L1_gnn_in['a_linears'], 'L1_gnn_relation_att': _L1_gnn_in['relation_att'], 'L1_gnn_relation_msg': _L1_gnn_in['relation_msg'], 'L1_gnn_relation_pri': _L1_gnn_in['relation_pri'], 'L1_gnn_skip': _L1_gnn_in['skip'], 'L1_mix_w_norm1': _L1_mix_in['w_norm1'], 'L1_mix_w_qkv': _L1_mix_in['w_qkv'], 'L1_mix_w_out': _L1_mix_in['w_out'], 'L1_mix_b_out': _L1_mix_in['b_out'], 'L1_mix_w_norm2': _L1_mix_in['w_norm2'], 'L1_ffn_Wg': _L1_ffn_in['Wg'], 'L1_ffn_bg': _L1_ffn_in['bg'], 'L1_ffn_W1': _L1_ffn_in['W1'], 'L1_ffn_b1': _L1_ffn_in['b1'], 'L1_ffn_W2': _L1_ffn_in['W2'], 'L1_ffn_b2': _L1_ffn_in['b2']}

def reference(x, src, dst, edge_attr_128, edge_type_8, node_type_4, L0_gnn_Wn, L0_gnn_bn, L0_gnn_We, L0_gnn_be, L0_gnn_attn, L0_mix_w_qkv, L0_mix_bn_gamma, L0_mix_bn_beta, L0_mix_w_dw, L0_mix_w_pw, L0_mix_w_res, L0_mix_b_res, L0_ffn_gate_w, L0_ffn_gate_b, L0_ffn_w1, L0_ffn_b1, L0_ffn_w2, L0_ffn_b2, L0_ffn_gamma, L0_ffn_beta, L1_gnn_k_linears, L1_gnn_q_linears, L1_gnn_v_linears, L1_gnn_a_linears, L1_gnn_relation_att, L1_gnn_relation_msg, L1_gnn_relation_pri, L1_gnn_skip, L1_mix_w_norm1, L1_mix_w_qkv, L1_mix_w_out, L1_mix_b_out, L1_mix_w_norm2, L1_ffn_Wg, L1_ffn_bg, L1_ffn_W1, L1_ffn_b1, L1_ffn_W2, L1_ffn_b2):
    import jax
    import jax.numpy as jnp

    def _L0_gnn_ref(x, edge_index, edge_attr, Wn, bn, We, be, attn):
        import jax, jax.numpy as jnp
        import numpy as np
        N_NODES = 3125
        N_EDGES = 50000
        IN_DIM = 256
        OUT_DIM = 256
        HEADS = 1
        EDGE_DIM = 128
        NEG_SLOPE = 0.01
        N = x.shape[0]
        H, C = (attn.shape[1], attn.shape[2])
        src, dst = (edge_index[0], edge_index[1])
        h = x @ Wn.T + bn
        e = edge_attr @ We.T + be
        xj = h[src].reshape(-1, H, C)
        ee = e.reshape(-1, H, C)
        a = jax.nn.leaky_relu(jnp.sum((xj + ee) * attn, axis=-1), NEG_SLOPE)
        m = jax.ops.segment_max(a, dst, num_segments=N)
        a = jnp.exp(a - m[dst])
        denom = jax.ops.segment_sum(a, dst, num_segments=N)
        a = a / (denom[dst] + 1e-16)
        msg = (xj * a[..., None]).reshape(-1, H * C)
        out = jax.ops.segment_sum(msg, dst, num_segments=N)
        return jax.nn.relu(out)

    def _L0_mix_ref(x, w_qkv, bn_gamma, bn_beta, w_dw, w_pw, w_res, b_res):
        import jax, jax.numpy as jnp
        import numpy as np
        C_CURV = 1.0
        MIN_NORM = 1e-15
        BALL_EPS = 1e-05
        ATT_EPS = 1e-15
        DIM = 32

        def _norm(x):
            return jnp.clip(jnp.linalg.norm(x, axis=-1, keepdims=True), MIN_NORM)

        def proj(x, c):
            maxnorm = (1.0 - BALL_EPS) / jnp.sqrt(c)
            n = _norm(x)
            return jnp.where(n > maxnorm, x / n * maxnorm, x)

        def expmap0(u, c):
            sc = jnp.sqrt(c)
            n = _norm(u)
            return jnp.tanh(sc * n) * u / (sc * n)

        def logmap0(p, c):
            sc = jnp.sqrt(c)
            n = _norm(p)
            return jnp.arctanh(jnp.clip(sc * n, -1.0 + 1e-07, 1.0 - 1e-07)) * p / (sc * n)

        def mobius_add(x, y, c):
            x2 = jnp.sum(x * x, -1, keepdims=True)
            y2 = jnp.sum(y * y, -1, keepdims=True)
            xy = jnp.sum(x * y, -1, keepdims=True)
            num = (1 + 2 * c * xy + c * y2) * x + (1 - c * x2) * y
            den = 1 + 2 * c * xy + c * c * x2 * y2
            return num / jnp.clip(den, MIN_NORM)

        def conv1d(x, w, pad, groups=1):
            return jax.lax.conv_general_dilated(x, w, (1,), [(pad, pad)], dimension_numbers=('NCH', 'OIH', 'NCH'), feature_group_count=groups)

        def batchnorm(x, gamma, beta):
            mean = jnp.mean(x, axis=(0, 2), keepdims=True)
            var = jnp.var(x, axis=(0, 2), keepdims=True)
            xn = (x - mean) * jax.lax.rsqrt(var + 1e-05)
            return gamma[None, :, None] * xn + beta[None, :, None]

        def _reference_tuple_inner(x, w_qkv, bn_gamma, bn_beta, w_dw, w_pw, w_res, b_res):
            c = C_CURV
            h = logmap0(proj(x, c), c)
            h = jnp.transpose(h, (1, 2, 0))
            h = conv1d(h, w_qkv, pad=2)
            h = batchnorm(h, bn_gamma, bn_beta)
            h = jax.nn.relu(jnp.transpose(h, (2, 0, 1)))
            qkv = proj(expmap0(h, c), c)
            t = jnp.transpose(logmap0(proj(qkv, c), c), (1, 2, 0))
            s = conv1d(t, w_dw, pad=2, groups=t.shape[1])
            s = conv1d(s, w_pw, pad=0, groups=t.shape[1] // DIM)
            cat = jnp.concatenate([t, s], axis=1)
            ai = proj(expmap0(jnp.transpose(cat, (2, 0, 1)), c), c)
            t2 = logmap0(proj(ai, c), c)
            L, N, C2 = t2.shape
            g = C2 // (3 * DIM)
            qkv3 = jnp.transpose(t2, (1, 2, 0)).reshape(N, g, 3 * DIM, L)
            q, k, v = jnp.split(qkv3, 3, axis=2)
            q = jax.nn.relu(q)
            k = jax.nn.relu(k)
            vk = jnp.einsum('ngdl,ngel->ngde', v, k)
            out = jnp.einsum('ngde,ngdl->ngdl', vk, q)
            out = out / (jnp.sum(v, -1, keepdims=True) + ATT_EPS)
            out = jnp.transpose(out.reshape(N, g * DIM, L), (2, 0, 1))
            fx_h = proj(expmap0(out, c), c)
            ft = jnp.transpose(logmap0(proj(fx_h, c), c), (1, 2, 0))
            ft = conv1d(ft, w_res, pad=0) + b_res[None, :, None]
            fx = proj(expmap0(jnp.transpose(ft, (2, 0, 1)), c), c)
            residual = mobius_add(fx, x, c)
            return (fx, residual)
        return _reference_tuple_inner(x, w_qkv, bn_gamma, bn_beta, w_dw, w_pw, w_res, b_res)[0]

    def _L0_ffn_ref(x, gate_w, gate_b, w1, b1, w2, b2, gamma, beta):
        import jax, jax.numpy as jnp
        import numpy as np
        B, S, H, F, E, K = (8, 256, 256, 512, 16, 2)
        EPS = 1e-05
        gate_logits = x @ gate_w + gate_b
        topk_vals, topk_idx = jax.lax.top_k(gate_logits, K)
        topk_w = jax.nn.softmax(topk_vals, axis=-1)
        h = jax.nn.relu(jnp.einsum('bsh,ehf->bsef', x, w1) + b1)
        expert_out = jnp.einsum('bsef,efh->bseh', h, w2) + b2
        sel = jnp.take_along_axis(expert_out, topk_idx[:, :, :, None], axis=2)
        moe = jnp.sum(topk_w[..., None] * sel, axis=2)
        y = x + moe
        mu = jnp.mean(y, axis=-1, keepdims=True)
        var = jnp.var(y, axis=-1, keepdims=True)
        return (y - mu) / jnp.sqrt(var + EPS) * gamma + beta

    def _L1_gnn_ref(h, k_linears, q_linears, v_linears, a_linears, relation_att, relation_msg, relation_pri, skip, node_type, etype, row_idx, col_idx):
        import jax, jax.numpy as jnp
        import numpy as np
        N_NODES = 1250
        N_EDGES = 20000
        IN_DIM = 256
        OUT_DIM = 256
        N_HEADS = 4
        D_K = OUT_DIM // N_HEADS
        N_NTYPES = 4
        N_RELS = 8
        SQRT_DK = float(np.sqrt(D_K))

        def _typed_matmul(x, W, node_type):
            all_t = jnp.einsum('ni,tio->tno', x, W)
            return all_t[node_type, jnp.arange(x.shape[0])]
        n = h.shape[0]
        k = _typed_matmul(h, k_linears, node_type).reshape(n, N_HEADS, D_K)
        q = _typed_matmul(h, q_linears, node_type).reshape(n, N_HEADS, D_K)
        v = _typed_matmul(h, v_linears, node_type).reshape(n, N_HEADS, D_K)
        q_att = jnp.einsum('nhd,rhde->rnhe', q, relation_att)
        v_msg = jnp.einsum('nhd,rhde->rnhe', v, relation_msg)
        aw_q_edge = q_att[etype, col_idx]
        msg_edge = v_msg[etype, row_idx]
        attn_score = jnp.sum(aw_q_edge * k[row_idx], axis=-1)
        score = attn_score * (relation_pri[etype] / SQRT_DK)
        m = jax.ops.segment_max(score, col_idx, num_segments=n)
        ex = jnp.exp(score - m[col_idx])
        denom = jax.ops.segment_sum(ex, col_idx, num_segments=n)
        alpha = ex / denom[col_idx]
        agg = jax.ops.segment_sum(alpha[..., None] * msg_edge, col_idx, num_segments=n)
        agg = agg.reshape(n, OUT_DIM)
        out = _typed_matmul(agg, a_linears, node_type)
        out = jax.nn.sigmoid(skip)[node_type][:, None] * out
        return out

    def _L1_mix_ref(x, w_norm1, w_qkv, w_out, b_out, w_norm2):
        import jax, jax.numpy as jnp
        import numpy as np
        EPS_NORM = 1e-06
        EPS_ATTN = 1e-06
        HEADS = 8

        def rmsnorm(x, w):
            ms = jnp.mean(x * x, axis=-1, keepdims=True)
            return w * (x * jax.lax.rsqrt(ms + EPS_NORM))

        def linear_attention(x, w_qkv, w_out, b_out):
            B, N, D = x.shape
            hd = D // HEADS
            qkv = (x @ w_qkv).reshape(B, N, 3, HEADS, hd)
            q, k, v = (qkv[:, :, 0], qkv[:, :, 1], qkv[:, :, 2])
            q = jax.nn.elu(q) + 1.0
            k = jax.nn.elu(k) + 1.0
            kv = jnp.einsum('bnhd,bnhm->bhdm', k, v)
            z = 1.0 / (jnp.einsum('bnhd,bhd->bnh', q, k.sum(axis=1)) + EPS_ATTN)
            out = jnp.einsum('bnhd,bhdm,bnh->bnhm', q, kv, z)
            out = out.reshape(B, N, D)
            return out @ w_out + b_out
        h = x + linear_attention(rmsnorm(x, w_norm1), w_qkv, w_out, b_out)
        return h + rmsnorm(h, w_norm2)

    def _L1_ffn_ref(x, Wg, bg, W1, b1, W2, b2):
        import jax, jax.numpy as jnp
        import numpy as np
        B, S, D, E, H, K = (4, 256, 256, 8, 512, 2)
        Bv, Sv, Dv = x.shape
        gate_scores = x @ Wg + bg
        _, idx = jax.lax.top_k(gate_scores, K)
        mask = jax.nn.one_hot(idx, E, dtype=x.dtype).sum(axis=-2)
        xf = x.reshape(-1, Dv)
        mf = mask.reshape(-1, E)
        h = jax.nn.gelu(jnp.einsum('td,edh->teh', xf, W1) + b1[None], approximate=False)
        y = jnp.einsum('teh,ehd->ted', h, W2) + b2[None]
        out = jnp.einsum('ted,te->td', y, mf)
        return out.reshape(Bv, Sv, Dv)
    edge_index = jnp.stack([src, dst])
    xn = _layernorm(x, axis=-1)
    x = x + _L0_gnn_ref(xn, edge_index, edge_attr_128, L0_gnn_Wn, L0_gnn_bn, L0_gnn_We, L0_gnn_be, L0_gnn_attn) + _L0_mix_ref(xn[None], L0_mix_w_qkv, L0_mix_bn_gamma, L0_mix_bn_beta, L0_mix_w_dw, L0_mix_w_pw, L0_mix_w_res, L0_mix_b_res)[0]
    x = x + _L0_ffn_ref(_layernorm(x, axis=-1)[None], L0_ffn_gate_w, L0_ffn_gate_b, L0_ffn_w1, L0_ffn_b1, L0_ffn_w2, L0_ffn_b2, L0_ffn_gamma, L0_ffn_beta)[0]
    xn = _layernorm(x, axis=-1)
    x = x + _L1_gnn_ref(xn, L1_gnn_k_linears, L1_gnn_q_linears, L1_gnn_v_linears, L1_gnn_a_linears, L1_gnn_relation_att, L1_gnn_relation_msg, L1_gnn_relation_pri, L1_gnn_skip, node_type_4, edge_type_8, src, dst) + _L1_mix_ref(xn[None], L1_mix_w_norm1, L1_mix_w_qkv, L1_mix_w_out, L1_mix_b_out, L1_mix_w_norm2)[0]
    x = x + _L1_ffn_ref(_layernorm(x, axis=-1)[None], L1_ffn_Wg, L1_ffn_bg, L1_ffn_W1, L1_ffn_b1, L1_ffn_W2, L1_ffn_b2)[0]
    return x

_drawn_inputs = setup_inputs


def setup_inputs(seed=0):
    import zlib

    import numpy as np

    out = dict(_drawn_inputs(seed))
    spreads = {'L0_gnn_bn': (0.0, 0.1),
     'L0_gnn_be': (0.0, 0.8),
     'L0_mix_bn_gamma': (1.0, 0.6),
     'L0_mix_bn_beta': (0.0, 0.434),
     'L0_mix_b_res': (0.0, 0.344),
     'L0_ffn_gate_b': (0.0, 0.1),
     'L0_ffn_b1': (0.0, 0.653),
     'L0_ffn_b2': (0.0, 0.1),
     'L0_ffn_gamma': (1.0, 0.2),
     'L0_ffn_beta': (0.0, 0.1),
     'L1_gnn_relation_pri': (1.0, 0.6),
     'L1_gnn_skip': (1.0, 0.6),
     'L1_mix_w_norm1': (1.0, 0.6),
     'L1_mix_b_out': (0.0, 0.1),
     'L1_mix_w_norm2': (1.0, 0.2),
     'L1_ffn_bg': (0.0, 0.301),
     'L1_ffn_b1': (0.0, 0.8),
     'L1_ffn_b2': (0.0, 0.1)}
    factors = {'L0_mix_w_dw': 6.12, 'L0_mix_w_pw': 5.996, 'L1_mix_w_qkv': 8.0, 'L1_mix_w_out': 8.0}
    for name, (base, spread) in spreads.items():
        noise = np.random.default_rng([zlib.crc32(name.encode()), seed]).standard_normal(out[name].shape)
        drawn = base * np.exp(spread * noise) if base else spread * noise
        out[name] = jnp.asarray(drawn.astype(out[name].dtype))
    for name, factor in factors.items():
        out[name] = (out[name] * factor).astype(out[name].dtype)
    return out
```

```python
from contextlib import ExitStack
import math

import numpy as np
import concourse.bass as bass
from concourse import mybir

F32 = mybir.dt.float32
I32 = mybir.dt.int32
U32 = mybir.dt.uint32
ALU = mybir.AluOpType
ACT = mybir.ActivationFunctionType
X_AX = mybir.AxisListType.X

N = 3125
P = 125
NT = 25
D = 256
E = 100000
C = 784
EP = 128 * C
QC = C // 4
NTI = EP // 512
NS = NTI + NT - 1
WROW = 2052
MS = (2 * N + 16 * 127) // 128 * 128
RW = 260
BIG = 1.0e30
PADN = 4000
MX = float(np.float32(0.99999))
T0 = float(0.5 * math.log((1.0 + MX) / (1.0 - MX)))
BLK = [(500 * b, min(500, N - 500 * b)) for b in range(7)]


class Eng:

    def __init__(self, engine, sem):
        self.engine, self.sem, self.n, self.seen = engine, sem, 0, {}

    def wait(self, *tokens):
        for t in tokens:
            if t is None:
                continue
            if isinstance(t, list):
                self.wait(*t)
                continue
            s, v = t
            if self.seen.get(id(s), 0) < v:
                self.seen[id(s)] = v
                self.engine.wait_ge(s, v)

    def op(self, fn, *tokens):
        self.wait(*tokens)
        self.n += 1
        fn(self.engine).then_inc(self.sem, 1)
        return (self.sem, self.n)

    def chain(self, fns, *tokens):
        t = None
        for k, fn in enumerate(fns):
            t = self.op(fn, t) if k else self.op(fn, *tokens)
        return t

    def do(self, fn, *tokens):
        self.wait(*tokens)
        fn(self.engine)

    @property
    def now(self):
        return (self.sem, self.n)


class Chan:

    def __init__(self, sem):
        self.sem, self.n = sem, 0

    def dma(self, eng, out, in_, *tokens):
        eng.wait(*tokens)
        self.n += 16
        eng.engine.dma_start(out, in_).then_inc(self.sem, 16)
        return (self.sem, self.n)

    def dma125(self, eng, out, in_, *tokens):
        self.dma(eng, out[0:112], in_[0:112], *tokens)
        return self.dma(eng, out[112:P], in_[112:P])

    @property
    def now(self):
        return (self.sem, self.n)


class Ring:

    def __init__(self, bufs):
        self.bufs, self.free, self.k = bufs, [None] * len(bufs), 0

    def take(self):
        i = self.k % len(self.bufs)
        self.k += 1
        return i, self.bufs[i], self.free[i]


def build(nc, I, out):
    ctx = ExitStack()
    with ctx:
        nsem = [0]

        def sem():
            nsem[0] += 1
            return ctx.enter_context(nc.semaphore(f"s{nsem[0]}"))

        V, A, T, G, S = (Eng(e, sem()) for e in (nc.vector, nc.scalar, nc.tensor, nc.gpsimd, nc.sync))
        ENG = [V, A, T, G, S]
        chans = []

        def chan():
            chans.append(Chan(sem()))
            return chans[-1]

        def barrier():
            every = [e.now for e in ENG if e.n] + [c.now for c in chans if c.n]
            for e in ENG:
                e.wait(every)

        WIDE = 52800
        mem = ctx.enter_context(nc.sbuf_tensor("mem", [128, WIDE], F32))
        bank = [ctx.enter_context(nc.psum_tensor(f"bank{i}", [128, 512], F32)) for i in range(8)]

        class Arena:
            def __init__(self, at):
                self.at = at

            def get(self, *dims, parts=128, dt=None):
                n = int(np.prod(dims))
                v = mem[0:parts, self.at:self.at + n]
                self.at += n
                assert self.at <= WIDE, self.at
                if dt is not None:
                    v = v.bitcast(dt)
                if len(dims) == 2:
                    v = v.rearrange("p (a b) -> p a b", b=dims[1])
                if len(dims) == 3:
                    v = v.rearrange("p (a b c) -> p a b c", b=dims[1], c=dims[2])
                return v

        def dram(name, shape, dt=F32):
            return nc.dram_tensor(name, shape, dt).ap()

        hp_d = dram("hp_d", [N, RW])
        hs_d = dram("hs_d", [EP, RW])
        rec0_d = dram("rec0_d", [EP, 2])
        rec1_d = dram("rec1_d", [EP, 5])
        q_d = dram("q_d", [N, D])
        kv_d = dram("kv_d", [8 * N, 2 * D])
        vs_d = dram("vs_d", [EP, D])
        xs_d = dram("xs_d", [MS, D])
        ys_d = dram("ys_d", [MS, D])

        def bc(ap, axis, n):
            v = ap.unsqueeze(axis)
            shape = list(v.shape)
            shape[axis] = n
            return v.to_broadcast(shape)

        def rowb(ap, off, n, parts=128):
            return bass.AP(ap.tensor, off, [[0, parts], [1, n]])

        top = Arena(0)
        ident = top.get(128)
        iota = top.get(128)
        blk = top.get(128)
        tri = top.get(128)
        hm4 = top.get(4)
        ones = top.get(128)
        JV = top.get(NS)
        REG = top.get(2, NS, dt=I32)
        XAT = top.at
        X = top.get(NT, D, parts=P)
        mv = top.get(NT, 2, parts=P)
        st = top.get(NT, 6, parts=P)
        rstd = top.get(NT, parts=P)
        BASE = top.at

        c_in = chan()
        c_x = chan()
        c_x.dma125(S, X, I["x"].rearrange("(t p) d -> p t d", p=P))
        for ap, name in ((ident, "c_ident"), (iota, "c_iota"), (blk, "c_blk"), (tri, "c_tri"), (hm4, "c_hm4")):
            c_in.dma(S, ap, I[name])
        t_ones = V.op(lambda e: e.memset(ones, 1.0))

        def ln_stats(src, eps, *tokens):
            ts = [V.op(lambda e, t=t: e.bn_stats(st[:, t, :], src[:, t, :]), *tokens) for t in range(NT)]
            for t in range(NT):
                tk = V.op(lambda e, t=t: e.bn_aggr(mv[:, t, :], st[:, t, :]), ts[t])
            tk = V.op(lambda e: e.tensor_scalar(rstd, mv[:, :, 1], eps, None, ALU.add), tk)
            tk = A.op(lambda e: e.activation(rstd, rstd, ACT.Sqrt), tk)
            return V.op(lambda e: e.reciprocal(rstd, rstd), tk)

        def ln_apply(dst, src, tok, *tokens):
            return [V.op(lambda e, t=t: e.tensor_scalar(dst[:, t, :], src[:, t, :], mv[:, t, 0:1], rstd[:, t:t + 1],
                                                        ALU.subtract, ALU.mult), tok, *tokens) for t in range(NT)]

        s2 = Arena(BASE)
        TT = s2.get(6, N)
        HQAT = s2.at
        HQ = s2.get(2, N)
        Wc = s2.get(2, 768)
        srcI = s2.get(C, dt=I32)
        dstF = s2.get(C)
        Pt = s2.get(C)
        tt = s2.get(C)
        wB = s2.get(129)
        bng = s2.get(6)
        bnb = s2.get(6)
        s2_own = Arena(s2.at)
        dstI = Pt.bitcast(I32)

        c_w = chan()
        c_w.dma(A, Wc, I["w_qkv"].rearrange("(k p) o -> p k o", p=128))
        c_e = chan()
        c_e.dma(S, srcI, I["src"])
        c_e.dma(S, dstI, I["dst"])
        c_w.dma(A, bng, I["bn_gamma"])
        c_w.dma(A, bnb, I["bn_beta"])

        s1 = Arena(s2.at)
        WnT = s1.get(2, D)
        WeB = s1.get(2, 129)
        attnC = s1.get(2)
        attnCB = s1.get(2, 128)
        attnB = s1.get(D)
        bnB = s1.get(D)
        XNb = [s1.get(D, parts=P) for _ in range(3)]
        H0b = [s1.get(D, parts=P) for _ in range(3)]
        XTb = [s1.get(2, P) for _ in range(2)]
        HPb = [s1.get(RW, parts=P) for _ in range(3)]
        junk = s1.get(D, parts=P)
        junk2 = s1.get(D, parts=P)
        ss = s1.get(NT, parts=P)
        fac = s1.get(NT, parts=P)
        sm = [s1.get(NT, parts=P) for _ in range(5)]
        c_1 = chan()
        c_1.dma(A, WnT, I["WnT"].rearrange("(k p) n -> p k n", p=128))
        c_1.dma(A, WeB, I["WeB"].rearrange("(k p) n -> p k n", p=128))
        c_1.dma(A, attnC, I["attnC"])
        c_1.dma(A, attnB, rowb(I["attn"], 0, D))
        c_1.dma(A, bnB, rowb(I["bn"], 0, D))

        tk = V.op(lambda e: e.tensor_copy(attnCB, bc(attnC, 2, 128)), c_1.now)
        for kc in range(2):
            tw = T.op(lambda e, kc=kc: e.matmul(bank[7][:, 0:129], attnCB[:, kc, :], WeB[:, kc, :],
                                                start=kc == 0, stop=kc == 1), tk, c_1.now)
        t_wB = V.op(lambda e: e.tensor_copy(wB, bank[7][:, 0:129]), tw)
        t_dst = V.op(lambda e: e.tensor_copy(dstF, dstI), c_e.now)

        trs = ln_stats(X, 1e-5, c_x.now)
        nmr = sm[4]
        tn = V.op(lambda e: e.scalar_tensor_tensor(nmr, mv[:, :, 0], -1.0, rstd, ALU.mult, ALU.mult), trs)
        for t in range(NT):
            tq = A.op(lambda e, t=t: e.activation(junk, X[:, t, :], ACT.Square, bias=nmr[:, t:t + 1],
                                                  scale=rstd[:, t:t + 1], accum_out=ss[:, t:t + 1]), tn, A.now)
        tq = A.op(lambda e: e.activation(ss, ss, ACT.Sqrt), tq)
        y, y2, r, u = sm[0:4]
        tk = V.chain([
            lambda e: e.tensor_scalar(ss, ss, 1e-15, None, ALU.max),
            lambda e: e.tensor_scalar(y, ss, MX, None, ALU.min),
            lambda e: e.tensor_scalar(r, y, -1.0, 1.0, ALU.mult, ALU.add),
            lambda e: e.reciprocal(r, r),
            lambda e: e.scalar_tensor_tensor(r, y, 1.0, r, ALU.add, ALU.mult),
        ], tq)
        tk = A.op(lambda e: e.activation(r, r, ACT.Ln), tk)
        tk = V.chain([
            lambda e: e.tensor_tensor(y2, y, y, ALU.mult),
            lambda e: e.tensor_scalar(u, y2, 1.0 / 7.0, 0.2, ALU.mult, ALU.add),
            lambda e: e.tensor_tensor(u, u, y2, ALU.mult),
            lambda e: e.tensor_scalar(u, u, 1.0 / 3.0, None, ALU.add),
            lambda e: e.tensor_tensor(u, u, y2, ALU.mult),
            lambda e: e.scalar_tensor_tensor(u, u, 1.0, y, ALU.add, ALU.mult),
            lambda e: e.tensor_scalar(r, r, 0.5, None, ALU.mult),
            lambda e: e.tensor_tensor(u, u, r, ALU.subtract),
            lambda e: e.tensor_scalar(y2, y, 0.05, None, ALU.is_lt),
            lambda e: e.tensor_tensor(u, u, y2, ALU.mult),
            lambda e: e.tensor_tensor(u, u, r, ALU.add),
            lambda e: e.reciprocal(fac, ss),
            lambda e: e.tensor_tensor(fac, fac, u, ALU.mult),
        ], tk)
        tfac = tk
        rx, rh, rt, rp = Ring(XNb), Ring(H0b), Ring(XTb), Ring(HPb)
        tone = [V.op(lambda e, b=b: e.memset(b, 1.0)) for b in HPb][-1]
        rb = Ring(bank[0:3])
        rm = Ring(bank[3:6])
        c_hp = [chan() for _ in range(3)]
        for t in range(NT):
            ix, xn, fx = rx.take()
            ih, h0, fh = rh.take()
            t1 = V.op(lambda e, t=t, xn=xn: e.tensor_scalar(xn, X[:, t, :], mv[:, t, 0:1], rstd[:, t:t + 1],
                                                           ALU.subtract, ALU.mult), trs, fx)
            t2 = A.op(lambda e, t=t, xn=xn, h0=h0: e.activation(h0, xn, ACT.Identity, scale=fac[:, t:t + 1]),
                      t1, tfac, fh)
            ib, b, fb = rb.take()
            T.wait(c_in.now, fb, t1, t2)
            for k in range(2):
                T.op(lambda e, k=k, xn=xn, b=b: e.transpose(b[:, 256 + k * P:256 + (k + 1) * P],
                                                            xn[:, 128 * k:128 * k + 128], ident[0:P, 0:P]))
            for k in range(2):
                tp = T.op(lambda e, k=k, h0=h0, b=b: e.transpose(b[:, k * P:(k + 1) * P],
                                                                 h0[:, 128 * k:128 * k + 128], ident[0:P, 0:P]))
            rx.free[ix] = tp
            rh.free[ih] = tp
            it, xt, ft = rt.take()
            t3 = V.op(lambda e, xt=xt, b=b: e.tensor_copy(xt, b[:, 256:256 + 2 * P].rearrange("p (k n) -> p k n", k=2)),
                      tp, ft)
            t4 = A.op(lambda e, t=t, b=b: e.activation(HQ[:, :, P * t:P * t + P],
                                                       b[:, 0:2 * P].rearrange("p (k n) -> p k n", k=2), ACT.Copy),
                      tp, t3)
            rb.free[ib] = t4
            im, m, fm = rm.take()
            for k in range(2):
                tm = T.op(lambda e, k=k, xt=xt, m=m: e.matmul(m[0:P, 0:D], xt[:, k, :], WnT[:, k, :],
                                                              start=k == 0, stop=k == 1), t3, fm, c_1.now)
            rt.free[it] = tm
            ip, hp, fp = rp.take()
            t5 = V.op(lambda e, hp=hp, m=m: e.tensor_tensor(hp[:, 0:D], m[0:P, 0:D], bnB[0:P, :], ALU.add),
                      tm, fp, tone)
            rm.free[im] = t5
            t6 = V.op(lambda e, hp=hp: e.tensor_tensor_reduce(junk2, hp[:, 0:D], attnB[0:P, :], 1.0, 0.0, ALU.mult,
                                                              ALU.add, hp[:, D + 1:D + 2]), t5)
            rp.free[ip] = c_hp[ip].dma125(S, hp_d[P * t:P * t + P, :], hp, t6)
        barrier()

        own = Arena(s2_own.at)
        gbuf = [own.get(4, RW) for _ in range(3)]
        EAb = [own.get(8, 128) for _ in range(2)]

        def pass1():
            rg = Ring(gbuf)
            cg = [chan() for _ in gbuf]
            cs = [chan() for _ in gbuf]
            hs_v = hs_d.rearrange("(p c) d -> p c d", p=128)
            for k in range(QC):
                i, g, fg = rg.take()
                G.wait(fg)
                for c in range(4):
                    cg[i].n += 16
                    G.do(lambda e, g=g, c=c, k=k, s=cg[i].sem: e.indirect_dma_start(
                        out=g[:, c, :], out_offset=None, in_=hp_d,
                        in_offset=bass.IndirectOffsetOnAxis(ap=srcI[:, 4 * k + c:4 * k + c + 1], axis=0)).then_inc(s, 16))
                ts = cs[i].dma(S, hs_v[:, 4 * k:4 * k + 4, :], g, cg[i].now)
                tv = V.op(lambda e, g=g, k=k: e.tensor_copy(Pt[:, 4 * k:4 * k + 4], g[:, :, D + 1]), cg[i].now)
                rg.free[i] = [ts, tv]
                yield

        def edge_logits():
            ce = [chan() for _ in EAb]
            re = Ring(EAb)
            tz = [V.op(lambda e, b=b: e.memset(b, 0.0)) for b in EAb][-1]
            ea = I["edge_attr"]
            full = (E - 127 * C) // 8
            for k in range(C // 8):
                i, b, fb = re.take()
                bf = b.rearrange("p a f -> p (a f)")

                def src(p0, n, k=k):
                    return bass.AP(ea.tensor, (C * p0 + 8 * k) * 128, [[C * 128, n], [1, 1024]])
                if k < full:
                    ce[i].dma(S, bf, src(0, 128), fb, tz)
                else:
                    ce[i].dma(S, bf[0:112], src(0, 112), fb, tz)
                    ce[i].dma(S, bf[112:127], src(112, 15))
                t1 = V.op(lambda e, b=b: e.tensor_tensor(b, b, bc(wB[:, 0:128], 1, 8), ALU.mult), ce[i].now)
                t2 = V.op(lambda e, b=b, k=k: e.tensor_reduce(tt[:, 8 * k:8 * k + 8], b, X_AX, ALU.add), t1)
                re.free[i] = t2
                yield

        mown = Arena(own.at)

        def mixer0():
            SB = mem[:, HQAT:HQAT + 3000].rearrange("p (c n) -> p c n", c=6)
            VF = mown.get(4, 500)
            RD = mown.get(4, 500)
            sqb = [mown.get(500) for _ in range(2)]
            nb = [mown.get(500) for _ in range(2)]
            Wd = mown.get(6, 128)
            bst = mown.get(7, 6)
            bmv = mown.get(6, 2)
            bsc = mown.get(6)
            bbi = mown.get(6)
            wres = mown.get(4, D)
            brB = mown.get(D)
            wdwC = mown.get(6)
            ss3 = mown.get(NT, parts=P)
            ss4 = mown.get(NT, parts=P)
            f3 = mown.get(NT, parts=P)
            f4 = mown.get(NT, parts=P)
            n4 = mown.get(NT, parts=P)
            FX = X
            c_m = chan()
            c_m.dma(A, wres, I["w_res"].rearrange("(k p) n -> p k n", p=128))
            c_m.dma(A, brB, rowb(I["b_res"], 0, D))
            c_m.dma(A, wdwC, I["w_dw"])
            rb = Ring(bank[0:3])
            tn = [None] * 6
            for oc in range(6):
                tst = []
                for b, (l0, n) in enumerate(BLK):
                    i, ps, f = rb.take()
                    for q in range(2):
                        tm = T.op(lambda e: e.matmul(ps[:, 0:n], Wc[:, q, 128 * oc:128 * oc + 128],
                                                     HQ[:, q, l0:l0 + n], start=q == 0, stop=q == 1), f, c_w.now)
                    ta = A.op(lambda e: e.activation(TT[:, oc, l0:l0 + n], ps[:, 0:n], ACT.Copy), tm)
                    rb.free[i] = ta
                    tst.append(V.op(lambda e: e.bn_stats(bst[:, b, :], TT[:, oc, l0:l0 + n]), ta,
                                    tn[oc - 1] if oc else None))
                    yield
                tk = V.op(lambda e: e.bn_aggr(bmv[:, oc, :], bst), *tst)
                tn[oc] = tk
                c1, c2 = bsc[:, oc:oc + 1], bbi[:, oc:oc + 1]
                tk = V.op(lambda e: e.tensor_scalar(c1, bmv[:, oc, 1:2], 1e-5, None, ALU.add), tk)
                tk = A.op(lambda e: e.activation(c1, c1, ACT.Sqrt), tk)
                tbn = V.chain([
                    lambda e: e.reciprocal(c1, c1),
                    lambda e: e.tensor_tensor(c1, c1, bng[:, oc:oc + 1], ALU.mult),
                    lambda e: e.tensor_tensor(c2, c1, bmv[:, oc, 0:1], ALU.mult),
                    lambda e: e.tensor_tensor(c2, bnb[:, oc:oc + 1], c2, ALU.subtract),
                ], tk, c_w.now)
            tconv = T.now
            tz = V.op(lambda e: e.memset(Wd, 0.0))
            for g in range(4):
                c_m.dma(S, Wd[32 * g:32 * g + 32, :, 32 * g:32 * g + 32], I["w_pw"][g], tz)
            for oc in range(6):
                twd = V.op(lambda e: e.tensor_scalar(Wd[:, oc, :], Wd[:, oc, :], wdwC[:, oc:oc + 1], None, ALU.mult),
                           c_m.now)
            yield
            rsq = Ring(sqb)
            rf = Ring([bank[4], bank[5]])

            def squares(src, k, last, tok):
                i, sq, f = rsq.take()
                n = src.shape[-1]
                ta = A.op(lambda e: e.activation(sq[:, 0:n], src, ACT.Square), f, tok)
                rsq.free[i] = T.op(lambda e: e.matmul(bank[3][:, 0:n], ones, sq[:, 0:n], start=k == 0, stop=k == last), ta)
                return ta

            def factor(n, free):
                a = A.op(lambda e: e.activation(nb[0][:, 0:n], bank[3][:, 0:n], ACT.Sqrt), T.now, free)
                t = V.chain([
                    lambda e: e.tensor_scalar(nb[0][:, 0:n], nb[0][:, 0:n], 1e-15, None, ALU.max),
                    lambda e: e.reciprocal(nb[1][:, 0:n], nb[0][:, 0:n]),
                    lambda e: e.scalar_tensor_tensor(nb[1][:, 0:n], nb[0][:, 0:n], T0, nb[1][:, 0:n], ALU.min, ALU.mult),
                ], a)
                return a, t

            fnorm = fnb = fO = None
            for b, (l0, n) in enumerate(BLK):
                tb = TT[:, :, l0:l0 + n]
                T.wait(fnorm)
                for oc in range(6):
                    ta = A.op(lambda e: e.activation(tb[:, oc, :], tb[:, oc, :], ACT.Relu, bias=bbi[:, oc:oc + 1],
                                                     scale=bsc[:, oc:oc + 1]), tbn)
                    squares(tb[:, oc, :], oc, 5, ta)
                fnorm, t = factor(n, fnb)
                tT = fnb = V.op(lambda e: e.tensor_tensor(tb, tb, bc(nb[1][:, 0:n], 1, 6), ALU.mult), t)
                T.wait(fnorm)
                yield
                for oc in range(6):
                    i, ps, f = rb.take()
                    tm = T.op(lambda e: e.matmul(ps[:, 0:n], Wd[:, oc, :], tb[:, oc, :], start=True, stop=True), f, tT, twd)
                    if oc < 4:
                        tv = V.op(lambda e: e.tensor_scalar(SB[:, oc, 0:n], ps[:, 0:n], 0.0, None, ALU.max), tm, tconv, fO)
                    else:
                        tv = V.op(lambda e: e.tensor_copy(SB[:, oc, 0:n], ps[:, 0:n]), tm, tconv, fO)
                    squares(tb[:, oc, :], 2 * oc, 11, tT)
                    rb.free[i] = squares(ps[:, 0:n], 2 * oc + 1, 11, tv)
                fnorm, t = factor(n, fnb)
                f2, g2 = nb[1][:, 0:n], nb[0][:, 0:n]
                V.op(lambda e: e.tensor_tensor(VF[:, 0:2, 0:n], tb[:, 4:6, :], bc(f2, 1, 2), ALU.mult), t, fO)
                V.op(lambda e: e.tensor_tensor(VF[:, 2:4, 0:n], SB[:, 4:6, 0:n], bc(f2, 1, 2), ALU.mult))
                V.op(lambda e: e.tensor_tensor(g2, f2, f2, ALU.mult))
                t = V.chain([
                    lambda e: e.tensor_scalar(RD[:, :, 0:n], VF[:, :, 0:n], 1e-15, None, ALU.add),
                    lambda e: e.reciprocal(RD[:, :, 0:n], RD[:, :, 0:n]),
                    lambda e: e.tensor_tensor(VF[:, :, 0:n], VF[:, :, 0:n], RD[:, :, 0:n], ALU.mult),
                    lambda e: e.tensor_tensor(VF[:, :, 0:n], VF[:, :, 0:n], bc(g2, 1, 4), ALU.mult),
                    lambda e: e.tensor_tensor(VF[:, 0:2, 0:n], VF[:, 0:2, 0:n], tb[:, 0:2, :], ALU.mult),
                    lambda e: e.tensor_tensor(VF[:, 2:4, 0:n], VF[:, 2:4, 0:n], SB[:, 0:2, 0:n], ALU.mult),
                ], V.now)
                fnb = V.now
                yield
                tv = V.now
                for q in range(4):
                    i, ps, f = rb.take()
                    kk = tb[:, 2 + q, :] if q < 2 else SB[:, q, 0:n]
                    tm = T.op(lambda e: e.matmul(ps[:, 0:n], blk, kk, start=True, stop=True), f, tv, c_in.now)
                    tv = rb.free[i] = V.op(lambda e: e.tensor_tensor(VF[:, q, 0:n], VF[:, q, 0:n], ps[:, 0:n], ALU.mult),
                                           tm, t)
                    ta = A.op(lambda e: e.activation(RD[:, q, 0:n], VF[:, q, 0:n], ACT.Square), tv)
                for m0 in range(0, n, P):
                    tile = (l0 + m0) // P
                    i, ps, f = rf.take()
                    T.wait(f, ta, tv, c_m.now)
                    for q in range(4):
                        T.op(lambda e: e.matmul(ps[0:P, 0:D], VF[:, q, m0:m0 + P], wres[:, q, :], start=q == 0, stop=q == 3))
                    for q in range(4):
                        tm = T.op(lambda e: e.matmul(ps[0:P, D:D + 1], RD[:, q, m0:m0 + P], ones[:, 0:1], start=q == 0,
                                                     stop=q == 3))
                    V.op(lambda e: e.tensor_copy(FX[:, tile, :], ps[0:P, 0:D]), tm)
                    tv2 = rf.free[i] = V.op(lambda e: e.tensor_copy(ss3[:, tile:tile + 1], ps[0:P, D:D + 1]))
                fO = tm
                yield
            XL = mem[0:P, BASE:BASE + NT * D].rearrange("p (t d) -> p t d", d=D)
            tx = c_x.dma125(S, XL, I["x"].rearrange("(t p) d -> p t d", p=P), A.now, V.now, T.now)
            a = A.op(lambda e: e.activation(ss3, ss3, ACT.Sqrt), tv2)
            t = V.chain([
                lambda e: e.tensor_scalar(ss3, ss3, 1e-15, None, ALU.max),
                lambda e: e.reciprocal(f3, ss3),
                lambda e: e.scalar_tensor_tensor(f3, ss3, T0, f3, ALU.min, ALU.mult),
            ], a)
            for m in range(NT):
                t1 = V.op(lambda e: e.scalar_tensor_tensor(FX[:, m, :], FX[:, m, :], f3[:, m:m + 1], brB[0:P, :],
                                                           ALU.mult, ALU.add), t, c_m.now)
                a = A.op(lambda e: e.activation(sqb[0][0:P, 0:D], FX[:, m, :], ACT.Square, accum_out=ss4[:, m:m + 1]),
                         t1, rsq.free, A.now)
            yield
            a = A.op(lambda e: e.activation(ss4, ss4, ACT.Sqrt), a)
            t = V.op(lambda e: e.tensor_scalar(n4, ss4, 1e-15, None, ALU.max), a)
            a = A.op(lambda e: e.activation(f4, n4, ACT.Tanh), t)
            t = V.chain([
                lambda e: e.reciprocal(n4, n4),
                lambda e: e.scalar_tensor_tensor(f4, f4, MX, n4, ALU.min, ALU.mult),
            ], a)
            for m in range(NT):
                V.op(lambda e: e.scalar_tensor_tensor(X[:, m, :], FX[:, m, :], f4[:, m:m + 1], XL[:, m, :],
                                                      ALU.mult, ALU.add), t, tx)
            yield

        def run(*gens):
            parts = [[g, n, 0] for g, n in gens]
            while parts:
                p = min(parts, key=lambda p: p[2] / p[1])
                p[2] += 1
                if next(p[0], p) is p:
                    parts.remove(p)

        zero = own.get(D)
        tz = V.op(lambda e: e.memset(zero, 0.0))
        chan().dma(A, xs_d.rearrange("(s p) d -> p s d", p=128), bc(zero, 1, MS // 128), tz)
        run((pass1(), 196), (edge_logits(), 98), (mixer0(), 66))
        barrier()

        def softmax(z, ex, dst, ar, heads, tok):
            same = ar.get(C)
            pf = ar.get(C)
            pb = ar.get(C)
            fw = ar.get(C)
            bw = ar.get(C)
            uu = ar.get(C)
            row = ar.get(8, 128)
            col = ar.get(8)
            cols = ar.get(2)
            tk = V.op(lambda e: e.tensor_tensor(same[:, 1:C], dst[:, 1:C], dst[:, 0:C - 1], ALU.not_equal), tok)
            V.op(lambda e: e.memset(pf[:, 0:1], -BIG))
            V.op(lambda e: e.memset(pb[:, C - 1:C], -BIG))
            V.op(lambda e: e.tensor_scalar(pf[:, 1:C], same[:, 1:C], -BIG, None, ALU.mult), tk)
            tpb = V.op(lambda e: e.tensor_scalar(pb[:, 0:C - 1], same[:, 1:C], -BIG, None, ALU.mult))
            cat = bank[0]
            T.op(lambda e: e.transpose(cat[0:1, 0:128], dst[:, 0:1], ident), tok)
            tt1 = T.op(lambda e: e.transpose(cat[0:1, 128:256], dst[:, C - 1:C], ident))
            fd, ld, df, db, ca, cb, wk = (row[0:1, i, :] for i in range(7))
            wide = lambda i: row[0:1, i, :]
            t = V.chain([
                lambda e: e.tensor_copy(fd, cat[0:1, 0:128]),
                lambda e: e.tensor_copy(ld, cat[0:1, 128:256]),
                lambda e: e.tensor_tensor(wk, fd, ld, ALU.not_equal),
                lambda e: e.tensor_tensor(ca[:, 1:128], fd[:, 1:128], ld[:, 0:127], ALU.not_equal),
                lambda e: e.memset(ca[:, 0:1], 1.0),
                lambda e: e.tensor_copy(cb[:, 0:127], ca[:, 1:128]),
                lambda e: e.memset(cb[:, 127:128], 1.0),
                lambda e: e.tensor_tensor(df, wk, ca, ALU.add),
                lambda e: e.tensor_tensor(db, wk, cb, ALU.add),
                lambda e: e.tensor_scalar(df, df, -BIG, None, ALU.mult),
                lambda e: e.tensor_scalar(db, db, -BIG, None, ALU.mult),
                lambda e: e.tensor_scalar(ca, ca, -BIG, None, ALU.mult),
                lambda e: e.tensor_scalar(cb, cb, -BIG, None, ALU.mult),
            ], tt1)
            tlast = None
            for h in range(heads):
                zh, eh = z(h), ex(h)
                t1 = V.op(lambda e, zh=zh: e.tensor_tensor_scan(fw, pf, zh, 0.0, ALU.add, ALU.max), t, tpb, tlast)
                t2 = V.op(lambda e, zh=zh: e.tensor_tensor_scan(bw[:, ::-1], pb[:, ::-1], zh[:, ::-1], 0.0, ALU.add,
                                                                ALU.max))
                T.op(lambda e: e.transpose(cat[0:1, 0:128], fw[:, C - 1:C], ident), t1, t)
                tp = T.op(lambda e: e.transpose(cat[0:1, 128:256], bw[:, 0:1], ident), t2)
                sf, sb_ = wide(6), wide(7)
                tv = V.chain([
                    lambda e: e.tensor_tensor_scan(sf, df, cat[0:1, 0:128], 0.0, ALU.add, ALU.max),
                    lambda e: e.tensor_tensor_scan(sb_[:, ::-1], db[:, ::-1], cat[0:1, 128:256][:, ::-1], 0.0, ALU.add,
                                                   ALU.max),
                    lambda e: e.tensor_tensor(fd[:, 1:128], sf[:, 0:127], ca[:, 1:128], ALU.add),
                    lambda e: e.memset(fd[:, 0:1], -BIG),
                    lambda e: e.tensor_tensor(ld[:, 0:127], sb_[:, 1:128], cb[:, 0:127], ALU.add),
                    lambda e: e.memset(ld[:, 127:128], -BIG),
                ], tp)
                T.op(lambda e: e.matmul(bank[1][:, 0:1], fd, ones[0:1, 0:1], start=True, stop=True), tv)
                tm = T.op(lambda e: e.matmul(bank[1][:, 1:2], ld, ones[0:1, 0:1], start=True, stop=True))
                tv = V.chain([
                    lambda e: e.tensor_copy(cols, bank[1][:, 0:2]),
                    lambda e: e.tensor_tensor(fw, fw, bw, ALU.max),
                    lambda e: e.tensor_scalar(uu, dst, dst[:, 0:1], -BIG, ALU.not_equal, ALU.mult),
                    lambda e: e.scalar_tensor_tensor(fw, uu, cols[:, 0:1], fw, ALU.add, ALU.max),
                    lambda e: e.tensor_scalar(uu, dst, dst[:, C - 1:C], -BIG, ALU.not_equal, ALU.mult),
                    lambda e: e.scalar_tensor_tensor(fw, uu, cols[:, 1:2], fw, ALU.add, ALU.max),
                    lambda e, zh=zh: e.tensor_tensor(fw, zh, fw, ALU.subtract),
                ], tm)
                tlast = A.op(lambda e, eh=eh: e.activation(eh, fw, ACT.Exp), tv)
            return tlast

        s3 = Arena(BASE)
        rec0 = s3.get(C, 2)
        aa = s3.get(C)
        zz = s3.get(C)
        t = V.chain([
            lambda e: e.tensor_tensor(zz, Pt, tt, ALU.add),
            lambda e: e.tensor_scalar(zz, zz, wB[:, 128:129], None, ALU.add),
            lambda e: e.tensor_scalar(aa, zz, 0.01, None, ALU.mult),
            lambda e: e.tensor_tensor(aa, aa, zz, ALU.max),
            lambda e: e.tensor_copy(rec0[:, :, 0], dstF),
        ])
        tx = softmax(lambda h: aa, lambda h: rec0[:, :, 1], dstF, s3, 1, t)
        c_r = chan()
        trec = c_r.dma(S, rec0_d.rearrange("(p c) f -> p c f", p=128), rec0, tx, t)
        cnt = s3.get(NT - 1)
        GJ = s3.get(NT - 1)
        GI = s3.get(NT - 1, dt=I32)
        jn = s3.get(NT - 1)
        gs = s3.get(NS)
        cmp = s3.get(NS, NT - 1)
        TJ = s3.get(NS)
        c_g = chan()
        c_g.dma(S, gs, I["c_steps"])
        for j in range(1, NT):
            tk = V.op(lambda e, j=j: e.tensor_scalar(aa, dstF, float(P * j), None, ALU.is_lt, ALU.add,
                                                     accum_out=cnt[:, j - 1:j]), tx, V.now)
        tm = T.op(lambda e: e.matmul(bank[2][:, 0:NT - 1], ones, cnt, start=True, stop=True), tk)
        tk = V.chain([
            lambda e: e.tensor_copy(GI, bank[2][:, 0:NT - 1]),
            lambda e: e.tensor_scalar(GI, GI, 9, None, ALU.arith_shift_right),
            lambda e: e.tensor_copy(GJ, GI),
            lambda e: e.tensor_tensor(GJ, GJ, iota[:, 1:NT], ALU.add),
            lambda e: e.tensor_tensor(cmp, bc(GJ, 1, NS), bc(gs, 2, NT - 1), ALU.is_le),
            lambda e: e.tensor_reduce(TJ, cmp, X_AX, ALU.add),
            lambda e: e.tensor_scalar(JV, TJ, float(P), None, ALU.mult),
            lambda e: e.tensor_copy(REG[:, 0, :], TJ),
            lambda e: e.tensor_tensor(TJ, gs, TJ, ALU.subtract),
            lambda e: e.tensor_copy(REG[:, 1, :], TJ),
        ], tm, c_g.now)
        tstep = tk
        barrier()

        def steps(acc, rows, rec, width, nrec, make, ar, tz):
            nb = 4
            rbuf = [ar.get(4, width) for _ in range(nb)]
            qbuf = [ar.get(4, nrec) for _ in range(nb)]
            mbuf = [ar.get(4, P) for _ in range(3)]
            dl = [ar.get(4) for _ in range(3)]
            rr, rq, rm, rdl = Ring(rbuf), Ring(qbuf), Ring(mbuf), Ring(dl)
            rp = Ring(bank[0:4])
            cr = [chan() for _ in range(nb)]
            r_v = rows.rearrange("(t p i) d -> t p (i d)", p=128, i=4)
            q_v = rec.rearrange("(t p i) f -> t p (i f)", p=128, i=4)
            last = tz
            LAG = 2
            pend = {}

            def add(g):
                ps, w, tm, ip = pend.pop(g)
                reg = V.engine.value_load(REG[0:1, 0, g:g + 1], min_val=0, max_val=NT - 1)
                a = acc[:, bass.ds(reg, 1), 0:w].rearrange("p a c -> p (a c)")
                rp.free[ip] = V.op(lambda e: e.tensor_tensor(a, a, ps[0:P, 0:w], ALU.add), tm, last)
                return rp.free[ip]

            for g in range(NS):
                i, rb_, fr = rr.take()
                _, qb_, _ = rq.take()
                S.wait(fr)
                cr[i].n += 32

                def load(e, g=g, rb_=rb_, qb_=qb_, s=cr[i].sem):
                    t = e.value_load(REG[0:1, 1, g:g + 1], min_val=0, max_val=NTI - 1)
                    e.dma_start(rb_.rearrange("p i d -> p (i d)"),
                                r_v[bass.ds(t, 1), :, :].rearrange("a p c -> (a p) c")).then_inc(s, 16)
                    e.dma_start(qb_.rearrange("p i f -> p (i f)"),
                                q_v[bass.ds(t, 1), :, :].rearrange("a p c -> (a p) c")).then_inc(s, 16)
                S.do(load)
                tin = cr[i].now
                im, M, fm = rm.take()
                _, dd, _ = rdl.take()
                td = V.op(lambda e, g=g, dd=dd, qb_=qb_: e.tensor_scalar(dd, qb_[:, :, 0], JV[:, g:g + 1], None,
                                                                            ALU.subtract), tin, fm)
                lhs, rhs, tv = make(M, dd, rb_, qb_, td, tin)
                ip, ps, fp = rp.take()
                T.wait(tv, tin, fp)
                for k in range(4):
                    tm = T.op(lambda e, k=k, ps=ps, lhs=lhs, rhs=rhs: e.matmul(ps[0:P, 0:rhs(k).shape[-1]], lhs[:, k, :],
                                                                               rhs(k), start=k == 0, stop=k == 3))
                rm.free[im] = tm
                rr.free[i] = tm
                pend[g] = (ps, rhs(0).shape[-1], tm, ip)
                if g >= LAG:
                    last = add(g - LAG)
            for g in range(NS - LAG, NS):
                last = add(g)
            return last

        s3 = Arena(BASE)
        acc0 = s3.get(NT, RW, parts=P)
        tz = V.op(lambda e: e.memset(acc0, 0.0))

        def make0(M, dd, rb_, qb_, td, tin):
            for k in range(4):
                tv = V.op(lambda e, k=k: e.tensor_scalar(M[:, k, :], iota[:, 0:P], dd[:, k:k + 1], qb_[:, k, 1:2],
                                                         ALU.is_equal, ALU.mult), td)
            return M, (lambda k: rb_[:, k, 0:D + 1]), tv

        last = steps(acc0, hs_d, rec0_d, RW, 2, make0, s3, tz)
        den = s3.get(NT, parts=P)
        t = V.chain([
            lambda e: e.tensor_scalar(den, acc0[:, :, D], 1e-16, None, ALU.add),
            lambda e: e.reciprocal(den, den),
        ], last)
        for m in range(NT):
            t1 = V.op(lambda e, m=m: e.tensor_scalar(acc0[:, m, 0:D], acc0[:, m, 0:D], den[:, m:m + 1], 0.0,
                                                     ALU.mult, ALU.max), t)
        tX = V.op(lambda e: e.tensor_tensor(X, X, acc0[:, :, 0:D], ALU.add), t1)
        barrier()

        def experts(ar, NE, y, wall, b2, gw, gb, func, weighted):
            nsl = (2 * N + NE * 127) // 128
            acc = ar.get(NT, D, parts=P)
            wb_ = [ar.get(WROW) for _ in range(5)]
            xb = [ar.get(2, D) for _ in range(3)]
            xTb = [ar.get(2, 128) for _ in range(2)]
            hTb = [ar.get(4, 128) for _ in range(2)]
            yb = [ar.get(D) for _ in range(3)]
            gb_ = [ar.get(2, D, parts=P) for _ in range(4)]
            yTb = [ar.get(2, P) for _ in range(3)]
            b2r = ar.get(D)
            gwc = ar.get(2, NE)
            gbB = ar.get(NE)
            lg = ar.get(NT, NE, parts=P)
            gate = ar.get(NT, NE, parts=P)
            oh1 = ar.get(NT, NE, parts=P)
            oh2 = ar.get(NT, NE, parts=P)
            cm = ar.get(NT, NE, parts=P)
            keep = ar.get(NE, NT, parts=P)
            cum = ar.get(NE, NT, parts=P)
            slot = ar.get(NE, NT, parts=P)
            mx = ar.get(NT, 8, parts=P)
            mi = ar.get(NT, 8, parts=P, dt=U32)
            mf = ar.get(NT, 8, parts=P)
            wa = ar.get(NT, parts=P)
            wb = ar.get(NT, parts=P)
            sl = ar.get(2, NT, parts=P)
            slI = ar.get(2, NT, parts=P, dt=I32)
            cnt = ar.get(NE, parts=P)
            cntI = ar.get(NE, parts=P, dt=I32)
            t0 = ar.get(NE, parts=P)
            cmp = ar.get(nsl, NE - 1, parts=P)
            es = ar.get(nsl, parts=P)
            esI = ar.get(nsl, parts=P, dt=I32)
            gT = ar.get(NT, P)
            cs = chan()
            cs.dma(A, b2r[0:NE, :], b2)
            cs.dma(A, gwc, gw.rearrange("(k p) n -> p k n", p=128))
            cs.dma(A, gbB, rowb(gb, 0, NE))
            rt = Ring(bank[0:2])
            ry = Ring(yTb)
            for t in range(NT):
                i, b, f = rt.take()
                for k in range(2):
                    tp = T.op(lambda e, t=t, k=k, b=b: e.transpose(b[:, k * P:(k + 1) * P], y[:, t, 128 * k:128 * k + 128],
                                                                  ident[0:P, 0:P]), f)
                iy, yT, fy = ry.take()
                rt.free[i] = ta = A.op(lambda e, yT=yT, b=b: e.activation(
                    yT, b[:, 0:2 * P].rearrange("p (k n) -> p k n", k=2), ACT.Copy), tp, fy)
                for k in range(2):
                    tm = T.op(lambda e, t=t, k=k, yT=yT: e.matmul(bank[2][0:P, NE * t:NE * t + NE], yT[:, k, :],
                                                                 gwc[:, k, :], start=k == 0, stop=k == 1), ta, cs.now)
                ry.free[iy] = tm
            tk = V.op(lambda e: e.tensor_tensor(lg, bank[2][0:P, 0:NT * NE].rearrange("p (t n) -> p t n", n=NE),
                                                bc(gbB[0:P, :], 1, NT), ALU.add), tm, cs.now)
            for t in range(NT):
                tk1 = V.op(lambda e, t=t: e.max(mx[:, t, :], lg[:, t, :]), tk)
            for t in range(NT):
                tk1 = V.op(lambda e, t=t: e.max_index(mi[:, t, :], mx[:, t, :], lg[:, t, :]), tk1)
            io = bc(iota[0:P, 0:NE], 1, NT)
            tc = V.chain([
                lambda e: e.tensor_copy(mf, mi),
                lambda e: e.tensor_tensor(oh1, io, bc(mf[:, :, 0], 2, NE), ALU.is_equal),
                lambda e: e.tensor_tensor(oh2, io, bc(mf[:, :, 1], 2, NE), ALU.is_equal),
                lambda e: e.tensor_tensor(cm, oh1, oh2, ALU.add),
            ], tk1)
            cme = cm.rearrange("p t e -> p e t")
            T.op(lambda e: e.matmul(bank[3][0:P, 0:NT * NE], tri[0:P, 0:P], cme, start=True, stop=True), tc)
            tm = T.op(lambda e: e.matmul(bank[4][0:P, 0:NT * NE], ones[0:P, 0:P], cme, start=True, stop=True))
            pre = bank[3][0:P, 0:NT * NE].rearrange("p (e t) -> p e t", t=NT)
            tot = bank[4][0:P, 0:NT * NE].rearrange("p (e t) -> p e t", t=NT)
            flat = lambda v: v.rearrange("p e t -> p (e t)")
            ts = V.chain([
                lambda e: e.memset(keep, 1.0),
                lambda e: e.memset(keep[:, :, 0:1], 0.0),
                lambda e: e.tensor_tensor_scan(flat(cum), flat(keep), bank[4][0:P, 0:NT * NE], 0.0, ALU.mult, ALU.add),
                lambda e: e.tensor_scalar(cntI, cum[:, :, NT - 1], 127.0, None, ALU.add),
                lambda e: e.tensor_scalar(cntI, cntI, 7, None, ALU.arith_shift_right),
                lambda e: e.tensor_copy(cnt, cntI),
                lambda e: e.tensor_tensor_scan(t0, ones[0:P, 0:NE], cnt, 0.0, ALU.mult, ALU.add),
                lambda e: e.tensor_tensor(t0, t0, cnt, ALU.subtract),
                lambda e: e.tensor_tensor(cmp, bc(t0[:, 1:NE], 1, nsl), bc(iota[0:P, 0:nsl], 2, NE - 1), ALU.is_le),
                lambda e: e.tensor_reduce(es, cmp, X_AX, ALU.add),
                lambda e: e.tensor_copy(esI, es),
            ], tm)
            tl = V.chain([
                lambda e: e.tensor_tensor(slot, cum, tot, ALU.subtract),
                lambda e: e.tensor_tensor(slot, slot, pre, ALU.add),
                lambda e: e.scalar_tensor_tensor(slot, bc(t0, 2, NT), 128.0, slot, ALU.mult, ALU.add),
                lambda e: e.tensor_tensor(cm, slot.rearrange("p e t -> p t e"), oh1, ALU.mult),
                lambda e: e.tensor_reduce(sl[:, 0, :], cm, X_AX, ALU.add),
                lambda e: e.tensor_tensor(cm, slot.rearrange("p e t -> p t e"), oh2, ALU.mult),
                lambda e: e.tensor_reduce(sl[:, 1, :], cm, X_AX, ALU.add),
                lambda e: e.tensor_copy(slI, sl),
            ], ts)
            csc = chan()
            G.wait(tl)
            for t in range(NT):
                for k in range(2):
                    csc.n += 16
                    G.do(lambda e, t=t, k=k: e.indirect_dma_start(
                        out=xs_d, out_offset=bass.IndirectOffsetOnAxis(ap=slI[:, k, t:t + 1], axis=0),
                        in_=y[:, t, :], in_offset=None).then_inc(csc.sem, 16))
            tsc = csc.now
            tg = tl
            if weighted:
                tk = V.op(lambda e: e.tensor_tensor(wb, mx[:, :, 1], mx[:, :, 0], ALU.subtract), tl)
                tk = A.op(lambda e: e.activation(wb, wb, ACT.Exp), tk)
                tg = V.chain([
                    lambda e: e.tensor_scalar(wa, wb, 1.0, None, ALU.add),
                    lambda e: e.reciprocal(wa, wa),
                    lambda e: e.tensor_tensor(wb, wb, wa, ALU.mult),
                    lambda e: e.tensor_tensor(oh1, oh1, bc(wa, 2, NE), ALU.mult),
                    lambda e: e.tensor_tensor(oh2, oh2, bc(wb, 2, NE), ALU.mult),
                ], tk)
            tg = V.op(lambda e: e.tensor_tensor(gate, oh1, oh2, ALU.add), tg)
            rg2 = Ring(bank[5:8])
            tgT = []
            for t in range(NT):
                i, b, f = rg2.take()
                tp = T.op(lambda e, t=t, b=b: e.transpose(b[0:NE, 0:P], gate[:, t, :], ident[0:P, 0:P]), tg, f)
                rg2.free[i] = A.op(lambda e, t=t, b=b: e.activation(gT[0:NE, t, :], b[0:NE, 0:P], ACT.Copy), tp)
                tgT.append(rg2.free[i])
            for t in range(NT):
                i, b, f = rg2.take()
                tm = T.op(lambda e, t=t, b=b: e.matmul(b[0:P, 0:D], gT[0:NE, t, :], b2r[0:NE, :], start=True,
                                                       stop=True), tgT[t], f)
                rg2.free[i] = tacc = V.op(lambda e, t=t, b=b: e.tensor_copy(acc[:, t, :], b[0:P, 0:D]), tm)
            rw, rx, rxT, rh, ryb = Ring(wb_), Ring(xb), Ring(xTb), Ring(hTb), Ring(yb)
            cw = [chan() for _ in wb_]
            cx = [chan() for _ in xb]
            cy = [chan() for _ in yb]
            rbt, rb1, rb2 = Ring(bank[0:2]), Ring(bank[2:5]), Ring(bank[5:8])
            rbt.free = [T.now, T.now]
            rb1.free = [T.now, ts, tl]
            rb2.free = rg2.free
            xs_v = xs_d[0:128 * nsl, :].rearrange("(s p) d -> p s d", p=128)
            S.wait(ts)
            xt, wt = {}, {}

            def fetch(s):
                i, w, f = rw.take()
                S.wait(f)
                reg = S.engine.value_load(esI[0:1, s:s + 1], min_val=0, max_val=NE - 1)
                wt[s] = (i, w, cw[i].dma(S, w, wall[bass.ds(reg, 1), :, :].rearrange("a p c -> (a p) c")))

            def turn(s):
                if s % 2 == 0:
                    i, x_, f = rx.take()
                    n = min(2, nsl - s)
                    turn.x = (i, x_, cx[i].dma(S, x_[:, 0:n, :], xs_v[:, s:s + n, :], f, tsc))
                i, x_, tin = turn.x
                ib, b, f = rbt.take()
                for k in range(2):
                    tp = T.op(lambda e: e.transpose(b[:, 128 * k:128 * k + 128], x_[:, s % 2, 128 * k:128 * k + 128], ident),
                              tin, f)
                rx.free[i] = tp
                it, x_T, ft = rxT.take()
                rbt.free[ib] = tv = V.op(lambda e: e.tensor_copy(x_T, b[:, 0:256].rearrange("p (k n) -> p k n", k=2)), tp, ft)
                xt[s] = (it, x_T, tv)

            def first(s):
                it, x_T, tv = xt.pop(s)
                iw, w, tw = wt[s]
                ib, b, f = rb1.take()
                ih, h, fh = rh.take()
                for c in range(4):
                    for q in range(2):
                        tm = T.op(lambda e: e.matmul(b[:, 128 * c:128 * c + 128], w[:, 512 * q + 128 * c:512 * q + 128 * c + 128],
                                                     x_T[:, q, :], start=q == 0, stop=q == 1), tv, tw, f)
                rxT.free[it] = tm
                for c in range(4):
                    ta = A.op(lambda e: e.activation(h[:, c, :], b[:, 128 * c:128 * c + 128], func,
                                                     bias=w[:, 2048 + c:2049 + c]), tm, fh)
                rb1.free[ib] = ta
                return ih, h, ta

            def second(s, ih, h, ta):
                iw, w, tw = wt.pop(s)
                ib, b, f = rb2.take()
                for c in range(4):
                    tm = T.op(lambda e: e.matmul(b[:, 0:D], h[:, c, :], w[:, 1024 + D * c:1024 + D * c + D], start=c == 0,
                                                 stop=c == 3), ta, f)
                rh.free[ih] = rw.free[iw] = tm
                iy, o, fy = ryb.take()
                rb2.free[ib] = tv = V.op(lambda e: e.tensor_copy(o, b[:, 0:D]), tm, fy)
                ryb.free[iy] = cy[iy].dma(S, ys_d[128 * s:128 * s + 128, :], o, tv)

            for s in range(3):
                fetch(s)
            turn(0)
            late = None
            for s in range(nsl):
                if s + 3 < nsl:
                    fetch(s + 3)
                if s + 1 < nsl:
                    turn(s + 1)
                now = first(s)
                if late:
                    second(s - 1, *late)
                late = now
            second(nsl - 1, *late)
            rg = Ring(gb_)
            cg = [chan() for _ in gb_]
            G.wait(ryb.free)
            for t in range(NT):
                i, g, f = rg.take()
                G.wait(f)
                for k in range(2):
                    cg[i].n += 16
                    G.do(lambda e: e.indirect_dma_start(
                        out=g[:, k, :], out_offset=None, in_=ys_d,
                        in_offset=bass.IndirectOffsetOnAxis(ap=slI[:, k, t:t + 1], axis=0)).then_inc(cg[i].sem, 16))
                tv = tacc
                for k, wk in ((0, wa), (1, wb)):
                    if weighted:
                        tv = V.op(lambda e: e.scalar_tensor_tensor(acc[:, t, :], g[:, k, :], wk[:, t:t + 1], acc[:, t, :],
                                                                   ALU.mult, ALU.add), cg[i].now, tv, tg)
                    else:
                        tv = V.op(lambda e: e.tensor_tensor(acc[:, t, :], acc[:, t, :], g[:, k, :], ALU.add), cg[i].now, tv)
                rg.free[i] = tv
            return acc, tv

        f0 = Arena(BASE)
        Y = f0.get(NT, D, parts=P)
        gam = f0.get(D)
        bet = f0.get(D)
        c_f = chan()
        c_f.dma(A, gam, rowb(I["f0_gamma"], 0, D))
        c_f.dma(A, bet, rowb(I["f0_beta"], 0, D))
        ty = ln_apply(Y, X, ln_stats(X, 1e-5))
        T.wait(ty)
        moe, tmoe = experts(f0, 16, Y, I["f0_w"], I["f0_b2"], I["f0_gw"], I["f0_gb"],
                            ACT.Relu, True)
        t = V.op(lambda e: e.tensor_tensor(Y, Y, moe, ALU.add), tmoe, T.now)
        tl = ln_apply(Y, Y, ln_stats(Y, 1e-5, t))
        for m in range(NT):
            t1 = V.op(lambda e, m=m: e.tensor_tensor(Y[:, m, :], Y[:, m, :], gam[0:P, :], ALU.mult), tl[m], c_f.now)
            t1 = V.op(lambda e, m=m: e.tensor_tensor(Y[:, m, :], Y[:, m, :], bet[0:P, :], ALU.add), t1)
        t1 = V.op(lambda e: e.tensor_tensor(X, X, Y, ALU.add), t1)
        barrier()

        g1 = Arena(BASE)
        XN = g1.get(NT, D, parts=P)
        dstF = g1.get(C)
        qI = g1.get(C, dt=I32)
        kvI = g1.get(C, dt=I32)
        SC = g1.get(C, 4)
        ntI = g1.get(NT, parts=P, dt=I32)
        ntF = g1.get(NT, parts=P)
        mk = g1.get(4, NT, parts=P)
        g1_own = g1.at
        s5 = Arena(g1.at)
        tyl = ln_apply(XN, X, ln_stats(X, 1e-5))
        srcI = s5.get(C, dt=I32)
        dstI = s5.get(C, dt=I32)
        etI = s5.get(C, dt=I32)
        f1_, f2_ = s5.get(C), s5.get(C)
        c_5 = chan()
        c_5.dma(S, srcI, I["src"])
        c_5.dma(S, dstI, I["dst"])
        c_5.dma(S, etI, I["etype"])
        c_5.dma(S, ntI, I["ntype"])
        V.chain([
            lambda e: e.tensor_copy(dstF, dstI),
            lambda e: e.tensor_scalar(f1_, dstF, float(N - 1), None, ALU.min),
            lambda e: e.tensor_copy(qI, f1_),
            lambda e: e.tensor_copy(f1_, srcI),
            lambda e: e.tensor_copy(f2_, etI),
            lambda e: e.scalar_tensor_tensor(f2_, f2_, float(N), f1_, ALU.mult, ALU.add),
            lambda e: e.tensor_copy(kvI, f2_),
            lambda e: e.tensor_copy(ntF, ntI),
        ], c_5.now)
        tmk = V.now
        for a in range(4):
            tmk = V.op(lambda e, a=a: e.tensor_scalar(mk[:, a, :], ntF, float(a), None, ALU.is_equal), V.now)
        LW = [s5.get(2, 1024) for _ in range(3)]
        RA = [s5.get(2, 1024) for _ in range(2)]
        priB = s5.get(32)
        c_l = chan()
        for m, name in enumerate(("k_lin", "q_lin", "v_lin")):
            for kc in range(2):
                c_l.dma(A, LW[m][:, kc, :].rearrange("p (t n) -> p t n", t=4),
                        I[name][:, 128 * kc:128 * kc + 128, :].rearrange("t p n -> p t n"))
        c_l.dma(A, priB, rowb(I["pri"], 0, 32))
        tz = [V.op(lambda e, m=m: e.memset(RA[m], 0.0)) for m in range(2)][-1]
        for m, name in enumerate(("att", "msg")):
            for h in range(4):
                hc, i = h // 2, h % 2
                c_l.dma(A, RA[m][64 * i:64 * i + 64, hc, :].rearrange("p (r o) -> p r o", r=8)[:, :, 64 * i:64 * i + 64],
                        I[name][h], tz)
        tk = V.op(lambda e: e.tensor_scalar(priB, priB, 0.125, None, ALU.mult), c_l.now)
        for hc in range(2):
            tk = V.op(lambda e, hc=hc: e.tensor_tensor(
                RA[0][:, hc, :].rearrange("p (r i d) -> p r i d", r=8, i=2),
                RA[0][:, hc, :].rearrange("p (r i d) -> p r i d", r=8, i=2),
                bc(priB.rearrange("p (r h i) -> p r h i", r=8, h=2)[:, :, hc, :], 3, 64), ALU.mult), tk)
        tra = tk
        XTb = [s5.get(2, P) for _ in range(2)]
        kqv = [[s5.get(D, parts=P) for _ in range(2)] for _ in range(3)]
        KTb = [s5.get(4, P) for _ in range(2)]
        KVo = [s5.get(8, 512, parts=P) for _ in range(2)]
        rx, rk, ro = Ring(XTb), Ring(KTb), Ring(KVo)
        rq = [Ring(b) for b in kqv]
        rb = Ring(bank[0:2])
        rm = Ring(bank[2:5])
        ro_ps = Ring(bank[5:8])
        c_q = [chan() for _ in range(2)]
        c_kv = [chan() for _ in range(2)]
        kv_v = kv_d.rearrange("(r n) d -> n r d", r=8)
        T.wait(tyl)
        for t in range(NT):
            i, b, f = rb.take()
            for k in range(2):
                tp = T.op(lambda e, t=t, k=k, b=b: e.transpose(b[:, k * P:(k + 1) * P], XN[:, t, 128 * k:128 * k + 128],
                                                              ident[0:P, 0:P]), f)
            ix, xt, fx = rx.take()
            ta = A.op(lambda e, b=b, xt=xt: e.activation(xt, b[:, 0:2 * P].rearrange("p (k n) -> p k n", k=2), ACT.Copy),
                      tp, fx)
            rb.free[i] = ta
            tdone = []
            outs = []
            for m in range(3):
                iq, o, fo = rq[m].take()
                tv = None
                for half in range(2):
                    im, ps, fm = rm.take()
                    for k in range(2):
                        tm = T.op(lambda e, m=m, k=k, half=half, ps=ps, xt=xt: e.matmul(
                            ps[0:P, :], xt[:, k, :], LW[m][:, k, 512 * half:512 * half + 512], start=k == 0, stop=k == 1),
                            ta, fm, c_l.now)
                    for a in range(2):
                        ty = 2 * half + a
                        if ty == 0:
                            tv = V.op(lambda e, o=o, ps=ps, t=t: e.tensor_scalar(o, ps[0:P, 0:D], mk[:, 0, t:t + 1], None,
                                                                                 ALU.mult), tm, fo, tmk)
                        else:
                            tv = V.op(lambda e, o=o, ps=ps, t=t, a=a, ty=ty: e.scalar_tensor_tensor(
                                o, ps[0:P, D * a:D * a + D], mk[:, ty, t:t + 1], o, ALU.mult, ALU.add), tm, tv)
                    rm.free[im] = tv
                outs.append((iq, o))
                tdone.append(tv)
            rx.free[ix] = tm
            iq, o = outs[1]
            rq[1].free[iq] = c_q[iq].dma125(S, q_d[P * t:P * t + P, :], o, tdone[1])
            i, b, f = rb.take()
            T.wait(f, tdone)
            for m in (0, 2):
                o = outs[m][1]
                for k in range(2):
                    c = m + k
                    tp = T.op(lambda e, o=o, k=k, c=c, b=b: e.transpose(b[:, c * P:(c + 1) * P], o[:, 128 * k:128 * k + 128],
                                                                       ident[0:P, 0:P]))
            for m in (0, 2):
                rq[m].free[outs[m][0]] = tp
            ik, kt, fk = rk.take()
            ta = A.op(lambda e, b=b, kt=kt: e.activation(kt, b[:, 0:4 * P].rearrange("p (k n) -> p k n", k=4), ACT.Copy),
                      tp, fk)
            rb.free[i] = ta
            io, ko, fo = ro.take()
            tev = []
            for m in range(2):
                for hc in range(2):
                    for half in range(2):
                        im, ps, fm = ro_ps.take()
                        tm = T.op(lambda e, m=m, hc=hc, half=half, ps=ps, kt=kt: e.matmul(
                            ps[0:P, :], kt[:, 2 * m + hc, :], RA[m][:, hc, 512 * half:512 * half + 512], start=True,
                            stop=True), ta, fm, tra)
                        eng = A if (m * 4 + hc * 2 + half) % 8 not in (1, 4, 6) else V
                        dst_ = ko[:, 4 * half:4 * half + 4, 256 * m + 128 * hc:256 * m + 128 * hc + 128]
                        src_ = ps[0:P, :].rearrange("p (r d) -> p r d", r=4)
                        if eng is A:
                            te = A.op(lambda e, dst_=dst_, src_=src_: e.activation(dst_, src_, ACT.Copy), tm, fo)
                        else:
                            te = V.op(lambda e, dst_=dst_, src_=src_: e.tensor_copy(dst_, src_), tm, fo)
                        ro_ps.free[im] = te
                        tev.append(te)
            rk.free[ik] = tm
            ro.free[io] = c_kv[io].dma125(S, kv_v[P * t:P * t + P], ko, tev)
        barrier()

        s6 = Arena(g1_own)
        kvb = [s6.get(4, 512) for _ in range(3)]
        qb = [s6.get(4, D) for _ in range(3)]
        prod = [s6.get(1024) for _ in range(2)]

        def pass2():
            rk, rp = Ring(kvb), Ring(prod)
            cg = [chan() for _ in kvb]
            cs = [chan() for _ in kvb]
            vs_v = vs_d.rearrange("(p c) d -> p c d", p=128)
            for k in range(QC):
                i, kv, fk = rk.take()
                q = qb[i]
                G.wait(fk)
                for c in range(4):
                    col = 4 * k + c
                    cg[i].n += 32
                    G.do(lambda e, kv=kv, c=c, col=col, s=cg[i].sem: e.indirect_dma_start(
                        out=kv[:, c, :], out_offset=None, in_=kv_d,
                        in_offset=bass.IndirectOffsetOnAxis(ap=kvI[:, col:col + 1], axis=0)).then_inc(s, 16))
                    G.do(lambda e, q=q, c=c, col=col, s=cg[i].sem: e.indirect_dma_start(
                        out=q[:, c, :], out_offset=None, in_=q_d,
                        in_offset=bass.IndirectOffsetOnAxis(ap=qI[:, col:col + 1], axis=0)).then_inc(s, 16))
                ts = cs[i].dma(S, vs_v[:, 4 * k:4 * k + 4, :], kv[:, :, D:2 * D], cg[i].now)
                ip, pr, fp = rp.take()
                t1 = V.op(lambda e, pr=pr, kv=kv, q=q: e.tensor_tensor(pr.rearrange("p (c d) -> p c d", c=4), kv[:, :, 0:D],
                                                                       q, ALU.mult), cg[i].now, fp)
                t2 = V.op(lambda e, pr=pr, k=k: e.tensor_reduce(
                    SC[:, 4 * k:4 * k + 4, :], pr.rearrange("p (c h d) -> p c h d", c=4, h=4), X_AX, ALU.add), t1)
                rp.free[ip] = t2
                rk.free[i] = [ts, t1]
                yield

        def mixer1():
            wq = s6.get(2, 768)
            wo = s6.get(2, D)
            boB = s6.get(D)
            wn1 = s6.get(2)
            wn2 = s6.get(D)
            QP = s6.get(2, N)
            HM = s6.get(NT, D, parts=P)
            x1 = [s6.get(D, parts=P) for _ in range(2)]
            x1T = [s6.get(2, P) for _ in range(2)]
            kph = [s6.get(D, parts=P) for _ in range(2)]
            vv = [s6.get(D + 1, parts=P) for _ in range(2)]
            em = [s6.get(D) for _ in range(2)]
            em2 = [s6.get(D) for _ in range(2)]
            KVm = s6.get(2, 132)
            sso = s6.get(NT, parts=P)
            r1 = s6.get(NT, parts=P)
            zt = [s6.get(2, 4, parts=P) for _ in range(2)]
            oo = [s6.get(D, parts=P) for _ in range(2)]
            oT = [s6.get(2, P) for _ in range(2)]
            jk = s6.get(D, parts=P)
            c_7 = chan()
            c_7.dma(A, wq, I["m1_wqkv"].rearrange("(k p) n -> p k n", p=128))
            c_7.dma(A, wo, I["m1_wout"].rearrange("(k p) n -> p k n", p=128))
            c_7.dma(A, boB, rowb(I["m1_bout"], 0, D))
            c_7.dma(A, wn1, I["m1_wn1"])
            c_7.dma(A, wn2, rowb(I["m1_wn2"], 0, D))

            def rms(src, tok):
                for t in range(NT):
                    a = A.op(lambda e, t=t: e.activation(jk, src[:, t, :], ACT.Square, accum_out=sso[:, t:t + 1]), tok, A.now)
                t_ = V.op(lambda e: e.tensor_scalar(r1, sso, 1.0 / D, 1e-6, ALU.mult, ALU.add), a)
                a = A.op(lambda e: e.activation(r1, r1, ACT.Sqrt), t_)
                return V.op(lambda e: e.reciprocal(r1, r1), a)

            tr = rms(XN, None)
            yield
            tv1 = [V.op(lambda e, b=b: e.memset(b[:, D:D + 1], 1.0)) for b in vv][-1]
            rx, rxt, rkp, rv, re, re2 = Ring(x1), Ring(x1T), Ring(kph), Ring(vv), Ring(em), Ring(em2)
            rb = Ring(bank[0:2])
            fkv = fq = None
            tqp = None
            for t in range(NT):
                ix, x_, fx = rx.take()
                t1 = V.op(lambda e, t=t, x_=x_: e.tensor_scalar(x_, XN[:, t, :], r1[:, t:t + 1], None, ALU.mult), tr, fx)
                ib, b, fb = rb.take()
                for k in range(2):
                    tp = T.op(lambda e, k=k, b=b, x_=x_: e.transpose(b[:, k * P:(k + 1) * P], x_[:, 128 * k:128 * k + 128],
                                                                    ident[0:P, 0:P]), t1, fb)
                rx.free[ix] = tp
                it, xt, ft = rxt.take()
                for k in range(2):
                    ta = A.op(lambda e, k=k, b=b, xt=xt: e.activation(xt[:, k, :], b[:, k * P:(k + 1) * P], ACT.Identity,
                                                                     scale=wn1[:, k:k + 1]), tp, ft, c_7.now)
                rb.free[ib] = ta
                for k in range(2):
                    tm = T.op(lambda e, k=k, xt=xt: e.matmul(bank[2][0:P, :], xt[:, k, :], wq[:, k, 256:768],
                                                             start=k == 0, stop=k == 1), ta, fkv, c_7.now)
                for c in range(2):
                    for k in range(2):
                        tm2 = T.op(lambda e, k=k, c=c, xt=xt: e.matmul(
                            bank[3][:, c * P:(c + 1) * P], wq[:, k, 128 * c:128 * c + 128], xt[:, k, :], start=k == 0,
                            stop=k == 1), fq)
                rxt.free[it] = tm2
                ie, e1, fe = re.take()
                ta = V.op(lambda e, e1=e1: e.tensor_scalar(e1[0:P, :], bank[2][0:P, 0:D], 0.0, None, ALU.min), tm, fe)
                ta = A.op(lambda e, e1=e1: e.activation(e1[0:P, :], e1[0:P, :], ACT.Exp), ta)
                ik, kp, fk = rkp.take()
                tk_ = V.op(lambda e, e1=e1, kp=kp: e.scalar_tensor_tensor(kp, bank[2][0:P, 0:D], 0.0, e1[0:P, :], ALU.max,
                                                                         ALU.add), ta, fk)
                re.free[ie] = tk_
                iv, v_, fv = rv.take()
                tvv = A.op(lambda e, v_=v_: e.activation(v_[:, 0:D], bank[2][0:P, D:2 * D], ACT.Copy), tm, tk_, fv, tv1)
                fkv = [tk_, tvv]
                ie, e2, fe = re2.take()
                ta = V.op(lambda e, e2=e2: e.tensor_scalar(e2[:, 0:2 * P], bank[3][:, 0:2 * P], 0.0, None, ALU.min), tm2, fe)
                ta = A.op(lambda e, e2=e2: e.activation(e2[:, 0:2 * P], e2[:, 0:2 * P], ACT.Exp), ta)
                fq = V.op(lambda e, e2=e2, t=t: e.scalar_tensor_tensor(
                    QP[:, :, P * t:P * t + P], bank[3][:, 0:2 * P].rearrange("p (c n) -> p c n", c=2), 0.0,
                    e2[:, 0:2 * P].rearrange("p (c n) -> p c n", c=2), ALU.max, ALU.add), ta)
                re2.free[ie] = fq
                for c in range(2):
                    tkv = T.op(lambda e, c=c, kp=kp, v_=v_, t=t: e.matmul(
                        bank[4 + c][:, 0:D + 1], kp[:, 128 * c:128 * c + 128], v_, start=t == 0, stop=t == NT - 1), fkv)
                rkp.free[ik] = tkv
                rv.free[iv] = tkv
                yield
            for c in range(2):
                V.op(lambda e, c=c: e.tensor_tensor(KVm[:, c, 0:128], bank[4 + c][:, 128 * c:128 * c + 128], blk, ALU.mult),
                     tkv)
                tm_ = V.op(lambda e, c=c: e.tensor_scalar(KVm[:, c, 128:132], hm4, bank[4 + c][:, D:D + 1], None, ALU.mult))
            ro, rot, rz = Ring(oo), Ring(oT), Ring(zt)
            fo = fo2 = None
            for t in range(NT):
                for c in range(2):
                    tm = T.op(lambda e, c=c, t=t: e.matmul(bank[2][0:P, 132 * c:132 * c + 132], QP[:, c, P * t:P * t + P],
                                                           KVm[:, c, :], start=True, stop=True), fq, tm_, fo, fkv)
                pv = bank[2][0:P, 0:264].rearrange("p (c w) -> p c w", c=2)
                iz, z, fz = rz.take()
                io_, o, fo_ = ro.take()
                t1 = V.op(lambda e, z=z, pv=pv: e.tensor_scalar(z, pv[:, :, 128:132], 1e-6, None, ALU.add), tm, fz)
                t1 = V.op(lambda e, z=z: e.reciprocal(z, z), t1)
                fo = V.op(lambda e, z=z, o=o, pv=pv: e.tensor_tensor(
                    o.rearrange("p (c h d) -> p c h d", c=2, h=4), pv[:, :, 0:128].rearrange("p c (h d) -> p c h d", h=4),
                    bc(z, 3, 32), ALU.mult), t1, fo_)
                rz.free[iz] = fo
                ib, b, fb = rb.take()
                for k in range(2):
                    tp = T.op(lambda e, k=k, b=b, o=o: e.transpose(b[:, k * P:(k + 1) * P], o[:, 128 * k:128 * k + 128],
                                                                  ident[0:P, 0:P]), fo, fb)
                ro.free[io_] = tp
                it, ot, ft = rot.take()
                ta = A.op(lambda e, b=b, ot=ot: e.activation(ot, b[:, 0:2 * P].rearrange("p (k n) -> p k n", k=2), ACT.Copy),
                          tp, ft)
                rb.free[ib] = ta
                for k in range(2):
                    tm = T.op(lambda e, k=k, ot=ot: e.matmul(bank[3][0:P, 0:D], ot[:, k, :], wo[:, k, :], start=k == 0,
                                                             stop=k == 1), ta, fo2, fq)
                rot.free[it] = tm
                fo2 = V.op(lambda e, t=t: e.tensor_tensor(HM[:, t, :], bank[3][0:P, 0:D], boB[0:P, :], ALU.add), tm)
                th = V.op(lambda e, t=t: e.tensor_tensor(HM[:, t, :], HM[:, t, :], XN[:, t, :], ALU.add), fo2)
                yield
            tr = rms(HM, th)
            for t in range(NT):
                V.op(lambda e, t=t: e.tensor_tensor(X[:, t, :], X[:, t, :], HM[:, t, :], ALU.add), th)
                t1 = V.op(lambda e, t=t: e.scalar_tensor_tensor(HM[:, t, :], HM[:, t, :], r1[:, t:t + 1], wn2[0:P, :],
                                                                ALU.mult, ALU.mult), tr, V.now)
                V.op(lambda e, t=t: e.tensor_tensor(X[:, t, :], X[:, t, :], HM[:, t, :], ALU.add), t1)
            yield

        run((pass2(), 196), (mixer1(), 52))
        barrier()

        s7 = Arena(g1_own)
        rec1 = s7.get(C, 5)
        tc = V.op(lambda e: e.tensor_copy(rec1[:, :, 0], dstF))
        tx = softmax(lambda h: SC[:, :, h], lambda h: rec1[:, :, 1 + h], dstF, s7, 4, tc)
        trec = c_r.dma(S, rec1_d.rearrange("(p c) f -> p c f", p=128), rec1, tx, tc)
        barrier()
        s7 = Arena(g1_own)
        acc1 = s7.get(NT, RW, parts=P)
        tz = V.op(lambda e: e.memset(acc1, 0.0))
        vw = [s7.get(4, RW) for _ in range(3)]
        rvw = Ring(vw)

        def make1(M, dd, rb_, qb_, td, tin):
            i, w, f = rvw.take()
            t1 = V.op(lambda e: e.tensor_tensor(M, bc(iota[:, 0:P], 1, 4), bc(dd, 2, P), ALU.is_equal), td)
            t2 = A.op(lambda e: e.activation(w[:, :, D:RW], qb_[:, :, 1:5], ACT.Copy), tin, f)
            tv = G.op(lambda e: e.tensor_tensor(w[:, :, 0:D].rearrange("p i (h d) -> p i h d", h=4),
                                                rb_.rearrange("p i (h d) -> p i h d", h=4),
                                                bc(qb_[:, :, 1:5], 3, 64), ALU.mult), tin, f)
            rvw.free[i] = (T.sem, T.n + 4)
            return M, (lambda k: w[:, k, :]), [t1, t2, tv]

        last = steps(acc1, vs_d, rec1_d, D, 5, make1, s7, tz)
        den = s7.get(NT, 4, parts=P)
        AL = s7.get(2, 1024)
        skB = s7.get(4)
        ag = [s7.get(D, parts=P) for _ in range(2)]
        agT = [s7.get(2, P) for _ in range(2)]
        c_a = chan()
        for kc in range(2):
            c_a.dma(A, AL[:, kc, :].rearrange("p (t n) -> p t n", t=4),
                    I["a_lin"][:, 128 * kc:128 * kc + 128, :].rearrange("t p n -> p t n"))
        c_a.dma(A, skB, rowb(I["skip"], 0, 4))
        ts = A.op(lambda e: e.activation(skB, skB, ACT.Sigmoid), c_a.now)
        for a in range(4):
            tsk = V.op(lambda e, a=a: e.tensor_scalar(mk[:, a, :], mk[:, a, :], skB[0:P, a:a + 1], None, ALU.mult), ts)
        t = V.chain([
            lambda e: e.tensor_scalar(den, acc1[:, :, D:RW], 1e-30, None, ALU.max),
            lambda e: e.reciprocal(den, den),
        ], last)
        rg, rt = Ring(ag), Ring(agT)
        rb = Ring(bank[4:6])
        rm = Ring(bank[0:4])
        T.wait(last)
        for m in range(NT):
            i, a_, f = rg.take()
            t1 = V.op(lambda e, m=m, a_=a_: e.tensor_tensor(
                a_.rearrange("p (h d) -> p h d", h=4), acc1[:, m, 0:D].rearrange("p (h d) -> p h d", h=4),
                bc(den[:, m, :], 2, 64), ALU.mult), t, f)
            ib, b, fb = rb.take()
            for k in range(2):
                tp = T.op(lambda e, k=k, b=b, a_=a_: e.transpose(b[:, k * P:(k + 1) * P], a_[:, 128 * k:128 * k + 128],
                                                                ident[0:P, 0:P]), t1, fb)
            rg.free[i] = tp
            it, at, ft = rt.take()
            ta = A.op(lambda e, b=b, at=at: e.activation(at, b[:, 0:2 * P].rearrange("p (k n) -> p k n", k=2), ACT.Copy),
                      tp, ft)
            rb.free[ib] = ta
            tv = None
            for half in range(2):
                im, ps, fm = rm.take()
                for k in range(2):
                    tm = T.op(lambda e, k=k, half=half, ps=ps, at=at: e.matmul(
                        ps[0:P, :], at[:, k, :], AL[:, k, 512 * half:512 * half + 512], start=k == 0, stop=k == 1),
                        ta, fm, c_a.now)
                for a in range(2):
                    tv = V.op(lambda e, m=m, ps=ps, a=a, half=half: e.scalar_tensor_tensor(
                        X[:, m, :], ps[0:P, D * a:D * a + D], mk[:, 2 * half + a, m:m + 1], X[:, m, :], ALU.mult, ALU.add),
                        tm, tsk, tv)
                rm.free[im] = tv
            rt.free[it] = tm
        barrier()

        f1 = Arena(BASE)
        Y = f1.get(NT, D, parts=P)
        ty = ln_apply(Y, X, ln_stats(X, 1e-5))
        T.wait(ty)
        moe, tmoe = experts(f1, 8, Y, I["f1_w"], I["f1_b2"], I["f1_gw"], I["f1_gb"],
                            ACT.Gelu, False)
        t = V.op(lambda e: e.tensor_tensor(X, X, moe, ALU.add), tmoe)
        c_o = chan()
        S.wait(c_o.dma125(S, out.rearrange("(t p) d -> p t d", p=P), X, t))
        barrier()


def kernel(**a):
    import concourse.bacc as bacc
    from concourse.bass_utils import run_bass_kernel_spmd

    def arr(v):
        return np.ascontiguousarray(np.asarray(v))

    a = {k: np.asarray(v) for k, v in a.items()}

    def edges(v, fill):
        w = np.full(EP, fill, v.dtype)
        w[:E] = v
        return w.reshape(128, C)

    def experts(w1, b1, w2):
        n = len(w1)
        return np.concatenate([w1.reshape(n, 2, 128, 512).transpose(0, 2, 1, 3).reshape(n, 128, 1024),
                               w2.reshape(n, 4, 128, D).transpose(0, 2, 1, 3).reshape(n, 128, 1024),
                               b1.reshape(n, 4, 128).transpose(0, 2, 1)], 2)

    perm = np.array([96 * (b % 8) + 32 * (b // 8) + i for b in range(24) for i in range(32)])
    p = np.arange(128)
    feeds = {
        "x": a["x"], "src": edges(a["src"], 0), "dst": edges(a["dst"], PADN), "etype": edges(a["edge_type_8"], 0),
        "edge_attr": a["edge_attr_128"], "ntype": a["node_type_4"].reshape(NT, P).T,
        "c_ident": np.eye(128, dtype=np.float32),
        "c_tri": (p[:, None] < p[None, :]).astype(np.float32),
        "c_iota": np.tile(np.arange(128, dtype=np.float32), (128, 1)),
        "c_blk": (p[:, None] // 32 == p[None, :] // 32).astype(np.float32),
        "c_hm4": (p[:, None] // 32 == np.arange(4)[None, :]).astype(np.float32),
        "c_steps": np.tile(np.arange(NS, dtype=np.float32), (128, 1)),
        "WnT": a["L0_gnn_Wn"].T, "bn": a["L0_gnn_bn"],
        "WeB": np.concatenate([a["L0_gnn_We"], a["L0_gnn_be"][:, None]], 1),
        "attn": a["L0_gnn_attn"].reshape(D), "attnC": a["L0_gnn_attn"].reshape(2, 128).T,
        "w_qkv": a["L0_mix_w_qkv"][perm][:, :, 2].T,
        "bn_gamma": a["L0_mix_bn_gamma"][perm].reshape(6, 128).T, "bn_beta": a["L0_mix_bn_beta"][perm].reshape(6, 128).T,
        "w_dw": a["L0_mix_w_dw"][perm][:, 0, 2].reshape(6, 128).T,
        "w_pw": a["L0_mix_w_pw"][perm].reshape(6, 4, 32, 32).transpose(1, 3, 0, 2),
        "w_res": a["L0_mix_w_res"][:, :, 0].T, "b_res": a["L0_mix_b_res"],
        "f0_gw": a["L0_ffn_gate_w"], "f0_gb": a["L0_ffn_gate_b"], "f0_w": experts(a["L0_ffn_w1"], a["L0_ffn_b1"], a["L0_ffn_w2"]),
        "f0_b2": a["L0_ffn_b2"],
        "f0_gamma": a["L0_ffn_gamma"], "f0_beta": a["L0_ffn_beta"],
        "k_lin": a["L1_gnn_k_linears"], "q_lin": a["L1_gnn_q_linears"], "v_lin": a["L1_gnn_v_linears"],
        "a_lin": a["L1_gnn_a_linears"], "pri": a["L1_gnn_relation_pri"].reshape(32), "skip": a["L1_gnn_skip"],
        "att": a["L1_gnn_relation_att"].transpose(1, 3, 0, 2), "msg": a["L1_gnn_relation_msg"].transpose(1, 2, 0, 3),
        "m1_wqkv": a["L1_mix_w_qkv"], "m1_wout": a["L1_mix_w_out"], "m1_bout": a["L1_mix_b_out"],
        "m1_wn1": a["L1_mix_w_norm1"].reshape(2, 128).T, "m1_wn2": a["L1_mix_w_norm2"],
        "f1_gw": a["L1_ffn_Wg"], "f1_gb": a["L1_ffn_bg"], "f1_w": experts(a["L1_ffn_W1"], a["L1_ffn_b1"], a["L1_ffn_W2"]),
        "f1_b2": a["L1_ffn_b2"],
    }
    nc = bacc.Bacc("TRN2", target_bir_lowering=False, num_devices=1)
    arrays, ins = {}, {}
    for name, v in feeds.items():
        v = arr(v)
        arrays["in_" + name] = v
        ins[name] = nc.dram_tensor("in_" + name, v.shape, mybir.dt.from_np(v.dtype), kind="ExternalInput").ap()
    out = nc.dram_tensor("out_0", (N, D), F32, kind="ExternalOutput").ap()
    build(nc, ins, out)
    r = run_bass_kernel_spmd(nc, [arrays], core_ids=[0])
    return r.results[0]["out_0"]
```

```python
from contextlib import ExitStack
import math

import numpy as np
import concourse.bass as bass
from concourse import mybir

F32 = mybir.dt.float32
I32 = mybir.dt.int32
U32 = mybir.dt.uint32
BF16 = mybir.dt.bfloat16
ALU = mybir.AluOpType
ACT = mybir.ActivationFunctionType
X_AX = mybir.AxisListType.X

N = 3125
P = 125
NT = 25
D = 256
E = 100000
C = 784
EP = 128 * C
QC = C // 4
NTI = EP // 512
NS = NTI + NT - 1
WROW = 2052
MS = (2 * N + 16 * 127) // 128 * 128
NTS = (N + 4 * 127) // 128
RW = 260
BIG = 1.0e30
PADN = 4000
MX = float(np.float32(0.99999))
T0 = float(0.5 * math.log((1.0 + MX) / (1.0 - MX)))
BLK = [(500 * b, min(500, N - 500 * b)) for b in range(7)]


class Eng:

    def __init__(self, engine, sem):
        self.engine, self.sem, self.n, self.seen = engine, sem, 0, {}

    def wait(self, *tokens):
        for t in tokens:
            if t is None:
                continue
            if isinstance(t, list):
                self.wait(*t)
                continue
            s, v = t
            if self.seen.get(id(s), 0) < v:
                self.seen[id(s)] = v
                self.engine.wait_ge(s, v)

    def op(self, fn, *tokens):
        self.wait(*tokens)
        self.n += 1
        fn(self.engine).then_inc(self.sem, 1)
        return (self.sem, self.n)

    def chain(self, fns, *tokens):
        t = None
        for k, fn in enumerate(fns):
            t = self.op(fn, t) if k else self.op(fn, *tokens)
        return t

    def do(self, fn, *tokens):
        self.wait(*tokens)
        fn(self.engine)

    @property
    def now(self):
        return (self.sem, self.n)


class Chan:

    def __init__(self, sem):
        self.sem, self.n = sem, 0

    def dma(self, eng, out, in_, *tokens):
        eng.wait(*tokens)
        self.n += 16
        eng.engine.dma_start(out, in_).then_inc(self.sem, 16)
        return (self.sem, self.n)

    def dma125(self, eng, out, in_, *tokens):
        self.dma(eng, out[0:112], in_[0:112], *tokens)
        return self.dma(eng, out[112:P], in_[112:P])

    @property
    def now(self):
        return (self.sem, self.n)


class Ring:

    def __init__(self, bufs):
        self.bufs, self.free, self.k = bufs, [None] * len(bufs), 0

    def take(self):
        i = self.k % len(self.bufs)
        self.k += 1
        return i, self.bufs[i], self.free[i]


def build(nc, I, out):
    ctx = ExitStack()
    with ctx:
        nsem = [0]

        def sem():
            nsem[0] += 1
            return ctx.enter_context(nc.semaphore(f"s{nsem[0]}"))

        V, A, T, G, S = (Eng(e, sem()) for e in (nc.vector, nc.scalar, nc.tensor, nc.gpsimd, nc.sync))
        ENG = [V, A, T, G, S]
        chans = []

        def chan():
            chans.append(Chan(sem()))
            return chans[-1]

        def barrier():
            every = [e.now for e in ENG if e.n] + [c.now for c in chans if c.n]
            for e in ENG:
                e.wait(every)

        WIDE = 52800
        mem = ctx.enter_context(nc.sbuf_tensor("mem", [128, WIDE], F32))
        bank = [ctx.enter_context(nc.psum_tensor(f"bank{i}", [128, 512], F32)) for i in range(8)]

        class Arena:
            def __init__(self, at):
                self.at = at

            def get(self, *dims, parts=128, dt=None):
                n = int(np.prod(dims))
                v = mem[0:parts, self.at:self.at + n]
                self.at += n
                assert self.at <= WIDE, self.at
                if dt is not None:
                    v = v.bitcast(dt)
                if len(dims) == 2:
                    v = v.rearrange("p (a b) -> p a b", b=dims[1])
                if len(dims) == 3:
                    v = v.rearrange("p (a b c) -> p a b c", b=dims[1], c=dims[2])
                return v

        def dram(name, shape, dt=F32):
            return nc.dram_tensor(name, shape, dt).ap()

        hp_d = dram("hp_d", [N, RW])
        hs_d = dram("hs_d", [EP, RW])
        rec0_d = dram("rec0_d", [EP, 2])
        rec1_d = dram("rec1_d", [EP, 5])
        kvi_d = dram("kvi_d", [EP, 1], I32)
        dst_d = dram("dst_d", [2, EP], BF16)
        sc_d = dram("sc_d", [EP + 512 * NT, 4])
        kv_d = dram("kv_d", [8 * (N + 128 * NTS), 2 * D])
        q3_d = dram("q3_d", [N + 128 * NTS, 3 * D], BF16)
        rid_d = dram("rid_d", [128 * NTS, 1], I32)
        vs_d = dram("vs_d", [512 * NS, D])
        xs_d = dram("xs_d", [MS, D])
        ys_d = dram("ys_d", [MS, D])

        def bc(ap, axis, n):
            v = ap.unsqueeze(axis)
            shape = list(v.shape)
            shape[axis] = n
            return v.to_broadcast(shape)

        def rowb(ap, off, n, parts=128):
            return bass.AP(ap.tensor, off, [[0, parts], [1, n]])

        top = Arena(0)
        ident = top.get(128)
        iota = top.get(128)
        blk = top.get(128)
        tri = top.get(128)
        hm4 = top.get(4)
        ones = top.get(128)
        JV = top.get(NS)
        REG = top.get(3, NS, dt=I32)
        SAME = top.get(NS)
        pid = top.get(1)
        mk = top.get(4, NT, parts=P)
        nid = top.get(NT, parts=P, dt=I32)
        tslI = top.get(NT, parts=P, dt=I32)
        tsrI = top.get(NT, parts=P, dt=I32)
        rid = top.get(NTS, dt=I32)
        tauI = top.get(NTS, parts=P, dt=I32)
        XAT = top.at
        X = top.get(NT, D, parts=P)
        mv = top.get(NT, 2, parts=P)
        st = top.get(NT, 6, parts=P)
        rstd = top.get(NT, parts=P)
        BASE = top.at

        c_in = chan()
        c_x = chan()
        c_x.dma125(S, X, I["x"].rearrange("(t p) d -> p t d", p=P))
        for ap, name in ((ident, "c_ident"), (iota, "c_iota"), (blk, "c_blk"), (tri, "c_tri"), (pid, "c_pid"), (nid, "c_nid"), (hm4, "c_hm4")):
            c_in.dma(S, ap, I[name])
        t_ones = V.op(lambda e: e.memset(ones, 1.0))

        def ln_stats(src, eps, *tokens):
            ts = [V.op(lambda e, t=t: e.bn_stats(st[:, t, :], src[:, t, :]), *tokens) for t in range(NT)]
            for t in range(NT):
                tk = V.op(lambda e, t=t: e.bn_aggr(mv[:, t, :], st[:, t, :]), ts[t])
            tk = V.op(lambda e: e.tensor_scalar(rstd, mv[:, :, 1], eps, None, ALU.add), tk)
            tk = A.op(lambda e: e.activation(rstd, rstd, ACT.Sqrt), tk)
            return V.op(lambda e: e.reciprocal(rstd, rstd), tk)

        def ln_apply(dst, src, tok, *tokens):
            return [V.op(lambda e, t=t: e.tensor_scalar(dst[:, t, :], src[:, t, :], mv[:, t, 0:1], rstd[:, t:t + 1],
                                                        ALU.subtract, ALU.mult), tok, *tokens) for t in range(NT)]

        s2 = Arena(BASE)
        TT = s2.get(6, N)
        HQAT = s2.at
        HQ = s2.get(2, N)
        Wc = s2.get(2, 768)
        srcI = s2.get(C, dt=I32)
        dstF = s2.get(C)
        Pt = s2.get(C)
        tt = s2.get(C)
        wB = s2.get(129)
        bng = s2.get(6)
        bnb = s2.get(6)
        ss = s2.get(NT, parts=P)
        fac = s2.get(NT, parts=P)
        sm = [s2.get(NT, parts=P) for _ in range(5)]
        s2_own = Arena(s2.at)
        dstI = Pt.bitcast(I32)

        c_w = chan()
        c_w.dma(A, Wc, I["w_qkv"].rearrange("(k p) o -> p k o", p=128))
        c_e = chan()
        c_e.dma(S, srcI, I["src"])
        c_e.dma(S, dstI, I["dst"])
        c_w.dma(A, bng, I["bn_gamma"])
        c_w.dma(A, bnb, I["bn_beta"])

        s1 = Arena(s2.at)
        WnT = s1.get(2, D)
        WeB = s1.get(2, 129)
        attnC = s1.get(2)
        attnCB = s1.get(2, 128)
        attnB = s1.get(D)
        bnB = s1.get(D)
        XNb = [s1.get(D, parts=P) for _ in range(3)]
        XTb = [s1.get(2, P) for _ in range(3)]
        HPb = [s1.get(RW, parts=P) for _ in range(4)]
        junk2 = s1.get(D, parts=P)
        c_1 = chan()
        c_1.dma(A, WnT, I["WnT"].rearrange("(k p) n -> p k n", p=128))
        c_1.dma(A, WeB, I["WeB"].rearrange("(k p) n -> p k n", p=128))
        c_1.dma(A, attnC, I["attnC"])
        c_1.dma(A, attnB, rowb(I["attn"], 0, D))
        c_1.dma(A, bnB, rowb(I["bn"], 0, D))

        tk = V.op(lambda e: e.tensor_copy(attnCB, bc(attnC, 2, 128)), c_1.now)
        for kc in range(2):
            tw = T.op(lambda e, kc=kc: e.matmul(bank[7][:, 0:129], attnCB[:, kc, :], WeB[:, kc, :],
                                                start=kc == 0, stop=kc == 1), tk, c_1.now)
        t_wB = V.op(lambda e: e.tensor_copy(wB, bank[7][:, 0:129]), tw)
        t_dst = V.op(lambda e: e.tensor_copy(dstF, dstI), c_e.now)

        trs = ln_stats(X, 1e-5, c_x.now)
        rx, rt, rp = Ring(XNb), Ring(XTb), Ring(HPb)
        tone = [V.op(lambda e, b=b: e.memset(b, 1.0)) for b in HPb][-1]
        rb = Ring(bank[0:3])
        rm = Ring(bank[3:6])
        c_hp = [chan() for _ in HPb]
        xns, xts = {}, {}

        def norm(t):
            ix, xn, fx = rx.take()
            xns[t] = (ix, xn, V.op(lambda e: e.tensor_scalar(xn, X[:, t, :], mv[:, t, 0:1], rstd[:, t:t + 1],
                                                             ALU.subtract, ALU.mult), trs, fx))

        def turn(t):
            ix, xn, t1 = xns.pop(t)
            ib, b, fb = rb.take()
            T.wait(c_in.now, fb, t1)
            for k in range(2):
                tp = T.op(lambda e: e.transpose(b[:, k * P:(k + 1) * P], xn[:, 128 * k:128 * k + 128], ident[0:P, 0:P]))
            rx.free[ix] = tp
            it, xt, ft = rt.take()
            rb.free[ib] = t3 = A.op(lambda e: e.activation(xt, b[:, 0:2 * P].rearrange("p (k n) -> p k n", k=2), ACT.Copy),
                                    tp, ft)
            xts[t] = (it, xt, t3)

        def table(t):
            it, xt, t3 = xts.pop(t)
            im, m, fm = rm.take()
            for k in range(2):
                tm = T.op(lambda e: e.matmul(m[0:P, 0:D], xt[:, k, :], WnT[:, k, :], start=k == 0, stop=k == 1),
                          t3, fm, c_1.now)
            rt.free[it] = tm
            ip, hp, fp = rp.take()
            t5 = V.op(lambda e: e.tensor_tensor(hp[:, 0:D], m[0:P, 0:D], bnB[0:P, :], ALU.add), tm, fp, tone)
            rm.free[im] = t5
            t6 = V.op(lambda e: e.tensor_tensor_reduce(junk2, hp[:, 0:D], attnB[0:P, :], 1.0, 0.0, ALU.mult,
                                                       ALU.add, hp[:, D + 1:D + 2]), t5, V.now)
            rp.free[ip] = c_hp[ip].dma125(S, hp_d[P * t:P * t + P, :], hp, t6)

        norm(0)
        norm(1)
        turn(0)
        for t in range(NT):
            if t + 2 < NT:
                norm(t + 2)
            if t + 1 < NT:
                turn(t + 1)
            table(t)
        barrier()

        own = Arena(s2_own.at)
        gbuf = [own.get(4, RW) for _ in range(5)]
        EAb = [own.get(8, 128) for _ in range(2)]

        def pass1():
            rg = Ring(gbuf)
            cg = [chan() for _ in gbuf]
            cs = [chan() for _ in gbuf]
            hs_v = hs_d.rearrange("(p c) d -> p c d", p=128)
            late = []

            def scores(k, i, g, tg):
                rg.free[i] = [rg.free[i], G.op(lambda e: e.tensor_copy(Pt[:, 4 * k:4 * k + 4], g[:, :, D + 1]), tg)]

            for k in range(QC):
                i, g, fg = rg.take()
                G.wait(fg)
                for c in range(4):
                    cg[i].n += 16
                    G.do(lambda e, g=g, c=c, k=k, s=cg[i].sem: e.indirect_dma_start(
                        out=g[:, c, :], out_offset=None, in_=hp_d,
                        in_offset=bass.IndirectOffsetOnAxis(ap=srcI[:, 4 * k + c:4 * k + c + 1], axis=0)).then_inc(s, 16))
                rg.free[i] = cs[i].dma(S, hs_v[:, 4 * k:4 * k + 4, :], g, cg[i].now)
                late.append((k, i, g, cg[i].now))
                if len(late) > 2:
                    scores(*late.pop(0))
                yield
            for x_ in late:
                scores(*x_)

        def edge_logits():
            ce = [chan() for _ in EAb]
            re = Ring(EAb)
            tz = [V.op(lambda e, b=b: e.memset(b, 0.0)) for b in EAb][-1]
            ea = I["edge_attr"]
            full = (E - 127 * C) // 8
            got = {}

            def load(k):
                i, b, fb = re.take()
                bf = b.rearrange("p a f -> p (a f)")

                def src(p0, n):
                    return bass.AP(ea.tensor, (C * p0 + 8 * k) * 128, [[C * 128, n], [1, 1024]])
                if k < full:
                    ce[i].dma(A, bf, src(0, 128), fb, tz)
                else:
                    ce[i].dma(A, bf[0:112], src(0, 112), fb, tz)
                    ce[i].dma(A, bf[112:127], src(112, 15))
                got[k] = (i, b, ce[i].now)

            load(0)
            for k in range(C // 8):
                if k + 1 < C // 8:
                    load(k + 1)
                i, b, tin = got.pop(k)
                t1 = V.op(lambda e: e.tensor_tensor(b, b, bc(wB[:, 0:128], 1, 8), ALU.mult), tin)
                re.free[i] = V.op(lambda e: e.tensor_reduce(tt[:, 8 * k:8 * k + 8], b, X_AX, ALU.add), t1)
                yield

        mown = Arena(own.at)

        def mixer0():
            SB = mem[:, HQAT:HQAT + 3000].rearrange("p (c n) -> p c n", c=6)
            VF = mown.get(4, 500)
            RD = mown.get(4, 500)
            sqb = [mown.get(500) for _ in range(2)]
            nb = [mown.get(500) for _ in range(2)]
            Wd = mown.get(6, 128)
            bst = mown.get(7, 6)
            bmv = mown.get(6, 2)
            bsc = mown.get(6)
            bbi = mown.get(6)
            wcf = Wc.rearrange("p k o -> p (k o)")
            wres = wcf[:, 0:4 * D].rearrange("p (k n) -> p k n", k=4)
            brB = wcf[:, 4 * D:5 * D]
            wdwC = mown.get(6)
            ss3, ss4, f3, f4, n4 = sm
            FX = X
            c_m = chan()
            c_m.dma(A, wdwC, I["w_dw"])
            junk = VF[0:P, 0, 0:D]
            H0b = [VF[0:P, q, 0:D] for q in range(1, 4)]
            nmr = sm[4]
            tn = V.op(lambda e: e.scalar_tensor_tensor(nmr, mv[:, :, 0], -1.0, rstd, ALU.mult, ALU.mult))
            for t in range(NT):
                tq = A.op(lambda e, t=t: e.activation(junk, X[:, t, :], ACT.Square, bias=nmr[:, t:t + 1],
                                                      scale=rstd[:, t:t + 1], accum_out=ss[:, t:t + 1]), tn, A.now)
            tq = A.op(lambda e: e.activation(ss, ss, ACT.Sqrt), tq)
            y, y2, r, u = sm[0:4]
            tk = V.chain([
                lambda e: e.tensor_scalar(ss, ss, 1e-15, None, ALU.max),
                lambda e: e.tensor_scalar(y, ss, MX, None, ALU.min),
                lambda e: e.tensor_scalar(r, y, -1.0, 1.0, ALU.mult, ALU.add),
                lambda e: e.reciprocal(r, r),
                lambda e: e.scalar_tensor_tensor(r, y, 1.0, r, ALU.add, ALU.mult),
            ], tq)
            tk = A.op(lambda e: e.activation(r, r, ACT.Ln), tk)
            tk = V.chain([
                lambda e: e.tensor_tensor(y2, y, y, ALU.mult),
                lambda e: e.tensor_scalar(u, y2, 1.0 / 7.0, 0.2, ALU.mult, ALU.add),
                lambda e: e.tensor_tensor(u, u, y2, ALU.mult),
                lambda e: e.tensor_scalar(u, u, 1.0 / 3.0, None, ALU.add),
                lambda e: e.tensor_tensor(u, u, y2, ALU.mult),
                lambda e: e.scalar_tensor_tensor(u, u, 1.0, y, ALU.add, ALU.mult),
                lambda e: e.tensor_scalar(r, r, 0.5, None, ALU.mult),
                lambda e: e.tensor_tensor(u, u, r, ALU.subtract),
                lambda e: e.tensor_scalar(y2, y, 0.05, None, ALU.is_lt),
                lambda e: e.tensor_tensor(u, u, y2, ALU.mult),
                lambda e: e.tensor_tensor(u, u, r, ALU.add),
                lambda e: e.reciprocal(fac, ss),
                lambda e: e.tensor_tensor(fac, fac, u, ALU.mult),
            ], tk)
            tfac = tk
            tk = V.chain([
                lambda e: e.tensor_tensor(nmr, nmr, fac, ALU.mult),
                lambda e: e.tensor_tensor(fac, fac, rstd, ALU.mult),
            ], tfac)
            yield
            rh = Ring(H0b)
            rb = Ring(bank[0:3])
            hs = {}

            def ball(t):
                ih, h0, fh = rh.take()
                hs[t] = (ih, h0, A.op(lambda e: e.activation(h0, X[:, t, :], ACT.Identity, bias=nmr[:, t:t + 1],
                                                             scale=fac[:, t:t + 1]), tk, fh))
            ball(0)
            for t in range(NT):
                if t + 1 < NT:
                    ball(t + 1)
                ih, h0, th = hs.pop(t)
                ib, b, fb = rb.take()
                for k in range(2):
                    tp = T.op(lambda e: e.transpose(b[:, k * P:(k + 1) * P], h0[:, 128 * k:128 * k + 128], ident[0:P, 0:P]),
                              th, fb)
                rh.free[ih] = tp
                rb.free[ib] = tHQ = V.op(lambda e: e.tensor_copy(HQ[:, :, P * t:P * t + P],
                                                                 b[:, 0:2 * P].rearrange("p (k n) -> p k n", k=2)), tp)
                yield
            T.wait(tHQ)
            tn = [None] * 6
            for oc in range(6):
                tst = []
                for b, (l0, n) in enumerate(BLK):
                    i, ps, f = rb.take()
                    for q in range(2):
                        tm = T.op(lambda e: e.matmul(ps[:, 0:n], Wc[:, q, 128 * oc:128 * oc + 128],
                                                     HQ[:, q, l0:l0 + n], start=q == 0, stop=q == 1), f, c_w.now)
                    ta = A.op(lambda e: e.activation(TT[:, oc, l0:l0 + n], ps[:, 0:n], ACT.Copy), tm)
                    rb.free[i] = ta
                    tst.append(V.op(lambda e: e.bn_stats(bst[:, b, :], TT[:, oc, l0:l0 + n]), ta,
                                    tn[oc - 1] if oc else None))
                    yield
                tk = V.op(lambda e: e.bn_aggr(bmv[:, oc, :], bst), *tst)
                tn[oc] = tk
                c1, c2 = bsc[:, oc:oc + 1], bbi[:, oc:oc + 1]
                tk = V.op(lambda e: e.tensor_scalar(c1, bmv[:, oc, 1:2], 1e-5, None, ALU.add), tk)
                tk = A.op(lambda e: e.activation(c1, c1, ACT.Sqrt), tk)
                tbn = V.chain([
                    lambda e: e.reciprocal(c1, c1),
                    lambda e: e.tensor_tensor(c1, c1, bng[:, oc:oc + 1], ALU.mult),
                    lambda e: e.tensor_tensor(c2, c1, bmv[:, oc, 0:1], ALU.mult),
                    lambda e: e.tensor_tensor(c2, bnb[:, oc:oc + 1], c2, ALU.subtract),
                ], tk, c_w.now)
            tconv = T.now
            c_m.dma(A, wres, I["w_res"].rearrange("(k p) n -> p k n", p=128), tconv)
            c_m.dma(A, brB, rowb(I["b_res"], 0, D))
            tz = V.op(lambda e: e.memset(Wd, 0.0))
            for g in range(4):
                c_m.dma(A, Wd[32 * g:32 * g + 32, :, 32 * g:32 * g + 32], I["w_pw"][g], tz)
            for oc in range(6):
                twd = V.op(lambda e: e.tensor_scalar(Wd[:, oc, :], Wd[:, oc, :], wdwC[:, oc:oc + 1], None, ALU.mult),
                           c_m.now)
            yield
            rsq = Ring(sqb)
            rf = Ring([bank[4], bank[5]])

            def squares(src, k, last, tok):
                i, sq, f = rsq.take()
                n = src.shape[-1]
                ta = A.op(lambda e: e.activation(sq[:, 0:n], src, ACT.Square), f, tok)
                rsq.free[i] = T.op(lambda e: e.matmul(bank[3][:, 0:n], ones, sq[:, 0:n], start=k == 0, stop=k == last), ta)
                return ta

            def factor(n, free):
                a = A.op(lambda e: e.activation(nb[0][:, 0:n], bank[3][:, 0:n], ACT.Sqrt), T.now, free)
                t = V.chain([
                    lambda e: e.tensor_scalar(nb[0][:, 0:n], nb[0][:, 0:n], 1e-15, None, ALU.max),
                    lambda e: e.reciprocal(nb[1][:, 0:n], nb[0][:, 0:n]),
                    lambda e: e.scalar_tensor_tensor(nb[1][:, 0:n], nb[0][:, 0:n], T0, nb[1][:, 0:n], ALU.min, ALU.mult),
                ], a)
                return a, t

            fnorm = fnb = fO = None
            for b, (l0, n) in enumerate(BLK):
                tb = TT[:, :, l0:l0 + n]
                T.wait(fnorm)
                for oc in range(6):
                    ta = A.op(lambda e: e.activation(tb[:, oc, :], tb[:, oc, :], ACT.Relu, bias=bbi[:, oc:oc + 1],
                                                     scale=bsc[:, oc:oc + 1]), tbn)
                    squares(tb[:, oc, :], oc, 5, ta)
                fnorm, t = factor(n, fnb)
                tT = fnb = V.op(lambda e: e.tensor_tensor(tb, tb, bc(nb[1][:, 0:n], 1, 6), ALU.mult), t)
                T.wait(fnorm)
                yield
                for oc in range(6):
                    i, ps, f = rb.take()
                    tm = T.op(lambda e: e.matmul(ps[:, 0:n], Wd[:, oc, :], tb[:, oc, :], start=True, stop=True), f, tT, twd)
                    if oc < 4:
                        tv = V.op(lambda e: e.tensor_scalar(SB[:, oc, 0:n], ps[:, 0:n], 0.0, None, ALU.max), tm, tconv, fO)
                    else:
                        tv = V.op(lambda e: e.tensor_copy(SB[:, oc, 0:n], ps[:, 0:n]), tm, tconv, fO)
                    squares(tb[:, oc, :], 2 * oc, 11, tT)
                    rb.free[i] = squares(ps[:, 0:n], 2 * oc + 1, 11, tv)
                fnorm, t = factor(n, fnb)
                f2, g2 = nb[1][:, 0:n], nb[0][:, 0:n]
                V.op(lambda e: e.tensor_tensor(VF[:, 0:2, 0:n], tb[:, 4:6, :], bc(f2, 1, 2), ALU.mult), t, fO)
                V.op(lambda e: e.tensor_tensor(VF[:, 2:4, 0:n], SB[:, 4:6, 0:n], bc(f2, 1, 2), ALU.mult))
                V.op(lambda e: e.tensor_tensor(g2, f2, f2, ALU.mult))
                t = V.chain([
                    lambda e: e.tensor_scalar(RD[:, :, 0:n], VF[:, :, 0:n], 1e-15, None, ALU.add),
                    lambda e: e.reciprocal(RD[:, :, 0:n], RD[:, :, 0:n]),
                    lambda e: e.tensor_tensor(VF[:, :, 0:n], VF[:, :, 0:n], RD[:, :, 0:n], ALU.mult),
                    lambda e: e.tensor_tensor(VF[:, :, 0:n], VF[:, :, 0:n], bc(g2, 1, 4), ALU.mult),
                    lambda e: e.tensor_tensor(VF[:, 0:2, 0:n], VF[:, 0:2, 0:n], tb[:, 0:2, :], ALU.mult),
                    lambda e: e.tensor_tensor(VF[:, 2:4, 0:n], VF[:, 2:4, 0:n], SB[:, 0:2, 0:n], ALU.mult),
                ], V.now)
                fnb = V.now
                yield
                tv = V.now
                for q in range(4):
                    i, ps, f = rb.take()
                    kk = tb[:, 2 + q, :] if q < 2 else SB[:, q, 0:n]
                    tm = T.op(lambda e: e.matmul(ps[:, 0:n], blk, kk, start=True, stop=True), f, tv, c_in.now)
                    tv = rb.free[i] = V.op(lambda e: e.tensor_tensor(VF[:, q, 0:n], VF[:, q, 0:n], ps[:, 0:n], ALU.mult),
                                           tm, t)
                    ta = A.op(lambda e: e.activation(RD[:, q, 0:n], VF[:, q, 0:n], ACT.Square), tv)
                for m0 in range(0, n, P):
                    tile = (l0 + m0) // P
                    i, ps, f = rf.take()
                    T.wait(f, ta, tv, c_m.now)
                    for q in range(4):
                        T.op(lambda e: e.matmul(ps[0:P, 0:D], VF[:, q, m0:m0 + P], wres[:, q, :], start=q == 0, stop=q == 3))
                    for q in range(4):
                        tm = T.op(lambda e: e.matmul(ps[0:P, D:D + 1], RD[:, q, m0:m0 + P], ones[:, 0:1], start=q == 0,
                                                     stop=q == 3))
                    V.op(lambda e: e.tensor_copy(FX[:, tile, :], ps[0:P, 0:D]), tm)
                    tv2 = rf.free[i] = V.op(lambda e: e.tensor_copy(ss3[:, tile:tile + 1], ps[0:P, D:D + 1]))
                fO = tm
                yield
            XL = mem[0:P, BASE:BASE + NT * D].rearrange("p (t d) -> p t d", d=D)
            tx = c_x.dma125(A, XL, I["x"].rearrange("(t p) d -> p t d", p=P), A.now, V.now, T.now)
            a = A.op(lambda e: e.activation(ss3, ss3, ACT.Sqrt), tv2)
            t = V.chain([
                lambda e: e.tensor_scalar(ss3, ss3, 1e-15, None, ALU.max),
                lambda e: e.reciprocal(f3, ss3),
                lambda e: e.scalar_tensor_tensor(f3, ss3, T0, f3, ALU.min, ALU.mult),
            ], a)
            for m in range(NT):
                t1 = V.op(lambda e: e.scalar_tensor_tensor(FX[:, m, :], FX[:, m, :], f3[:, m:m + 1], brB[0:P, :],
                                                           ALU.mult, ALU.add), t, c_m.now)
                a = A.op(lambda e: e.activation(sqb[0][0:P, 0:D], FX[:, m, :], ACT.Square, accum_out=ss4[:, m:m + 1]),
                         t1, rsq.free, A.now)
            yield
            a = A.op(lambda e: e.activation(ss4, ss4, ACT.Sqrt), a)
            t = V.op(lambda e: e.tensor_scalar(n4, ss4, 1e-15, None, ALU.max), a)
            a = A.op(lambda e: e.activation(f4, n4, ACT.Tanh), t)
            t = V.chain([
                lambda e: e.reciprocal(n4, n4),
                lambda e: e.scalar_tensor_tensor(f4, f4, MX, n4, ALU.min, ALU.mult),
            ], a)
            for m in range(NT):
                V.op(lambda e: e.scalar_tensor_tensor(X[:, m, :], FX[:, m, :], f4[:, m:m + 1], XL[:, m, :],
                                                      ALU.mult, ALU.add), t, tx)
            yield

        def run(*gens):
            parts = [[g, n, 0] for g, n in gens]
            while parts:
                p = min(parts, key=lambda p: p[2] / p[1])
                p[2] += 1
                if next(p[0], p) is p:
                    parts.remove(p)

        zero = own.get(D)
        tz = V.op(lambda e: e.memset(zero, 0.0))
        chan().dma(A, xs_d.rearrange("(s p) d -> p s d", p=128), bc(zero, 1, MS // 128), tz)
        run((pass1(), 196), (edge_logits(), 98), (mixer0(), 92))
        barrier()

        def softmax(z, ex, dst, ar, heads, tok):
            same = ar.get(C)
            pf = ar.get(C)
            pb = ar.get(C)
            fw = ar.get(C)
            bw = ar.get(C)
            uu = ar.get(C)
            row = ar.get(8, 128)
            col = ar.get(8)
            cols = ar.get(2)
            tk = V.op(lambda e: e.tensor_tensor(same[:, 1:C], dst[:, 1:C], dst[:, 0:C - 1], ALU.not_equal), tok)
            V.op(lambda e: e.memset(pf[:, 0:1], -BIG))
            V.op(lambda e: e.memset(pb[:, C - 1:C], -BIG))
            V.op(lambda e: e.tensor_scalar(pf[:, 1:C], same[:, 1:C], -BIG, None, ALU.mult), tk)
            tpb = V.op(lambda e: e.tensor_scalar(pb[:, 0:C - 1], same[:, 1:C], -BIG, None, ALU.mult))
            cat = bank[0]
            T.op(lambda e: e.transpose(cat[0:1, 0:128], dst[:, 0:1], ident), tok)
            tt1 = T.op(lambda e: e.transpose(cat[0:1, 128:256], dst[:, C - 1:C], ident))
            fd, ld, df, db, ca, cb, wk = (row[0:1, i, :] for i in range(7))
            wide = lambda i: row[0:1, i, :]
            t = V.chain([
                lambda e: e.tensor_copy(fd, cat[0:1, 0:128]),
                lambda e: e.tensor_copy(ld, cat[0:1, 128:256]),
                lambda e: e.tensor_tensor(wk, fd, ld, ALU.not_equal),
                lambda e: e.tensor_tensor(ca[:, 1:128], fd[:, 1:128], ld[:, 0:127], ALU.not_equal),
                lambda e: e.memset(ca[:, 0:1], 1.0),
                lambda e: e.tensor_copy(cb[:, 0:127], ca[:, 1:128]),
                lambda e: e.memset(cb[:, 127:128], 1.0),
                lambda e: e.tensor_tensor(df, wk, ca, ALU.add),
                lambda e: e.tensor_tensor(db, wk, cb, ALU.add),
                lambda e: e.tensor_scalar(df, df, -BIG, None, ALU.mult),
                lambda e: e.tensor_scalar(db, db, -BIG, None, ALU.mult),
                lambda e: e.tensor_scalar(ca, ca, -BIG, None, ALU.mult),
                lambda e: e.tensor_scalar(cb, cb, -BIG, None, ALU.mult),
            ], tt1)
            tlast = None
            for h in range(heads):
                zh, eh = z(h), ex(h)
                t1 = V.op(lambda e, zh=zh: e.tensor_tensor_scan(fw, pf, zh, 0.0, ALU.add, ALU.max), t, tpb, tlast)
                t2 = V.op(lambda e, zh=zh: e.tensor_tensor_scan(bw[:, ::-1], pb[:, ::-1], zh[:, ::-1], 0.0, ALU.add,
                                                                ALU.max))
                T.op(lambda e: e.transpose(cat[0:1, 0:128], fw[:, C - 1:C], ident), t1, t)
                tp = T.op(lambda e: e.transpose(cat[0:1, 128:256], bw[:, 0:1], ident), t2)
                sf, sb_ = wide(6), wide(7)
                tv = V.chain([
                    lambda e: e.tensor_tensor_scan(sf, df, cat[0:1, 0:128], 0.0, ALU.add, ALU.max),
                    lambda e: e.tensor_tensor_scan(sb_[:, ::-1], db[:, ::-1], cat[0:1, 128:256][:, ::-1], 0.0, ALU.add,
                                                   ALU.max),
                    lambda e: e.tensor_tensor(fd[:, 1:128], sf[:, 0:127], ca[:, 1:128], ALU.add),
                    lambda e: e.memset(fd[:, 0:1], -BIG),
                    lambda e: e.tensor_tensor(ld[:, 0:127], sb_[:, 1:128], cb[:, 0:127], ALU.add),
                    lambda e: e.memset(ld[:, 127:128], -BIG),
                ], tp)
                T.op(lambda e: e.matmul(bank[1][:, 0:1], fd, ones[0:1, 0:1], start=True, stop=True), tv)
                tm = T.op(lambda e: e.matmul(bank[1][:, 1:2], ld, ones[0:1, 0:1], start=True, stop=True))
                tv = V.chain([
                    lambda e: e.tensor_copy(cols, bank[1][:, 0:2]),
                    lambda e: e.tensor_tensor(fw, fw, bw, ALU.max),
                    lambda e: e.tensor_scalar(uu, dst, dst[:, 0:1], -BIG, ALU.not_equal, ALU.mult),
                    lambda e: e.scalar_tensor_tensor(fw, uu, cols[:, 0:1], fw, ALU.add, ALU.max),
                    lambda e: e.tensor_scalar(uu, dst, dst[:, C - 1:C], -BIG, ALU.not_equal, ALU.mult),
                    lambda e: e.scalar_tensor_tensor(fw, uu, cols[:, 1:2], fw, ALU.add, ALU.max),
                    lambda e, zh=zh: e.tensor_tensor(fw, zh, fw, ALU.subtract),
                ], tm)
                tlast = A.op(lambda e, eh=eh: e.activation(eh, fw, ACT.Exp), tv)
            return tlast

        def slots(ar, hot, NE, nsl, groupI, tok):
            keep = ar.get(NE, NT, parts=P)
            cum = ar.get(NE, NT, parts=P)
            slot = ar.get(NE, NT, parts=P)
            cnt = ar.get(NE, parts=P)
            cntI = ar.get(NE, parts=P, dt=I32)
            t0 = ar.get(NE, parts=P)
            cmp = ar.get(nsl, NE - 1, parts=P)
            es = ar.get(nsl, parts=P)
            T.op(lambda e: e.matmul(bank[3][0:P, 0:NT * NE], tri[0:P, 0:P], hot, start=True, stop=True), tok)
            tm = T.op(lambda e: e.matmul(bank[4][0:P, 0:NT * NE], ones[0:P, 0:P], hot, start=True, stop=True))
            pre = bank[3][0:P, 0:NT * NE].rearrange("p (e t) -> p e t", t=NT)
            tot = bank[4][0:P, 0:NT * NE].rearrange("p (e t) -> p e t", t=NT)
            flat = lambda v: v.rearrange("p e t -> p (e t)")
            return slot, V.chain([
                lambda e: e.memset(keep, 1.0),
                lambda e: e.memset(keep[:, :, 0:1], 0.0),
                lambda e: e.tensor_tensor_scan(flat(cum), flat(keep), bank[4][0:P, 0:NT * NE], 0.0, ALU.mult, ALU.add),
                lambda e: e.tensor_scalar(cntI, cum[:, :, NT - 1], 127.0, None, ALU.add),
                lambda e: e.tensor_scalar(cntI, cntI, 7, None, ALU.arith_shift_right),
                lambda e: e.tensor_copy(cnt, cntI),
                lambda e: e.tensor_tensor_scan(t0, ones[0:P, 0:NE], cnt, 0.0, ALU.mult, ALU.add),
                lambda e: e.tensor_tensor(t0, t0, cnt, ALU.subtract),
                lambda e: e.tensor_tensor(cmp, bc(t0[:, 1:NE], 1, nsl), bc(iota[0:P, 0:nsl], 2, NE - 1), ALU.is_le),
                lambda e: e.tensor_reduce(es, cmp, X_AX, ALU.add),
                lambda e: e.tensor_copy(groupI, es),
                lambda e: e.tensor_tensor(slot, cum, tot, ALU.subtract),
                lambda e: e.tensor_tensor(slot, slot, pre, ALU.add),
                lambda e: e.scalar_tensor_tensor(slot, bc(t0, 2, NT), 128.0, slot, ALU.mult, ALU.add),
            ], tm)

        s3 = Arena(BASE)
        rec0 = s3.get(C, 2)
        aa = s3.get(C)
        zz = s3.get(C)
        t = V.chain([
            lambda e: e.tensor_tensor(zz, Pt, tt, ALU.add),
            lambda e: e.tensor_scalar(zz, zz, wB[:, 128:129], None, ALU.add),
            lambda e: e.tensor_scalar(aa, zz, 0.01, None, ALU.mult),
            lambda e: e.tensor_tensor(aa, aa, zz, ALU.max),
            lambda e: e.tensor_copy(rec0[:, :, 0], dstF),
        ])
        tx = softmax(lambda h: aa, lambda h: rec0[:, :, 1], dstF, s3, 1, t)
        c_r = chan()
        trec = c_r.dma(S, rec0_d.rearrange("(p c) f -> p c f", p=128), rec0, tx, t)
        cnt = s3.get(NT - 1)
        GJ = s3.get(NT - 1)
        GI = s3.get(NT - 1, dt=I32)
        jn = s3.get(NT - 1)
        gs = s3.get(NS)
        cmp = s3.get(NS, NT - 1)
        TJ = s3.get(NS)
        ntI = s3.get(NT, parts=P, dt=I32)
        ntF = s3.get(NT, parts=P)
        c_g = chan()
        c_g.dma(S, gs, I["c_steps"])
        c_g.dma(S, ntI, I["ntype"])
        for j in range(1, NT):
            tk = V.op(lambda e, j=j: e.tensor_scalar(aa, dstF, float(P * j), None, ALU.is_lt, ALU.add,
                                                     accum_out=cnt[:, j - 1:j]), tx, V.now)
        tm = T.op(lambda e: e.matmul(bank[2][:, 0:NT - 1], ones, cnt, start=True, stop=True), tk)
        tk = V.chain([
            lambda e: e.tensor_copy(GI, bank[2][:, 0:NT - 1]),
            lambda e: e.tensor_scalar(GI, GI, 9, None, ALU.arith_shift_right),
            lambda e: e.tensor_copy(GJ, GI),
            lambda e: e.tensor_tensor(GJ, GJ, iota[:, 1:NT], ALU.add),
            lambda e: e.tensor_tensor(cmp, bc(GJ, 1, NS), bc(gs, 2, NT - 1), ALU.is_le),
            lambda e: e.tensor_reduce(TJ, cmp, X_AX, ALU.add),
            lambda e: e.tensor_scalar(JV, TJ, float(P), None, ALU.mult),
            lambda e: e.tensor_copy(REG[:, 0, :], TJ),
            lambda e: e.tensor_tensor(TJ, gs, TJ, ALU.subtract),
            lambda e: e.tensor_copy(REG[:, 1, :], TJ),
            lambda e: e.memset(SAME[:, 0:1], 0.0),
            lambda e: e.tensor_tensor(SAME[:, 1:NS], TJ[:, 1:NS], TJ[:, 0:NS - 1], ALU.is_equal),
            lambda e: e.tensor_tensor(gs, gs, TJ, ALU.subtract),
            lambda e: e.tensor_tensor(gs, gs, TJ, ALU.subtract),
            lambda e: e.tensor_scalar(gs, gs, float(NTI), None, ALU.add),
            lambda e: e.tensor_tensor(gs[:, 0:NS - 1], gs[:, 0:NS - 1], SAME[:, 1:NS], ALU.mult),
            lambda e: e.memset(gs[:, NS - 1:NS], 0.0),
            lambda e: e.tensor_tensor(gs, gs, TJ, ALU.add),
            lambda e: e.tensor_copy(REG[:, 2, :], gs),
        ], tm, c_g.now)
        tstep = tk
        sm_ = s3.get(4, NT, parts=P)
        slF = s3.get(NT, parts=P)
        spare = s3.get(NTS)
        tk = V.op(lambda e: e.tensor_copy(ntF, ntI), c_g.now)
        for a in range(4):
            tk = V.op(lambda e: e.tensor_scalar(mk[:, a, :], ntF, float(a), None, ALU.is_equal), V.now)
        slot, tk = slots(s3, mk, 4, NTS, tauI, tk)
        V.chain([
            lambda e: e.tensor_tensor(sm_, slot, mk, ALU.mult),
            lambda e: e.tensor_reduce(slF, sm_.rearrange("p e t -> p t e"), X_AX, ALU.add),
            lambda e: e.tensor_copy(tslI, slF),
            lambda e: e.tensor_scalar(tsrI, tslI, 7, None, ALU.arith_shift_right),
            lambda e: e.tensor_copy(ntF, tsrI),
            lambda e: e.scalar_tensor_tensor(slF, ntF, -128.0, slF, ALU.mult, ALU.add),
            lambda e: e.scalar_tensor_tensor(slF, slF, float(NTS), ntF, ALU.mult, ALU.add),
            lambda e: e.tensor_copy(tsrI, slF),
            lambda e: e.tensor_scalar(spare, ones[:, 0:NTS], pid, float(NTS), ALU.mult, ALU.mult),
            lambda e: e.tensor_tensor(spare, spare, iota[:, 0:NTS], ALU.add),
            lambda e: e.tensor_scalar(rid, spare, float(N), None, ALU.add),
        ], tk)
        barrier()
        c_rid, c_rids = chan(), chan()
        rid_v = rid_d.rearrange("(p s) a -> p (s a)", p=128)
        G.wait(c_rid.dma(A, rid_v, rid))
        for t in range(NT):
            c_rids.n += 16
            G.do(lambda e: e.indirect_dma_start(
                out=rid_d, out_offset=bass.IndirectOffsetOnAxis(ap=tsrI[:, t:t + 1], axis=0),
                in_=nid[:, t:t + 1], in_offset=None).then_inc(c_rids.sem, 16))
        c_rid.dma(A, rid, rid_v, c_rids.now)

        def steps(acc, rows, rec, width, nrec, make, ar, tz, by_step):
            nb = 4
            rbuf = [ar.get(4, width) for _ in range(nb)]
            qbuf = [ar.get(4, nrec) for _ in range(nb)]
            mbuf = [ar.get(4, P) for _ in range(3)]
            dl = [ar.get(4) for _ in range(3)]
            rr, rq, rm, rdl = Ring(rbuf), Ring(qbuf), Ring(mbuf), Ring(dl)
            rp = Ring(bank[0:4])
            cr = [chan() for _ in range(nb)]
            r_v = rows.rearrange("(t p i) d -> t p (i d)", p=128, i=4)
            q_v = rec.rearrange("(t p i) f -> t p (i f)", p=128, i=4)
            last = tz
            LAG = 2
            pend = {}

            def add(g):
                ps, w, tm, ip = pend.pop(g)
                reg = V.engine.value_load(REG[0:1, 0, g:g + 1], min_val=0, max_val=NT - 1)
                a = acc[:, bass.ds(reg, 1), 0:w].rearrange("p a c -> p (a c)")
                rp.free[ip] = V.op(lambda e: e.tensor_tensor(a, a, ps[0:P, 0:w], ALU.add), tm, last)
                return rp.free[ip]

            for g in range(NS):
                i, rb_, fr = rr.take()
                _, qb_, _ = rq.take()
                S.wait(fr)
                cr[i].n += 32

                def load(e, g=g, rb_=rb_, qb_=qb_, s=cr[i].sem):
                    t = e.value_load(REG[0:1, 1, g:g + 1], min_val=0, max_val=NTI - 1)
                    src = r_v[g] if by_step else r_v[bass.ds(t, 1), :, :].rearrange("a p c -> (a p) c")
                    e.dma_start(rb_.rearrange("p i d -> p (i d)"), src).then_inc(s, 16)
                    e.dma_start(qb_.rearrange("p i f -> p (i f)"),
                                q_v[bass.ds(t, 1), :, :].rearrange("a p c -> (a p) c")).then_inc(s, 16)
                S.do(load)
                tin = cr[i].now
                im, M, fm = rm.take()
                _, dd, _ = rdl.take()
                td = V.op(lambda e, g=g, dd=dd, qb_=qb_: e.tensor_scalar(dd, qb_[:, :, 0], JV[:, g:g + 1], None,
                                                                            ALU.subtract), tin, fm)
                lhs, rhs, tv = make(M, dd, rb_, qb_, td, tin)
                ip, ps, fp = rp.take()
                T.wait(tv, tin, fp)
                for k in range(4):
                    tm = T.op(lambda e, k=k, ps=ps, lhs=lhs, rhs=rhs: e.matmul(ps[0:P, 0:rhs(k).shape[-1]], lhs[:, k, :],
                                                                               rhs(k), start=k == 0, stop=k == 3))
                rm.free[im] = tm
                rr.free[i] = tm
                pend[g] = (ps, rhs(0).shape[-1], tm, ip)
                if g >= LAG:
                    last = add(g - LAG)
            for g in range(NS - LAG, NS):
                last = add(g)
            return last

        s3 = Arena(BASE)
        acc0 = s3.get(NT, RW, parts=P)
        tz = V.op(lambda e: e.memset(acc0, 0.0))

        def make0(M, dd, rb_, qb_, td, tin):
            for k in range(4):
                tv = V.op(lambda e, k=k: e.tensor_scalar(M[:, k, :], iota[:, 0:P], dd[:, k:k + 1], qb_[:, k, 1:2],
                                                         ALU.is_equal, ALU.mult), td)
            return M, (lambda k: rb_[:, k, 0:D + 1]), tv

        last = steps(acc0, hs_d, rec0_d, RW, 2, make0, s3, tz, False)
        den = s3.get(NT, parts=P)
        t = V.chain([
            lambda e: e.tensor_scalar(den, acc0[:, :, D], 1e-16, None, ALU.add),
            lambda e: e.reciprocal(den, den),
        ], last)
        for m in range(NT):
            t1 = V.op(lambda e, m=m: e.tensor_scalar(acc0[:, m, 0:D], acc0[:, m, 0:D], den[:, m:m + 1], 0.0,
                                                     ALU.mult, ALU.max), t)
        tX = V.op(lambda e: e.tensor_tensor(X, X, acc0[:, :, 0:D], ALU.add), t1)
        barrier()

        def experts(ar, NE, y, wall, b2, gw, gb, func, weighted):
            nsl = (2 * N + NE * 127) // 128
            acc = ar.get(NT, D, parts=P)
            wb_ = [ar.get(WROW) for _ in range(5)]
            xb = [ar.get(2, D) for _ in range(4)]
            xTb = [ar.get(2, 128) for _ in range(2)]
            hTb = [ar.get(4, 128) for _ in range(2)]
            yb = [ar.get(D) for _ in range(4)]
            gb_ = [ar.get(2, D, parts=P) for _ in range(4)]
            yTb = [ar.get(2, P) for _ in range(3)]
            b2r = ar.get(D)
            gwc = ar.get(2, NE)
            gbB = ar.get(NE)
            lg = ar.get(NT, NE, parts=P)
            gate = ar.get(NT, NE, parts=P)
            oh1 = ar.get(NT, NE, parts=P)
            oh2 = ar.get(NT, NE, parts=P)
            cm = ar.get(NT, NE, parts=P)
            mx = ar.get(NT, 8, parts=P)
            mi = ar.get(NT, 8, parts=P, dt=U32)
            mf = ar.get(NT, 8, parts=P)
            wa = ar.get(NT, parts=P)
            wb = ar.get(NT, parts=P)
            sl = ar.get(2, NT, parts=P)
            slI = ar.get(2, NT, parts=P, dt=I32)
            esI = ar.get(nsl, parts=P, dt=I32)
            gT = ar.get(NT, P)
            cs = chan()
            cs.dma(A, b2r[0:NE, :], b2)
            cs.dma(A, gwc, gw.rearrange("(k p) n -> p k n", p=128))
            cs.dma(A, gbB, rowb(gb, 0, NE))
            rt = Ring(bank[0:2])
            ry = Ring(yTb)
            yTs = {}

            def turn_y(t):
                i, b, f = rt.take()
                for k in range(2):
                    tp = T.op(lambda e: e.transpose(b[:, k * P:(k + 1) * P], y[:, t, 128 * k:128 * k + 128],
                                                    ident[0:P, 0:P]), f)
                iy, yT, fy = ry.take()
                rt.free[i] = ta = A.op(lambda e: e.activation(
                    yT, b[:, 0:2 * P].rearrange("p (k n) -> p k n", k=2), ACT.Copy), tp, fy)
                yTs[t] = (iy, yT, ta)

            turn_y(0)
            for t in range(NT):
                if t + 1 < NT:
                    turn_y(t + 1)
                iy, yT, ta = yTs.pop(t)
                for k in range(2):
                    tm = T.op(lambda e: e.matmul(bank[2][0:P, NE * t:NE * t + NE], yT[:, k, :], gwc[:, k, :],
                                                 start=k == 0, stop=k == 1), ta, cs.now)
                ry.free[iy] = tm
            tk = V.op(lambda e: e.tensor_tensor(lg, bank[2][0:P, 0:NT * NE].rearrange("p (t n) -> p t n", n=NE),
                                                bc(gbB[0:P, :], 1, NT), ALU.add), tm, cs.now)
            for t in range(NT):
                tk1 = V.op(lambda e, t=t: e.max(mx[:, t, :], lg[:, t, :]), tk)
            for t in range(NT):
                tk1 = V.op(lambda e, t=t: e.max_index(mi[:, t, :], mx[:, t, :], lg[:, t, :]), tk1)
            io = bc(iota[0:P, 0:NE], 1, NT)
            tc = V.chain([
                lambda e: e.tensor_copy(mf, mi),
                lambda e: e.tensor_tensor(oh1, io, bc(mf[:, :, 0], 2, NE), ALU.is_equal),
                lambda e: e.tensor_tensor(oh2, io, bc(mf[:, :, 1], 2, NE), ALU.is_equal),
                lambda e: e.tensor_tensor(cm, oh1, oh2, ALU.add),
            ], tk1)
            slot, ts = slots(ar, cm.rearrange("p t e -> p e t"), NE, nsl, esI, tc)
            tl = V.chain([
                lambda e: e.tensor_tensor(cm, slot.rearrange("p e t -> p t e"), oh1, ALU.mult),
                lambda e: e.tensor_reduce(sl[:, 0, :], cm, X_AX, ALU.add),
                lambda e: e.tensor_tensor(cm, slot.rearrange("p e t -> p t e"), oh2, ALU.mult),
                lambda e: e.tensor_reduce(sl[:, 1, :], cm, X_AX, ALU.add),
                lambda e: e.tensor_copy(slI, sl),
            ], ts)
            csc = chan()
            G.wait(tl)
            for t in range(NT):
                for k in range(2):
                    csc.n += 16
                    G.do(lambda e, t=t, k=k: e.indirect_dma_start(
                        out=xs_d, out_offset=bass.IndirectOffsetOnAxis(ap=slI[:, k, t:t + 1], axis=0),
                        in_=y[:, t, :], in_offset=None).then_inc(csc.sem, 16))
            tsc = csc.now
            tg = tl
            if weighted:
                tk = V.op(lambda e: e.tensor_tensor(wb, mx[:, :, 1], mx[:, :, 0], ALU.subtract), tl)
                tk = A.op(lambda e: e.activation(wb, wb, ACT.Exp), tk)
                tg = V.chain([
                    lambda e: e.tensor_scalar(wa, wb, 1.0, None, ALU.add),
                    lambda e: e.reciprocal(wa, wa),
                    lambda e: e.tensor_tensor(wb, wb, wa, ALU.mult),
                    lambda e: e.tensor_tensor(oh1, oh1, bc(wa, 2, NE), ALU.mult),
                    lambda e: e.tensor_tensor(oh2, oh2, bc(wb, 2, NE), ALU.mult),
                ], tk)
            tg = V.op(lambda e: e.tensor_tensor(gate, oh1, oh2, ALU.add), tg)
            rg2 = Ring(bank[5:8])
            tgT = []
            for t in range(NT):
                i, b, f = rg2.take()
                tp = T.op(lambda e, t=t, b=b: e.transpose(b[0:NE, 0:P], gate[:, t, :], ident[0:P, 0:P]), tg, f)
                rg2.free[i] = A.op(lambda e, t=t, b=b: e.activation(gT[0:NE, t, :], b[0:NE, 0:P], ACT.Copy), tp)
                tgT.append(rg2.free[i])
            for t in range(NT):
                i, b, f = rg2.take()
                tm = T.op(lambda e, t=t, b=b: e.matmul(b[0:P, 0:D], gT[0:NE, t, :], b2r[0:NE, :], start=True,
                                                       stop=True), tgT[t], f)
                rg2.free[i] = tacc = V.op(lambda e, t=t, b=b: e.tensor_copy(acc[:, t, :], b[0:P, 0:D]), tm)
            rw, rx, rxT, rh, ryb = Ring(wb_), Ring(xb), Ring(xTb), Ring(hTb), Ring(yb)
            cw = [chan() for _ in wb_]
            cx = [chan() for _ in xb]
            cy = [chan() for _ in yb]
            rbt, rb1, rb2 = Ring(bank[0:2]), Ring(bank[2:5]), Ring(bank[5:8])
            rbt.free = [T.now, T.now]
            rb1.free = [T.now, ts, tl]
            rb2.free = rg2.free
            xs_v = xs_d[0:128 * nsl, :].rearrange("(s p) d -> p s d", p=128)
            S.wait(ts)
            xt, wt, got, done = {}, {}, {}, {}

            def fetch(s):
                i, w, f = rw.take()
                S.wait(f)
                reg = S.engine.value_load(esI[0:1, s:s + 1], min_val=0, max_val=NE - 1)
                wt[s] = (i, w, cw[i].dma(S, w, wall[bass.ds(reg, 1), :, :].rearrange("a p c -> (a p) c")))

            def rows(s):
                i, x_, f = rx.take()
                n = min(2, nsl - s)
                got[s] = got[s + 1] = (i, x_, cx[i].dma(S, x_[:, 0:n, :], xs_v[:, s:s + n, :], f, tsc))

            def turn(s):
                i, x_, tin = got.pop(s)
                ib, b, f = rbt.take()
                for k in range(2):
                    tp = T.op(lambda e: e.transpose(b[:, 128 * k:128 * k + 128], x_[:, s % 2, 128 * k:128 * k + 128], ident),
                              tin, f)
                rx.free[i] = tp
                it, x_T, ft = rxT.take()
                rbt.free[ib] = tv = V.op(lambda e: e.tensor_copy(x_T, b[:, 0:256].rearrange("p (k n) -> p k n", k=2)), tp, ft)
                xt[s] = (it, x_T, tv)

            def first(s):
                it, x_T, tv = xt.pop(s)
                iw, w, tw = wt[s]
                ib, b, f = rb1.take()
                ih, h, fh = rh.take()
                for c in range(4):
                    for q in range(2):
                        tm = T.op(lambda e: e.matmul(b[:, 128 * c:128 * c + 128], w[:, 512 * q + 128 * c:512 * q + 128 * c + 128],
                                                     x_T[:, q, :], start=q == 0, stop=q == 1), tv, tw, f)
                rxT.free[it] = tm
                for c in range(4):
                    ta = A.op(lambda e: e.activation(h[:, c, :], b[:, 128 * c:128 * c + 128], func,
                                                     bias=w[:, 2048 + c:2049 + c]), tm, fh)
                rb1.free[ib] = ta
                return ih, h, ta

            def second(s, ih, h, ta):
                iw, w, tw = wt.pop(s)
                ib, b, f = rb2.take()
                for c in range(4):
                    tm = T.op(lambda e: e.matmul(b[:, 0:D], h[:, c, :], w[:, 1024 + D * c:1024 + D * c + D], start=c == 0,
                                                 stop=c == 3), ta, f)
                rh.free[ih] = rw.free[iw] = tm
                iy, o, fy = ryb.take()
                rb2.free[ib] = tv = V.op(lambda e: e.tensor_copy(o, b[:, 0:D]), tm, fy)
                done[s] = (iy, o, tv)

            def store(s):
                iy, o, tv = done.pop(s)
                ryb.free[iy] = cy[iy].dma(S, ys_d[128 * s:128 * s + 128, :], o, tv)

            for s in range(3):
                fetch(s)
            rows(0)
            rows(2)
            turn(0)
            late = None
            for s in range(nsl):
                if s >= 2:
                    store(s - 2)
                if s + 3 < nsl:
                    fetch(s + 3)
                if s % 2 == 0 and s + 4 < nsl:
                    rows(s + 4)
                if s + 1 < nsl:
                    turn(s + 1)
                now = first(s)
                if late:
                    second(s - 1, *late)
                late = now
            second(nsl - 1, *late)
            store(nsl - 2)
            store(nsl - 1)
            rg = Ring(gb_)
            cg = [chan() for _ in gb_]
            G.wait(ryb.free)
            for t in range(NT):
                i, g, f = rg.take()
                G.wait(f)
                for k in range(2):
                    cg[i].n += 16
                    G.do(lambda e: e.indirect_dma_start(
                        out=g[:, k, :], out_offset=None, in_=ys_d,
                        in_offset=bass.IndirectOffsetOnAxis(ap=slI[:, k, t:t + 1], axis=0)).then_inc(cg[i].sem, 16))
                tv = tacc
                for k, wk in ((0, wa), (1, wb)):
                    if weighted:
                        tv = V.op(lambda e: e.scalar_tensor_tensor(acc[:, t, :], g[:, k, :], wk[:, t:t + 1], acc[:, t, :],
                                                                   ALU.mult, ALU.add), cg[i].now, tv, tg)
                    else:
                        tv = V.op(lambda e: e.tensor_tensor(acc[:, t, :], acc[:, t, :], g[:, k, :], ALU.add), cg[i].now, tv)
                rg.free[i] = tv
            return acc, tv

        f0 = Arena(BASE)
        Y = f0.get(NT, D, parts=P)
        gam = f0.get(D)
        bet = f0.get(D)
        c_f = chan()
        c_f.dma(A, gam, rowb(I["f0_gamma"], 0, D))
        c_f.dma(A, bet, rowb(I["f0_beta"], 0, D))
        ty = ln_apply(Y, X, ln_stats(X, 1e-5))
        T.wait(ty)
        moe, tmoe = experts(f0, 16, Y, I["f0_w"], I["f0_b2"], I["f0_gw"], I["f0_gb"],
                            ACT.Relu, True)
        t = V.op(lambda e: e.tensor_tensor(Y, Y, moe, ALU.add), tmoe, T.now)
        tl = ln_apply(Y, Y, ln_stats(Y, 1e-5, t))
        for m in range(NT):
            t1 = V.op(lambda e, m=m: e.tensor_tensor(Y[:, m, :], Y[:, m, :], gam[0:P, :], ALU.mult), tl[m], c_f.now)
            t1 = V.op(lambda e, m=m: e.tensor_tensor(Y[:, m, :], Y[:, m, :], bet[0:P, :], ALU.add), t1)
        t1 = V.op(lambda e: e.tensor_tensor(X, X, Y, ALU.add), t1)
        barrier()

        g1 = Arena(BASE)
        XN = g1.get(NT, D, parts=P)
        dstF = g1.get(C)
        Q3 = g1.get(NT * 3 * D // 2, parts=P, dt=BF16).rearrange("p (t s d) -> p t s d", s=3, d=D)
        g1_own = g1.at
        s5 = Arena(g1.at)
        tyl = ln_apply(XN, X, ln_stats(X, 1e-5))
        etI = s5.get(C, dt=I32)
        kvI = etI
        dst2 = [s5.get(C // 2, dt=BF16) for _ in range(2)]
        rest = [s5.get(D) for _ in range(2)]
        KVo = [s5.get(8, 512) for _ in range(2)]
        early = Arena(s5.at - 4096)
        srcI = early.get(C, dt=I32)
        dstI = early.get(C, dt=I32)
        f1_, f2_ = early.get(C), early.get(C)
        c_5 = chan()
        c_5.dma(S, srcI, I["src"])
        c_5.dma(S, dstI, I["dst"])
        c_5.dma(S, etI, I["etype"])
        V.chain([
            lambda e: e.tensor_copy(dstF, dstI),
            lambda e: e.tensor_copy(f1_, srcI),
            lambda e: e.tensor_copy(f2_, etI),
            lambda e: e.scalar_tensor_tensor(f2_, f1_, 8.0, f2_, ALU.mult, ALU.add),
            lambda e: e.tensor_copy(kvI, f2_),
            lambda e: e.tensor_scalar(dstI, dstI, 5, None, ALU.arith_shift_right),
            lambda e: e.tensor_copy(f1_, dstI),
            lambda e: e.tensor_scalar(f1_, f1_, 32.0, None, ALU.mult),
            lambda e: e.tensor_copy(dst2[0], f1_),
            lambda e: e.tensor_tensor(f1_, dstF, f1_, ALU.subtract),
            lambda e: e.tensor_copy(dst2[1], f1_),
        ], c_5.now)
        tmk = V.now
        c_i = chan()
        c_i.dma(S, kvi_d.rearrange("(p c) a -> p (c a)", p=128), kvI, tmk)
        for k in range(2):
            c_i.dma(S, dst_d[k].rearrange("(p c) -> p c", p=128), dst2[k], tmk)
        LW = [s5.get(2, 1024) for _ in range(3)]
        RA = [s5.get(2, 1024) for _ in range(2)]
        priB = s5.get(32)
        c_l = chan()
        for m, name in enumerate(("k_lin", "q_lin", "v_lin")):
            for kc in range(2):
                c_l.dma(A, LW[m][:, kc, :].rearrange("p (t n) -> p t n", t=4),
                        I[name][:, 128 * kc:128 * kc + 128, :].rearrange("t p n -> p t n"))
        c_l.dma(A, priB, rowb(I["pri"], 0, 32))
        tz = [V.op(lambda e, m=m: e.memset(RA[m], 0.0)) for m in range(2)][-1]
        for m, name in enumerate(("att", "msg")):
            for h in range(4):
                hc, i = h // 2, h % 2
                c_l.dma(A, RA[m][64 * i:64 * i + 64, hc, :].rearrange("p (r o) -> p r o", r=8)[:, :, 64 * i:64 * i + 64],
                        I[name][h], tz)
        tk = V.op(lambda e: e.tensor_scalar(priB, priB, 0.125, None, ALU.mult), c_l.now)
        for hc in range(2):
            tk = V.op(lambda e, hc=hc: e.tensor_tensor(
                RA[0][:, hc, :].rearrange("p (r i d) -> p r i d", r=8, i=2),
                RA[0][:, hc, :].rearrange("p (r i d) -> p r i d", r=8, i=2),
                bc(priB.rearrange("p (r h i) -> p r h i", r=8, h=2)[:, :, hc, :], 3, 64), ALU.mult), tk)
        tra = tk
        xb = [s5.get(2, D) for _ in range(3)]
        XTb = [s5.get(2, 128) for _ in range(2)]
        kvr = [s5.get(512) for _ in range(2)]
        qo = [s5.get(3 * D // 2, dt=BF16).rearrange("p (s d) -> p s d", s=3) for _ in range(2)]
        KTb = [s5.get(4, 128) for _ in range(2)]
        csc = chan()
        G.wait(tyl)
        for t in range(NT):
            csc.n += 16
            G.do(lambda e: e.indirect_dma_start(
                out=xs_d, out_offset=bass.IndirectOffsetOnAxis(ap=tslI[:, t:t + 1], axis=0),
                in_=XN[:, t, :], in_offset=None).then_inc(csc.sem, 16))
        tsc = csc.now
        rxb, rx, rkv, rqo, rk, ro, rr = Ring(xb), Ring(XTb), Ring(kvr), Ring(qo), Ring(KTb), Ring(KVo), Ring(rest)
        ro_ps = Ring([b[:, :] for b in bank[4:8]])
        cx = [chan() for _ in xb]
        c_kv = [chan() for _ in KVo]
        c_q = [chan() for _ in qo]
        xs_v = xs_d[0:128 * NTS, :].rearrange("(s p) d -> p s d", p=128)
        kv_v = kv_d.rearrange("(n r) d -> n (r d)", r=8)
        LWv = [w.rearrange("p k (t n) -> p k t n", t=4) for w in LW]
        got, xts, kvs, kts = {}, {}, {}, {}
        ft = fkv = fq = fkt = None

        def rows(s):
            i, x_, f = rxb.take()
            n = min(2, NTS - s)
            got[s] = got[s + 1] = (i, x_, cx[i].dma(S, x_[:, 0:n, :], xs_v[:, s:s + n, :], f, tsc))

        def turn(s):
            nonlocal ft
            i, x_, tin = got.pop(s)
            for k in range(2):
                tp = T.op(lambda e: e.transpose(bank[0][:, 128 * k:128 * k + 128], x_[:, s % 2, 128 * k:128 * k + 128], ident),
                          tin, ft)
            rxb.free[i] = tp
            ix, xt, fx = rx.take()
            ft = A.op(lambda e: e.activation(xt, bank[0][:, 0:256].rearrange("p (k n) -> p k n", k=2), ACT.Copy), tp, fx)
            xts[s] = (ix, xt, ft)

        def typed(s):
            nonlocal fkv, fq
            ix, xt, ta = xts.pop(s)
            tau = T.engine.value_load(tauI[0:1, s:s + 1], min_val=0, max_val=3)
            for m, ps, f in ((0, bank[1][:, 0:D], fkv), (2, bank[1][:, D:2 * D], fkv), (1, bank[2][:, 0:D], fq)):
                for k in range(2):
                    tm = T.op(lambda e: e.matmul(ps, xt[:, k, :], LWv[m][:, k, bass.ds(tau, 1), :].rearrange("p a n -> p (a n)"),
                                                 start=k == 0, stop=k == 1), ta, f, c_l.now)
                if m == 2:
                    tkv = tm
            rx.free[ix] = tm
            ik, kv, fk = rkv.take()
            fkv = V.op(lambda e: e.tensor_copy(kv, bank[1][:, :]), tkv, fk)
            kvs[s] = (ik, kv, fkv)
            iq, o, fo = rqo.take()
            ir, r_, fr = rr.take()
            t1 = A.op(lambda e: e.activation(o[:, 0, :], bank[2][:, 0:D], ACT.Copy), tm, fo)
            fq = t1 = V.op(lambda e: e.tensor_tensor(r_, bank[2][:, 0:D], o[:, 0, :], ALU.subtract), t1, fr)
            t1 = A.op(lambda e: e.activation(o[:, 1, :], r_, ACT.Copy), t1)
            t1 = rr.free[ir] = V.op(lambda e: e.tensor_tensor(o[:, 2, :], r_, o[:, 1, :], ALU.subtract), t1)
            G.wait(t1)
            c_q[iq].n += 16
            G.do(lambda e: e.indirect_dma_start(
                out=q3_d, out_offset=bass.IndirectOffsetOnAxis(ap=rid[:, s:s + 1], axis=0),
                in_=o.rearrange("p s d -> p (s d)"), in_offset=None).then_inc(c_q[iq].sem, 16))
            rqo.free[iq] = c_q[iq].now

        def turn2(s):
            nonlocal fkt
            ik, kv, tkv = kvs.pop(s)
            for c in range(4):
                tp = T.op(lambda e: e.transpose(bank[3][:, 128 * c:128 * c + 128], kv[:, 128 * c:128 * c + 128], ident), tkv, fkt)
            rkv.free[ik] = tp
            it, kt, f = rk.take()
            fkt = A.op(lambda e: e.activation(kt, bank[3][:, :].rearrange("p (k n) -> p k n", k=4), ACT.Copy), tp, f)
            kts[s] = (it, kt, fkt)

        def relate(s):
            it, kt, ta = kts.pop(s)
            io, ko, fo = ro.take()
            tev = []
            for m in range(2):
                for hc in range(2):
                    for half in range(2):
                        im, ps, fm = ro_ps.take()
                        tm = T.op(lambda e: e.matmul(ps, kt[:, 2 * m + hc, :], RA[m][:, hc, 512 * half:512 * half + 512],
                                                     start=True, stop=True), ta, fm, tra)
                        dst_ = ko[:, 4 * half:4 * half + 4, 256 * m + 128 * hc:256 * m + 128 * hc + 128]
                        src_ = ps.rearrange("p (r d) -> p r d", r=4)
                        if half == 0:
                            te = A.op(lambda e: e.activation(dst_, src_, ACT.Copy), tm, fo)
                        else:
                            te = V.op(lambda e: e.tensor_copy(dst_, src_), tm, fo)
                        ro_ps.free[im] = te
                        tev.append(te)
            rk.free[it] = tm
            G.wait(tev)
            c_kv[io].n += 16
            G.do(lambda e: e.indirect_dma_start(
                out=kv_v, out_offset=bass.IndirectOffsetOnAxis(ap=rid[:, s:s + 1], axis=0),
                in_=ko.rearrange("p r d -> p (r d)"), in_offset=None).then_inc(c_kv[io].sem, 16))
            ro.free[io] = c_kv[io].now

        rows(0)
        rows(2)
        turn(0)
        typed(0)
        turn(1)
        turn2(0)
        for s in range(NTS):
            if s % 2 == 0 and s + 4 < NTS:
                rows(s + 4)
            if s + 1 < NTS:
                typed(s + 1)
            relate(s)
            if s + 2 < NTS:
                turn(s + 2)
            if s + 1 < NTS:
                turn2(s + 1)
        c_5.dma125(S, Q3, q3_d[0:N, :].rearrange("(t p) (s d) -> p t s d", p=P, s=3), rqo.free)
        barrier()

        s6 = Arena(g1_own)
        kvb = [s6.get(4, 512) for _ in range(4)]
        prod = [s6.get(1024)]
        red = [s6.get(16) for _ in range(2)]
        SCg = s6.get(NS, 16)
        JP = s6.get(NS)
        kib = [s6.get(4, dt=I32) for _ in range(8)]
        drb = [s6.get(256, dt=BF16) for _ in range(4)]
        one2 = s6.get(64, dt=BF16)
        MTb = [s6.get(256, dt=BF16) for _ in range(3)]

        def pass2():
            rk, rp, rr, ri, rd, rmt = Ring(kvb), Ring(prod), Ring(red), Ring(kib), Ring(drb), Ring(MTb)
            ci = [chan() for _ in kib]
            cg = [chan() for _ in kvb]
            cs = [chan() for _ in kvb]
            c_sc = chan()
            kvi_v = kvi_d.rearrange("(t p i) a -> t p (i a)", p=128, i=4)
            dst_v = dst_d.rearrange("k (t e) -> t k e", e=512)
            vs_v = vs_d.rearrange("(g p i) d -> g p i d", p=128, i=4)
            sc_v = sc_d.rearrange("(t p i) h -> t p (i h)", p=128, i=4)
            V.op(lambda e: e.memset(one2, 1.0))
            tjp = V.op(lambda e: e.tensor_scalar(JP, JV, pid, None, ALU.add))
            rbq = Ring(bank[3:7])
            tbs, exs = {}, {}
            fbc = None
            inp, kvs, mts, scs = {}, {}, {}, {}
            tsc = None

            def load(g):
                i, ki, f1 = ri.take()
                i2, dr, f2 = rd.take()
                S.wait(f1, f2)
                t = S.engine.value_load(REG[0:1, 1, g:g + 1], min_val=0, max_val=NTI - 1)
                ci[i].dma(S, ki, kvi_v[bass.ds(t, 1), :, :].rearrange("a p c -> (a p) c"))
                inp[g] = (i, ki, i2, dr, ci[i].dma(S, dr[0:2, :], dst_v[bass.ds(t, 1), :, :].rearrange("a k e -> (a k) e")))

            def spread(g):
                ii, ki, i2, dr, tin = inp[g]
                tbs[g] = rd.free[i2] = T.op(lambda e: e.matmul(bank[7][0:P, :], one2[0:2, 0:P], dr[0:2, :], start=True,
                                                               stop=True), tin, fbc, tjp)

            def expand(g):
                im, M, tM = mts.pop(g)
                j = T.engine.value_load(REG[0:1, 0, g:g + 1], min_val=0, max_val=NT - 1)
                q = [Q3[:, bass.ds(j, 1), x_, :].rearrange("p a d -> p (a d)") for x_ in range(3)]
                Mv = M.rearrange("p (e i) -> p i e", i=4)
                exs[g] = []
                for half in range(2):
                    ib, b, fb = rbq.take()
                    for k in range(2):
                        for x_ in range(3):
                            tm = T.op(lambda e: e.matmul(b[:, D * k:D * k + D], Mv[0:P, 2 * half + k, :], q[x_],
                                                         start=x_ == 0, stop=x_ == 2), tM, fb)
                    exs[g].append((ib, b, tm))
                rmt.free[im] = tm

            def score(g):
                nonlocal tsc
                i, kv, tg = kvs.pop(g)
                rk.free[i] = [cs[i].dma(S, vs_v[g], kv[:, :, D:2 * D], tg)]
                ip, pr, fp = rp.take()
                for half, (ib, b, tm) in enumerate(exs.pop(g)):
                    rbq.free[ib] = tv = V.op(lambda e: e.tensor_tensor(
                        pr[:, 512 * half:512 * half + 512].rearrange("p (c d) -> p c d", c=2), kv[:, 2 * half:2 * half + 2, 0:D],
                        b.rearrange("p (c d) -> p c d", c=2), ALU.mult), tm, tg, fp)
                rk.free[i].append(tv)
                prv = pr.rearrange("p (c d) -> p c d", c=16)
                if g == 0:
                    rp.free[ip] = tsc = V.op(lambda e: e.tensor_reduce(SCg[:, 0, :], prv, X_AX, ALU.add), V.now)
                else:
                    ir, r, fr = rr.take()
                    rp.free[ip] = t1 = V.op(lambda e: e.tensor_reduce(r, prv, X_AX, ALU.add), V.now, fr)
                    rr.free[ir] = tsc = V.op(lambda e: e.scalar_tensor_tensor(
                        SCg[:, g, :], SCg[:, g - 1, :], SAME[:, g:g + 1], r, ALU.mult, ALU.add), t1, tsc)
                scs[g] = tsc

            def store(g):
                t = S.engine.value_load(REG[0:1, 2, g:g + 1], min_val=0, max_val=NTI + NT - 1)
                c_sc.dma(S, sc_v[bass.ds(t, 1), :, :].rearrange("a p c -> (a p) c"), SCg[:, g, :], scs.pop(g))

            for g in range(3):
                load(g)
            spread(0)
            for g in range(NS):
                if g >= 1:
                    expand(g - 1)
                im, M, fm = rmt.take()
                fbc = V.op(lambda e: e.tensor_scalar(M[0:P, :], bank[7][0:P, :], JP[0:P, g:g + 1], None, ALU.is_equal),
                           tbs.pop(g), fm, tjp)
                mts[g] = (im, M, fbc)
                if g + 1 < NS:
                    spread(g + 1)
                ii, ki, i2, dr, tin = inp.pop(g)
                i, kv, f = rk.take()
                G.wait(f, tin)
                for c in range(4):
                    cg[i].n += 16
                    G.do(lambda e: e.indirect_dma_start(
                        out=kv[:, c, :], out_offset=None, in_=kv_d[0:8 * N, :],
                        in_offset=bass.IndirectOffsetOnAxis(ap=ki[:, c:c + 1], axis=0)).then_inc(cg[i].sem, 16))
                ri.free[ii] = cg[i].now
                kvs[g] = (i, kv, cg[i].now)
                if g >= 2:
                    score(g - 2)
                if g >= 4:
                    store(g - 4)
                if g + 3 < NS:
                    load(g + 3)
                yield
            expand(NS - 1)
            for g in range(NS - 2, NS):
                score(g)
            for g in range(NS - 4, NS):
                store(g)
            yield

        def mixer1():
            wq = s6.get(2, 768)
            wo = s6.get(2, D)
            boB = s6.get(D)
            wn1 = s6.get(2)
            wn2 = s6.get(D)
            qph = [s6.get(2, P) for _ in range(2)]
            HM = XN
            x1 = [s6.get(D, parts=P) for _ in range(2)]
            x1T = [s6.get(2, P) for _ in range(2)]
            kph = [s6.get(D, parts=P) for _ in range(2)]
            vv = [s6.get(2, 129, parts=P) for _ in range(2)]
            em = [s6.get(D) for _ in range(2)]
            em2 = [s6.get(D) for _ in range(2)]
            KVm = s6.get(2, 132)
            sso = s6.get(NT, parts=P)
            r1 = s6.get(NT, parts=P)
            zt = [s6.get(2, 4, parts=P) for _ in range(2)]
            oo = [s6.get(D, parts=P) for _ in range(2)]
            oT = [s6.get(2, P) for _ in range(2)]
            jk = s6.get(D, parts=P)
            c_7 = chan()
            c_7.dma(A, wq, I["m1_wqkv"].rearrange("(k p) n -> p k n", p=128))
            c_7.dma(A, wo, I["m1_wout"].rearrange("(k p) n -> p k n", p=128))
            c_7.dma(A, boB, rowb(I["m1_bout"], 0, D))
            c_7.dma(A, wn1, I["m1_wn1"])
            c_7.dma(A, wn2, rowb(I["m1_wn2"], 0, D))

            def rms(src, tok):
                for t in range(NT):
                    a = A.op(lambda e, t=t: e.activation(jk, src[:, t, :], ACT.Square, accum_out=sso[:, t:t + 1]), tok, A.now)
                t_ = V.op(lambda e: e.tensor_scalar(r1, sso, 1.0 / D, 1e-6, ALU.mult, ALU.add), a)
                a = A.op(lambda e: e.activation(r1, r1, ACT.Sqrt), t_)
                return V.op(lambda e: e.reciprocal(r1, r1), a)

            tr = rms(XN, None)
            yield
            tv1 = [V.op(lambda e, b=b: e.memset(b[:, :, 128:129], 1.0)) for b in vv][-1]
            rx, rxt, rkp, rv, re, re2 = Ring(x1), Ring(x1T), Ring(kph), Ring(vv), Ring(em), Ring(em2)
            rb = Ring(bank[0:1])
            fkv = fq = None

            def turned(t):
                ix, x_, fx = rx.take()
                t1 = V.op(lambda e: e.tensor_scalar(x_, XN[:, t, :], r1[:, t:t + 1], None, ALU.mult), tr, fx)
                ib, b, fb = rb.take()
                for k in range(2):
                    tp = T.op(lambda e: e.transpose(b[:, k * P:(k + 1) * P], x_[:, 128 * k:128 * k + 128], ident[0:P, 0:P]),
                              t1, fb)
                rx.free[ix] = tp
                yield
                it, xt, ft = rxt.take()
                for k in range(2):
                    ta = A.op(lambda e: e.activation(xt[:, k, :], b[:, k * P:(k + 1) * P], ACT.Identity,
                                                     scale=wn1[:, k:k + 1]), tp, ft, c_7.now)
                rb.free[ib] = ta
                return it, xt, ta

            for t in range(NT):
                it, xt, ta = yield from turned(t)
                for k in range(2):
                    tm = T.op(lambda e: e.matmul(bank[1][0:P, :], xt[:, k, :], wq[:, k, 256:768],
                                                 start=k == 0, stop=k == 1), ta, fkv, c_7.now)
                rxt.free[it] = tm
                yield
                ie, e1, fe = re.take()
                ta = V.op(lambda e: e.tensor_scalar(e1[0:P, :], bank[1][0:P, 0:D], 0.0, None, ALU.min), tm, fe)
                ta = A.op(lambda e: e.activation(e1[0:P, :], e1[0:P, :], ACT.Exp), ta)
                yield
                ik, kp, fk = rkp.take()
                tk_ = V.op(lambda e: e.scalar_tensor_tensor(kp, bank[1][0:P, 0:D], 0.0, e1[0:P, :], ALU.max, ALU.add), ta, fk)
                re.free[ie] = tk_
                iv, v_, fv = rv.take()
                tvv = A.op(lambda e: e.activation(v_[:, :, 0:128], bank[1][0:P, D:2 * D].rearrange("p (c d) -> p c d", c=2), ACT.Copy), tm, tk_, fv, tv1)
                fkv = [tk_, tvv]
                for c in range(2):
                    tkv = T.op(lambda e: e.matmul(bank[2][:, 129 * c:129 * c + 129], kp[:, 128 * c:128 * c + 128], v_[:, c, :],
                                                  start=t == 0 and c == 0, stop=t == NT - 1 and c == 1), fkv)
                rkp.free[ik] = tkv
                rv.free[iv] = tkv
                yield
            for c in range(2):
                V.op(lambda e: e.tensor_tensor(KVm[:, c, 0:128], bank[2][:, 129 * c:129 * c + 128], blk, ALU.mult), tkv)
                tm_ = V.op(lambda e: e.tensor_scalar(KVm[:, c, 128:132], hm4, bank[2][:, 129 * c + 128:129 * c + 129], None, ALU.mult))
            ro, rot, rz, rqp = Ring(oo), Ring(oT), Ring(zt), Ring(qph)
            fo = fo2 = None
            for t in range(NT):
                it, xt, ta = yield from turned(t)
                for c in range(2):
                    for k in range(2):
                        tm2 = T.op(lambda e: e.matmul(bank[1][:, c * P:(c + 1) * P], wq[:, k, 128 * c:128 * c + 128],
                                                      xt[:, k, :], start=k == 0, stop=k == 1), ta, fo2)
                rxt.free[it] = tm2
                yield
                ie, e2, fe = re2.take()
                ta = V.op(lambda e: e.tensor_scalar(e2[:, 0:2 * P], bank[1][:, 0:2 * P], 0.0, None, ALU.min), tm2, fe)
                ta = A.op(lambda e: e.activation(e2[:, 0:2 * P], e2[:, 0:2 * P], ACT.Exp), ta)
                yield
                iq, qp, fq_ = rqp.take()
                fq = V.op(lambda e: e.scalar_tensor_tensor(
                    qp, bank[1][:, 0:2 * P].rearrange("p (c n) -> p c n", c=2), 0.0,
                    e2[:, 0:2 * P].rearrange("p (c n) -> p c n", c=2), ALU.max, ALU.add), ta, fq_)
                re2.free[ie] = fq
                for c in range(2):
                    tm = T.op(lambda e: e.matmul(bank[2][0:P, 132 * c:132 * c + 132], qp[:, c, :], KVm[:, c, :], start=True,
                                                 stop=True), fq, tm_, fo, fkv)
                rqp.free[iq] = tm
                yield
                pv = bank[2][0:P, 0:264].rearrange("p (c w) -> p c w", c=2)
                iz, z, fz = rz.take()
                io_, o, fo_ = ro.take()
                t1 = V.op(lambda e: e.tensor_scalar(z, pv[:, :, 128:132], 1e-6, None, ALU.add), tm, fz)
                t1 = V.op(lambda e: e.reciprocal(z, z), t1)
                fo = V.op(lambda e: e.tensor_tensor(
                    o.rearrange("p (c h d) -> p c h d", c=2, h=4), pv[:, :, 0:128].rearrange("p c (h d) -> p c h d", h=4),
                    bc(z, 3, 32), ALU.mult), t1, fo_)
                rz.free[iz] = fo
                ib, b, fb = rb.take()
                for k in range(2):
                    tp = T.op(lambda e: e.transpose(b[:, k * P:(k + 1) * P], o[:, 128 * k:128 * k + 128], ident[0:P, 0:P]),
                              fo, fb)
                ro.free[io_] = tp
                yield
                it, ot, ft = rot.take()
                ta = A.op(lambda e: e.activation(ot, b[:, 0:2 * P].rearrange("p (k n) -> p k n", k=2), ACT.Copy), tp, ft)
                rb.free[ib] = ta
                for k in range(2):
                    tm = T.op(lambda e: e.matmul(bank[1][0:P, 256:256 + D], ot[:, k, :], wo[:, k, :], start=k == 0,
                                                 stop=k == 1), ta, fq)
                rot.free[it] = tm
                yield
                fo2 = V.op(lambda e: e.tensor_tensor(HM[:, t, :], HM[:, t, :], bank[1][0:P, 256:256 + D], ALU.add), tm)
                th = V.op(lambda e: e.tensor_tensor(HM[:, t, :], HM[:, t, :], boB[0:P, :], ALU.add), fo2)
                r, ssq = r1[:, t:t + 1], sso[:, t:t + 1]
                ta = A.op(lambda e: e.activation(jk, HM[:, t, :], ACT.Square, accum_out=ssq), th, A.now)
                t1 = V.op(lambda e: e.tensor_tensor(X[:, t, :], X[:, t, :], HM[:, t, :], ALU.add), th)
                yield
                t2 = V.op(lambda e: e.tensor_scalar(r, ssq, 1.0 / D, 1e-6, ALU.mult, ALU.add), ta)
                ta = A.op(lambda e: e.activation(r, r, ACT.Sqrt), t2)
                yield
                t2 = V.op(lambda e: e.reciprocal(r, r), ta)
                t2 = V.op(lambda e: e.scalar_tensor_tensor(HM[:, t, :], HM[:, t, :], r, wn2[0:P, :], ALU.mult, ALU.mult),
                          t1, t2)
                V.op(lambda e: e.tensor_tensor(X[:, t, :], X[:, t, :], HM[:, t, :], ALU.add), t2)
                yield

        run((pass2(), NS + 1), (mixer1(), 326))
        barrier()

        s7 = Arena(g1_own)
        rec1 = s7.get(C, 5)
        SC = s7.get(C, 4)
        tsc = c_r.dma(S, SC, sc_d[0:EP, :].rearrange("(p c) h -> p c h", p=128))
        tc = V.op(lambda e: e.tensor_copy(rec1[:, :, 0], dstF))
        tx = softmax(lambda h: SC[:, :, h], lambda h: rec1[:, :, 1 + h], dstF, s7, 4, [tc, tsc])
        trec = c_r.dma(S, rec1_d.rearrange("(p c) f -> p c f", p=128), rec1, tx, tc)
        barrier()
        s7 = Arena(g1_own)
        acc1 = s7.get(NT, RW, parts=P)
        tz = V.op(lambda e: e.memset(acc1, 0.0))
        vw = [s7.get(4, RW) for _ in range(3)]
        rvw = Ring(vw)

        def make1(M, dd, rb_, qb_, td, tin):
            i, w, f = rvw.take()
            t1 = V.op(lambda e: e.tensor_tensor(M, bc(iota[:, 0:P], 1, 4), bc(dd, 2, P), ALU.is_equal), td)
            t2 = A.op(lambda e: e.activation(w[:, :, D:RW], qb_[:, :, 1:5], ACT.Copy), tin, f)
            tv = G.op(lambda e: e.tensor_tensor(w[:, :, 0:D].rearrange("p i (h d) -> p i h d", h=4),
                                                rb_.rearrange("p i (h d) -> p i h d", h=4),
                                                bc(qb_[:, :, 1:5], 3, 64), ALU.mult), tin, f)
            rvw.free[i] = (T.sem, T.n + 4)
            return M, (lambda k: w[:, k, :]), [t1, t2, tv]

        last = steps(acc1, vs_d, rec1_d, D, 5, make1, s7, tz, True)
        den = s7.get(NT, 4, parts=P)
        AL = s7.get(2, 1024)
        skB = s7.get(4)
        ag = [s7.get(D, parts=P) for _ in range(2)]
        agT = [s7.get(2, P) for _ in range(2)]
        c_a = chan()
        for kc in range(2):
            c_a.dma(A, AL[:, kc, :].rearrange("p (t n) -> p t n", t=4),
                    I["a_lin"][:, 128 * kc:128 * kc + 128, :].rearrange("t p n -> p t n"))
        c_a.dma(A, skB, rowb(I["skip"], 0, 4))
        ts = A.op(lambda e: e.activation(skB, skB, ACT.Sigmoid), c_a.now)
        for a in range(4):
            tsk = V.op(lambda e, a=a: e.tensor_scalar(mk[:, a, :], mk[:, a, :], skB[0:P, a:a + 1], None, ALU.mult), ts)
        t = V.chain([
            lambda e: e.tensor_scalar(den, acc1[:, :, D:RW], 1e-30, None, ALU.max),
            lambda e: e.reciprocal(den, den),
        ], last)
        rg, rt = Ring(ag), Ring(agT)
        rb = Ring(bank[4:6])
        rm = Ring(bank[0:4])
        T.wait(last)
        ats = {}

        def pre(m):
            i, a_, f = rg.take()
            t1 = V.op(lambda e: e.tensor_tensor(
                a_.rearrange("p (h d) -> p h d", h=4), acc1[:, m, 0:D].rearrange("p (h d) -> p h d", h=4),
                bc(den[:, m, :], 2, 64), ALU.mult), t, f)
            ib, b, fb = rb.take()
            for k in range(2):
                tp = T.op(lambda e: e.transpose(b[:, k * P:(k + 1) * P], a_[:, 128 * k:128 * k + 128], ident[0:P, 0:P]),
                          t1, fb)
            rg.free[i] = tp
            it, at, ft = rt.take()
            ta = A.op(lambda e: e.activation(at, b[:, 0:2 * P].rearrange("p (k n) -> p k n", k=2), ACT.Copy), tp, ft)
            rb.free[ib] = ta
            ats[m] = (it, at, ta)

        def post(m):
            it, at, ta = ats.pop(m)
            tv = None
            for half in range(2):
                im, ps, fm = rm.take()
                for k in range(2):
                    tm = T.op(lambda e: e.matmul(ps[0:P, :], at[:, k, :], AL[:, k, 512 * half:512 * half + 512],
                                                 start=k == 0, stop=k == 1), ta, fm, c_a.now)
                for a in range(2):
                    tv = V.op(lambda e: e.scalar_tensor_tensor(
                        X[:, m, :], ps[0:P, D * a:D * a + D], mk[:, 2 * half + a, m:m + 1], X[:, m, :], ALU.mult, ALU.add),
                        tm, tsk, tv)
                rm.free[im] = tv
            rt.free[it] = tm

        pre(0)
        for m in range(NT):
            if m + 1 < NT:
                pre(m + 1)
            post(m)
        barrier()

        f1 = Arena(BASE)
        Y = f1.get(NT, D, parts=P)
        ty = ln_apply(Y, X, ln_stats(X, 1e-5))
        T.wait(ty)
        moe, tmoe = experts(f1, 8, Y, I["f1_w"], I["f1_b2"], I["f1_gw"], I["f1_gb"],
                            ACT.Gelu, False)
        t = V.op(lambda e: e.tensor_tensor(X, X, moe, ALU.add), tmoe)
        c_o = chan()
        S.wait(c_o.dma125(S, out.rearrange("(t p) d -> p t d", p=P), X, t))
        barrier()


def kernel(**a):
    import concourse.bacc as bacc
    from concourse.bass_utils import run_bass_kernel_spmd

    def arr(v):
        return np.ascontiguousarray(np.asarray(v))

    a = {k: np.asarray(v) for k, v in a.items()}

    def edges(v, fill):
        w = np.full(EP, fill, v.dtype)
        w[:E] = v
        return w.reshape(128, C)

    def experts(w1, b1, w2):
        n = len(w1)
        return np.concatenate([w1.reshape(n, 2, 128, 512).transpose(0, 2, 1, 3).reshape(n, 128, 1024),
                               w2.reshape(n, 4, 128, D).transpose(0, 2, 1, 3).reshape(n, 128, 1024),
                               b1.reshape(n, 4, 128).transpose(0, 2, 1)], 2)

    perm = np.array([96 * (b % 8) + 32 * (b // 8) + i for b in range(24) for i in range(32)])
    p = np.arange(128)
    feeds = {
        "x": a["x"], "src": edges(a["src"], 0), "dst": edges(a["dst"], PADN), "etype": edges(a["edge_type_8"], 0),
        "edge_attr": a["edge_attr_128"], "ntype": a["node_type_4"].reshape(NT, P).T,
        "c_ident": np.eye(128, dtype=np.float32),
        "c_nid": np.arange(N, dtype=np.int32).reshape(NT, P).T,
        "c_pid": p[:, None].astype(np.float32), "c_tri": (p[:, None] < p[None, :]).astype(np.float32),
        "c_iota": np.tile(np.arange(128, dtype=np.float32), (128, 1)),
        "c_blk": (p[:, None] // 32 == p[None, :] // 32).astype(np.float32),
        "c_hm4": (p[:, None] // 32 == np.arange(4)[None, :]).astype(np.float32),
        "c_steps": np.tile(np.arange(NS, dtype=np.float32), (128, 1)),
        "WnT": a["L0_gnn_Wn"].T, "bn": a["L0_gnn_bn"],
        "WeB": np.concatenate([a["L0_gnn_We"], a["L0_gnn_be"][:, None]], 1),
        "attn": a["L0_gnn_attn"].reshape(D), "attnC": a["L0_gnn_attn"].reshape(2, 128).T,
        "w_qkv": a["L0_mix_w_qkv"][perm][:, :, 2].T,
        "bn_gamma": a["L0_mix_bn_gamma"][perm].reshape(6, 128).T, "bn_beta": a["L0_mix_bn_beta"][perm].reshape(6, 128).T,
        "w_dw": a["L0_mix_w_dw"][perm][:, 0, 2].reshape(6, 128).T,
        "w_pw": a["L0_mix_w_pw"][perm].reshape(6, 4, 32, 32).transpose(1, 3, 0, 2),
        "w_res": a["L0_mix_w_res"][:, :, 0].T, "b_res": a["L0_mix_b_res"],
        "f0_gw": a["L0_ffn_gate_w"], "f0_gb": a["L0_ffn_gate_b"], "f0_w": experts(a["L0_ffn_w1"], a["L0_ffn_b1"], a["L0_ffn_w2"]),
        "f0_b2": a["L0_ffn_b2"],
        "f0_gamma": a["L0_ffn_gamma"], "f0_beta": a["L0_ffn_beta"],
        "k_lin": a["L1_gnn_k_linears"], "q_lin": a["L1_gnn_q_linears"], "v_lin": a["L1_gnn_v_linears"],
        "a_lin": a["L1_gnn_a_linears"], "pri": a["L1_gnn_relation_pri"].reshape(32), "skip": a["L1_gnn_skip"],
        "att": a["L1_gnn_relation_att"].transpose(1, 3, 0, 2), "msg": a["L1_gnn_relation_msg"].transpose(1, 2, 0, 3),
        "m1_wqkv": a["L1_mix_w_qkv"], "m1_wout": a["L1_mix_w_out"], "m1_bout": a["L1_mix_b_out"],
        "m1_wn1": a["L1_mix_w_norm1"].reshape(2, 128).T, "m1_wn2": a["L1_mix_w_norm2"],
        "f1_gw": a["L1_ffn_Wg"], "f1_gb": a["L1_ffn_bg"], "f1_w": experts(a["L1_ffn_W1"], a["L1_ffn_b1"], a["L1_ffn_W2"]),
        "f1_b2": a["L1_ffn_b2"],
    }
    nc = bacc.Bacc("TRN2", target_bir_lowering=False, num_devices=1)
    arrays, ins = {}, {}
    for name, v in feeds.items():
        v = arr(v)
        arrays["in_" + name] = v
        ins[name] = nc.dram_tensor("in_" + name, v.shape, mybir.dt.from_np(v.dtype), kind="ExternalInput").ap()
    out = nc.dram_tensor("out_0", (N, D), F32, kind="ExternalOutput").ap()
    build(nc, ins, out)
    r = run_bass_kernel_spmd(nc, [arrays], core_ids=[0])
    return r.results[0]["out_0"]
```

```python
from contextlib import ExitStack
import math

import numpy as np
import concourse.bass as bass
from concourse import mybir

F32 = mybir.dt.float32
I32 = mybir.dt.int32
U32 = mybir.dt.uint32
BF16 = mybir.dt.bfloat16
ALU = mybir.AluOpType
ACT = mybir.ActivationFunctionType
X_AX = mybir.AxisListType.X

N = 3125
P = 125
NT = 25
D = 256
E = 100000
C = 784
EP = 128 * C
QC = C // 4
NTI = EP // 512
NS = NTI + NT - 1
WROW = 2052
MS = (2 * N + 16 * 127) // 128 * 128
NTS = (N + 4 * 127) // 128
RW = 260
BIG = 1.0e30
PADN = 4000
MX = float(np.float32(0.99999))
T0 = float(0.5 * math.log((1.0 + MX) / (1.0 - MX)))
BLK = [(500 * b, min(500, N - 500 * b)) for b in range(7)]


class Eng:

    def __init__(self, engine, sem):
        self.engine, self.sem, self.n, self.seen = engine, sem, 0, {}

    def wait(self, *tokens):
        for t in tokens:
            if t is None:
                continue
            if isinstance(t, list):
                self.wait(*t)
                continue
            s, v = t
            if self.seen.get(id(s), 0) < v:
                self.seen[id(s)] = v
                self.engine.wait_ge(s, v)

    def op(self, fn, *tokens):
        self.wait(*tokens)
        self.n += 1
        fn(self.engine).then_inc(self.sem, 1)
        return (self.sem, self.n)

    def chain(self, fns, *tokens):
        t = None
        for k, fn in enumerate(fns):
            t = self.op(fn, t) if k else self.op(fn, *tokens)
        return t

    def do(self, fn, *tokens):
        self.wait(*tokens)
        fn(self.engine)

    @property
    def now(self):
        return (self.sem, self.n)


class Chan:

    def __init__(self, sem):
        self.sem, self.n = sem, 0

    def dma(self, eng, out, in_, *tokens):
        eng.wait(*tokens)
        self.n += 16
        eng.engine.dma_start(out, in_).then_inc(self.sem, 16)
        return (self.sem, self.n)

    def dma125(self, eng, out, in_, *tokens):
        self.dma(eng, out[0:112], in_[0:112], *tokens)
        return self.dma(eng, out[112:P], in_[112:P])

    @property
    def now(self):
        return (self.sem, self.n)


class Ring:

    def __init__(self, bufs):
        self.bufs, self.free, self.k = bufs, [None] * len(bufs), 0

    def take(self):
        i = self.k % len(self.bufs)
        self.k += 1
        return i, self.bufs[i], self.free[i]


def build(nc, I, out):
    ctx = ExitStack()
    with ctx:
        nsem = [0]

        def sem():
            nsem[0] += 1
            return ctx.enter_context(nc.semaphore(f"s{nsem[0]}"))

        V, A, T, G, S = (Eng(e, sem()) for e in (nc.vector, nc.scalar, nc.tensor, nc.gpsimd, nc.sync))
        ENG = [V, A, T, G, S]
        chans = []

        def chan():
            chans.append(Chan(sem()))
            return chans[-1]

        def barrier():
            every = [e.now for e in ENG if e.n] + [c.now for c in chans if c.n]
            for e in ENG:
                e.wait(every)

        WIDE = 52800
        mem = ctx.enter_context(nc.sbuf_tensor("mem", [128, WIDE], F32))
        bank = [ctx.enter_context(nc.psum_tensor(f"bank{i}", [128, 512], F32)) for i in range(8)]

        class Arena:
            def __init__(self, at):
                self.at = at

            def get(self, *dims, parts=128, dt=None):
                n = int(np.prod(dims))
                v = mem[0:parts, self.at:self.at + n]
                self.at += n
                assert self.at <= WIDE, self.at
                if dt is not None:
                    v = v.bitcast(dt)
                if len(dims) == 2:
                    v = v.rearrange("p (a b) -> p a b", b=dims[1])
                if len(dims) == 3:
                    v = v.rearrange("p (a b c) -> p a b c", b=dims[1], c=dims[2])
                return v

        def dram(name, shape, dt=F32):
            return nc.dram_tensor(name, shape, dt).ap()

        hp_d = dram("hp_d", [N, RW])
        hs_d = dram("hs_d", [EP, RW])
        rec0_d = dram("rec0_d", [EP, 2])
        rec1_d = dram("rec1_d", [EP, 5])
        kvi_d = dram("kvi_d", [EP, 1], I32)
        dst_d = dram("dst_d", [2, EP], BF16)
        sc_d = dram("sc_d", [EP + 512 * NT, 4])
        kv_d = dram("kv_d", [8 * (N + 128 * NTS), 2 * D])
        q3_d = dram("q3_d", [N + 128 * NTS, 3 * D], BF16)
        rid_d = dram("rid_d", [128 * NTS, 1], I32)
        vs_d = dram("vs_d", [512 * NS, D])
        xs_d = dram("xs_d", [MS, D])
        ys_d = dram("ys_d", [2 * N + MS, D])
        rie_d = dram("rie_d", [MS, 1], I32)

        def bc(ap, axis, n):
            v = ap.unsqueeze(axis)
            shape = list(v.shape)
            shape[axis] = n
            return v.to_broadcast(shape)

        def rowb(ap, off, n, parts=128):
            return bass.AP(ap.tensor, off, [[0, parts], [1, n]])

        top = Arena(0)
        ident = top.get(128)
        iota = top.get(128)
        blk = top.get(128)
        tri = top.get(128)
        hm4 = top.get(4)
        ones = top.get(128)
        JV = top.get(NS)
        REG = top.get(3, NS, dt=I32)
        SAME = top.get(NS)
        pid = top.get(1)
        mk = top.get(4, NT, parts=P)
        nid = top.get(2, NT, parts=P, dt=I32)
        tslI = top.get(NT, parts=P, dt=I32)
        tsrI = top.get(NT, parts=P, dt=I32)
        rid = top.get(NTS, dt=I32)
        tauI = top.get(NTS, parts=P, dt=I32)
        XAT = top.at
        X = top.get(NT, D, parts=P)
        mv = top.get(NT, 2, parts=P)
        st = top.get(NT, 6, parts=P)
        rstd = top.get(NT, parts=P)
        BASE = top.at

        c_in = chan()
        c_x = chan()
        x_v = I["x"].rearrange("(t p) d -> p t d", p=P)
        GRP = [range(g, g + 5) for g in range(0, NT, 5)]
        c_xg = [chan() for _ in GRP]
        for g, c in zip(GRP, c_xg):
            c.dma125(S, X[:, g[0]:g[-1] + 1, :], x_v[:, g[0]:g[-1] + 1, :])
        for ap, name in ((ident, "c_ident"), (iota, "c_iota"), (blk, "c_blk"), (tri, "c_tri"), (pid, "c_pid"), (nid, "c_nid"), (hm4, "c_hm4")):
            c_in.dma(S, ap, I[name])
        t_ones = V.op(lambda e: e.memset(ones, 1.0))

        def ln_begin(g, src, eps, *tokens):
            a, b = g[0], g[-1] + 1
            for t in g:
                V.op(lambda e: e.bn_stats(st[:, t, :], src[:, t, :]), *tokens)
            for t in g:
                tk = V.op(lambda e: e.bn_aggr(mv[:, t, :], st[:, t, :]), V.now)
            tk = V.op(lambda e: e.tensor_scalar(rstd[:, a:b], mv[:, a:b, 1], eps, None, ALU.add), tk)
            return A.op(lambda e: e.activation(rstd[:, a:b], rstd[:, a:b], ACT.Sqrt), tk)

        def ln_end(g, dst, src, tok):
            a, b = g[0], g[-1] + 1
            tk = V.op(lambda e: e.reciprocal(rstd[:, a:b], rstd[:, a:b]), tok)
            tk = V.op(lambda e: e.scalar_tensor_tensor(mv[:, a:b, 0], mv[:, a:b, 0], -1.0, rstd[:, a:b], ALU.mult, ALU.mult), tk)
            return [A.op(lambda e: e.activation(dst[:, t, :], src[:, t, :], ACT.Identity, bias=mv[:, t, 0:1],
                                                scale=rstd[:, t:t + 1]), tk) for t in g]

        def ln_pipe(dst, src, eps, before):
            done, late = [], None
            for g in GRP:
                for t in g:
                    tk = before(t)
                now = (g, ln_begin(g, src, eps, tk))
                if late:
                    done += ln_end(late[0], dst, src, late[1])
                late = now
            return done + ln_end(late[0], dst, src, late[1])

        s2 = Arena(BASE)
        TT = s2.get(6, N)
        HQAT = s2.at
        HQ = s2.get(2, N)
        Wc = s2.get(2, 768)
        srcI = s2.get(C, dt=I32)
        dstF = s2.get(C)
        Pt = s2.get(C)
        tt = s2.get(C)
        wB = s2.get(129)
        bng = s2.get(6)
        bnb = s2.get(6)
        ss = s2.get(NT, parts=P)
        fac = s2.get(NT, parts=P)
        sm = [s2.get(NT, parts=P) for _ in range(5)]
        s2_own = Arena(s2.at)
        dstI = Pt.bitcast(I32)

        c_w = chan()
        c_w.dma(A, Wc, I["w_qkv"].rearrange("(k p) o -> p k o", p=128))
        c_e = chan()
        c_e.dma(S, srcI, I["src"])
        c_e.dma(S, dstI, I["dst"])
        c_w.dma(A, bng, I["bn_gamma"])
        c_w.dma(A, bnb, I["bn_beta"])

        s1 = Arena(s2.at)
        WnT = s1.get(2, D)
        WeB = s1.get(2, 129)
        attnC = s1.get(2)
        attnCB = s1.get(2, 128)
        attnB = s1.get(D)
        bnB = s1.get(D)
        XNb = [s1.get(D, parts=P) for _ in range(3)]
        XTb = [s1.get(2, P) for _ in range(3)]
        HPb = [s1.get(RW, parts=P) for _ in range(4)]
        junk2 = s1.get(D, parts=P)
        c_1 = chan()
        c_1.dma(A, WnT, I["WnT"].rearrange("(k p) n -> p k n", p=128))
        c_1.dma(A, WeB, I["WeB"].rearrange("(k p) n -> p k n", p=128))
        c_1.dma(A, attnC, I["attnC"])
        c_1.dma(A, attnB, rowb(I["attn"], 0, D))
        c_1.dma(A, bnB, rowb(I["bn"], 0, D))

        tk = V.op(lambda e: e.tensor_copy(attnCB, bc(attnC, 2, 128)), c_1.now)
        for kc in range(2):
            tw = T.op(lambda e, kc=kc: e.matmul(bank[7][:, 0:129], attnCB[:, kc, :], WeB[:, kc, :],
                                                start=kc == 0, stop=kc == 1), tk, c_1.now)
        t_wB = V.op(lambda e: e.tensor_copy(wB, bank[7][:, 0:129]), tw)
        t_dst = V.op(lambda e: e.tensor_copy(dstF, dstI), c_e.now)

        late = [ln_begin(g, X, 1e-5, c.now) for g, c in zip(GRP, c_xg)]
        for g, tk in zip(GRP, late):
            trs = V.op(lambda e: e.reciprocal(rstd[:, g[0]:g[-1] + 1], rstd[:, g[0]:g[-1] + 1]), tk)
        rx, rt, rp = Ring(XNb), Ring(XTb), Ring(HPb)
        tone = [V.op(lambda e, b=b: e.memset(b, 1.0)) for b in HPb][-1]
        rb = Ring(bank[0:3])
        rm = Ring(bank[3:6])
        c_hp = [chan() for _ in HPb]
        xns, xts = {}, {}

        def norm(t):
            ix, xn, fx = rx.take()
            xns[t] = (ix, xn, V.op(lambda e: e.tensor_scalar(xn, X[:, t, :], mv[:, t, 0:1], rstd[:, t:t + 1],
                                                             ALU.subtract, ALU.mult), trs, fx))

        def turn(t):
            ix, xn, t1 = xns.pop(t)
            ib, b, fb = rb.take()
            T.wait(c_in.now, fb, t1)
            for k in range(2):
                tp = T.op(lambda e: e.transpose(b[:, k * P:(k + 1) * P], xn[:, 128 * k:128 * k + 128], ident[0:P, 0:P]))
            rx.free[ix] = tp
            it, xt, ft = rt.take()
            rb.free[ib] = t3 = A.op(lambda e: e.activation(xt, b[:, 0:2 * P].rearrange("p (k n) -> p k n", k=2), ACT.Copy),
                                    tp, ft)
            xts[t] = (it, xt, t3)

        def table(t):
            it, xt, t3 = xts.pop(t)
            im, m, fm = rm.take()
            for k in range(2):
                tm = T.op(lambda e: e.matmul(m[0:P, 0:D], xt[:, k, :], WnT[:, k, :], start=k == 0, stop=k == 1),
                          t3, fm, c_1.now)
            rt.free[it] = tm
            ip, hp, fp = rp.take()
            t5 = V.op(lambda e: e.tensor_tensor(hp[:, 0:D], m[0:P, 0:D], bnB[0:P, :], ALU.add), tm, fp, tone)
            rm.free[im] = t5
            t6 = V.op(lambda e: e.tensor_tensor_reduce(junk2, hp[:, 0:D], attnB[0:P, :], 1.0, 0.0, ALU.mult,
                                                       ALU.add, hp[:, D + 1:D + 2]), t5, V.now)
            rp.free[ip] = c_hp[ip].dma125(S, hp_d[P * t:P * t + P, :], hp, t6)

        s1t = Arena(BASE)
        under = s1t.get(C)
        cnt = s1t.get(NT - 1)
        GJ = s1t.get(NT - 1)
        GI = s1t.get(NT - 1, dt=I32)
        jn = s1t.get(NT - 1)
        gs = s1t.get(NS)
        cmp = s1t.get(NS, NT - 1)
        TJ = s1t.get(NS)
        ntI = s1t.get(NT, parts=P, dt=I32)
        ntF = s1t.get(NT, parts=P)
        c_g = chan()
        c_g.dma(S, gs, I["c_steps"])
        c_g.dma(S, ntI, I["ntype"])

        def begun(j):
            return V.op(lambda e: e.tensor_scalar(under, dstF, float(P * j), None, ALU.is_lt, ALU.add,
                                                  accum_out=cnt[:, j - 1:j]), t_dst, V.now)

        norm(0)
        norm(1)
        turn(0)
        for t in range(NT):
            if t + 2 < NT:
                norm(t + 2)
            if t + 1 < NT:
                turn(t + 1)
            table(t)
        barrier()

        def slots(ar, hot, NE, nsl, groupI, tok):
            keep = ar.get(NE, NT, parts=P)
            cum = ar.get(NE, NT, parts=P)
            slot = ar.get(NE, NT, parts=P)
            cnt = ar.get(NE, parts=P)
            cntI = ar.get(NE, parts=P, dt=I32)
            t0 = ar.get(NE, parts=P)
            cmp = ar.get(nsl, NE - 1, parts=P)
            es = ar.get(nsl, parts=P)
            T.op(lambda e: e.matmul(bank[3][0:P, 0:NT * NE], tri[0:P, 0:P], hot, start=True, stop=True), tok)
            tm = T.op(lambda e: e.matmul(bank[4][0:P, 0:NT * NE], ones[0:P, 0:P], hot, start=True, stop=True))
            pre = bank[3][0:P, 0:NT * NE].rearrange("p (e t) -> p e t", t=NT)
            tot = bank[4][0:P, 0:NT * NE].rearrange("p (e t) -> p e t", t=NT)
            flat = lambda v: v.rearrange("p e t -> p (e t)")
            return slot, V.chain([
                lambda e: e.memset(keep, 1.0),
                lambda e: e.memset(keep[:, :, 0:1], 0.0),
                lambda e: e.tensor_tensor_scan(flat(cum), flat(keep), bank[4][0:P, 0:NT * NE], 0.0, ALU.mult, ALU.add),
                lambda e: e.tensor_scalar(cntI, cum[:, :, NT - 1], 127.0, None, ALU.add),
                lambda e: e.tensor_scalar(cntI, cntI, 7, None, ALU.arith_shift_right),
                lambda e: e.tensor_copy(cnt, cntI),
                lambda e: e.tensor_tensor_scan(t0, ones[0:P, 0:NE], cnt, 0.0, ALU.mult, ALU.add),
                lambda e: e.tensor_tensor(t0, t0, cnt, ALU.subtract),
                lambda e: e.tensor_tensor(cmp, bc(t0[:, 1:NE], 1, nsl), bc(iota[0:P, 0:nsl], 2, NE - 1), ALU.is_le),
                lambda e: e.tensor_reduce(es, cmp, X_AX, ALU.add),
                lambda e: e.tensor_copy(groupI, es),
                lambda e: e.tensor_tensor(slot, cum, tot, ALU.subtract),
                lambda e: e.tensor_tensor(slot, slot, pre, ALU.add),
                lambda e: e.scalar_tensor_tensor(slot, bc(t0, 2, NT), 128.0, slot, ALU.mult, ALU.add),
            ], tm)

        def slow(fns, *tokens):
            for k, fn in enumerate(fns):
                tk = V.op(fn, *(tokens if k == 0 else (V.now,)))
                if k % 4 == 3:
                    yield
            return tk

        def prepare():
            tm = T.op(lambda e: e.matmul(bank[7][:, 0:NT - 1], ones, cnt, start=True, stop=True), V.now)
            tk = yield from slow([
                lambda e: e.tensor_copy(GI, bank[7][:, 0:NT - 1]),
                lambda e: e.tensor_scalar(GI, GI, 9, None, ALU.arith_shift_right),
                lambda e: e.tensor_copy(GJ, GI),
                lambda e: e.tensor_tensor(GJ, GJ, iota[:, 1:NT], ALU.add),
                lambda e: e.tensor_tensor(cmp, bc(GJ, 1, NS), bc(gs, 2, NT - 1), ALU.is_le),
                lambda e: e.tensor_reduce(TJ, cmp, X_AX, ALU.add),
                lambda e: e.tensor_scalar(JV, TJ, float(P), None, ALU.mult),
                lambda e: e.tensor_copy(REG[:, 0, :], TJ),
                lambda e: e.tensor_tensor(TJ, gs, TJ, ALU.subtract),
                lambda e: e.tensor_copy(REG[:, 1, :], TJ),
                lambda e: e.memset(SAME[:, 0:1], 0.0),
                lambda e: e.tensor_tensor(SAME[:, 1:NS], TJ[:, 1:NS], TJ[:, 0:NS - 1], ALU.is_equal),
                lambda e: e.tensor_tensor(gs, gs, TJ, ALU.subtract),
                lambda e: e.tensor_tensor(gs, gs, TJ, ALU.subtract),
                lambda e: e.tensor_scalar(gs, gs, float(NTI), None, ALU.add),
                lambda e: e.tensor_tensor(gs[:, 0:NS - 1], gs[:, 0:NS - 1], SAME[:, 1:NS], ALU.mult),
                lambda e: e.memset(gs[:, NS - 1:NS], 0.0),
                lambda e: e.tensor_tensor(gs, gs, TJ, ALU.add),
                lambda e: e.tensor_copy(REG[:, 2, :], gs),
            ], tm, c_g.now)
            sm_ = s1t.get(4, NT, parts=P)
            slF = s1t.get(NT, parts=P)
            spare = s1t.get(NTS)
            tk = V.op(lambda e: e.tensor_copy(ntF, ntI), c_g.now)
            for a in range(4):
                tk = V.op(lambda e: e.tensor_scalar(mk[:, a, :], ntF, float(a), None, ALU.is_equal), V.now)
            yield
            slot, tk = slots(s1t, mk, 4, NTS, tauI, tk)
            yield
            yield from slow([
                lambda e: e.tensor_tensor(sm_, slot, mk, ALU.mult),
                lambda e: e.tensor_reduce(slF, sm_.rearrange("p e t -> p t e"), X_AX, ALU.add),
                lambda e: e.tensor_copy(tslI, slF),
                lambda e: e.tensor_scalar(tsrI, tslI, 7, None, ALU.arith_shift_right),
                lambda e: e.tensor_copy(ntF, tsrI),
                lambda e: e.scalar_tensor_tensor(slF, ntF, -128.0, slF, ALU.mult, ALU.add),
                lambda e: e.scalar_tensor_tensor(slF, slF, float(NTS), ntF, ALU.mult, ALU.add),
                lambda e: e.tensor_copy(tsrI, slF),
                lambda e: e.tensor_scalar(spare, ones[:, 0:NTS], pid, float(NTS), ALU.mult, ALU.mult),
                lambda e: e.tensor_tensor(spare, spare, iota[:, 0:NTS], ALU.add),
                lambda e: e.tensor_scalar(rid, spare, float(N), None, ALU.add),
            ], tk)

        own = Arena(s2_own.at)
        gbuf = [own.get(4, RW) for _ in range(4)]
        EAb = [own.get(8, 128) for _ in range(2)]

        def pass1():
            rg = Ring(gbuf)
            cg = [chan() for _ in gbuf]
            cs = [chan() for _ in gbuf]
            hs_v = hs_d.rearrange("(p c) d -> p c d", p=128)
            late = []

            def scores(k, i, g, tg):
                rg.free[i] = [rg.free[i], G.op(lambda e: e.tensor_copy(Pt[:, 4 * k:4 * k + 4], g[:, :, D + 1]), tg)]

            for k in range(QC):
                i, g, fg = rg.take()
                G.wait(fg)
                for c in range(4):
                    cg[i].n += 16
                    G.do(lambda e, g=g, c=c, k=k, s=cg[i].sem: e.indirect_dma_start(
                        out=g[:, c, :], out_offset=None, in_=hp_d,
                        in_offset=bass.IndirectOffsetOnAxis(ap=srcI[:, 4 * k + c:4 * k + c + 1], axis=0)).then_inc(s, 16))
                rg.free[i] = cs[i].dma(S, hs_v[:, 4 * k:4 * k + 4, :], g, cg[i].now)
                late.append((k, i, g, cg[i].now))
                if len(late) > 2:
                    scores(*late.pop(0))
                yield
            for x_ in late:
                scores(*x_)

        def edge_logits():
            ce = [chan() for _ in EAb]
            re = Ring(EAb)
            tz = [V.op(lambda e, b=b: e.memset(b, 0.0)) for b in EAb][-1]
            ea = I["edge_attr"]
            full = (E - 127 * C) // 8
            got = {}

            def load(k):
                i, b, fb = re.take()
                bf = b.rearrange("p a f -> p (a f)")

                def src(p0, n):
                    return bass.AP(ea.tensor, (C * p0 + 8 * k) * 128, [[C * 128, n], [1, 1024]])
                if k < full:
                    ce[i].dma(A, bf, src(0, 128), fb, tz)
                else:
                    ce[i].dma(A, bf[0:112], src(0, 112), fb, tz)
                    ce[i].dma(A, bf[112:127], src(112, 15))
                got[k] = (i, b, ce[i].now)

            load(0)
            for k in range(C // 8):
                if k + 1 < C // 8:
                    load(k + 1)
                i, b, tin = got.pop(k)
                t1 = V.op(lambda e: e.tensor_tensor(b, b, bc(wB[:, 0:128], 1, 8), ALU.mult), tin)
                re.free[i] = V.op(lambda e: e.tensor_reduce(tt[:, 8 * k:8 * k + 8], b, X_AX, ALU.add), t1)
                yield

        mown = Arena(own.at)

        def mixer0():
            SBs = [mem[:, HQAT + 3000 * k:HQAT + 3000 * k + 3000].rearrange("p (c n) -> p c n", c=6) for k in range(2)]
            RDs = [mown.get(4, 500) for _ in range(2)]
            sqb = [mown.get(500) for _ in range(2)]
            nbs = [[mown.get(500) for _ in range(2)] for _ in range(2)]
            Wd = mown.get(6, 128)
            bst = mown.get(7, 6)
            bmv = mown.get(6, 2)
            bsc = mown.get(6)
            bbi = mown.get(6)
            wcf = Wc.rearrange("p k o -> p (k o)")
            wres = wcf[:, 0:4 * D].rearrange("p (k n) -> p k n", k=4)
            brB = wcf[:, 4 * D:5 * D]
            wdwC = mown.get(6)
            ss3, ss4, f3, f4, n4 = sm
            FX = X
            c_m = chan()
            c_m.dma(A, wdwC, I["w_dw"])
            junk = RDs[0][0:P, 0, 0:D]
            H0b = [RDs[0][0:P, q, 0:D] for q in range(1, 4)]
            nmr = sm[4]
            tn = V.op(lambda e: e.scalar_tensor_tensor(nmr, mv[:, :, 0], -1.0, rstd, ALU.mult, ALU.mult))
            for t in range(NT):
                tq = A.op(lambda e, t=t: e.activation(junk, X[:, t, :], ACT.Square, bias=nmr[:, t:t + 1],
                                                      scale=rstd[:, t:t + 1], accum_out=ss[:, t:t + 1]), tn, A.now)
            tq = A.op(lambda e: e.activation(ss, ss, ACT.Sqrt), tq)
            y, y2, r, u = sm[0:4]
            tk = V.chain([
                lambda e: e.tensor_scalar(ss, ss, 1e-15, None, ALU.max),
                lambda e: e.tensor_scalar(y, ss, MX, None, ALU.min),
                lambda e: e.tensor_scalar(r, y, -1.0, 1.0, ALU.mult, ALU.add),
                lambda e: e.reciprocal(r, r),
                lambda e: e.scalar_tensor_tensor(r, y, 1.0, r, ALU.add, ALU.mult),
            ], tq)
            tk = A.op(lambda e: e.activation(r, r, ACT.Ln), tk)
            tk = V.chain([
                lambda e: e.tensor_tensor(y2, y, y, ALU.mult),
                lambda e: e.tensor_scalar(u, y2, 1.0 / 7.0, 0.2, ALU.mult, ALU.add),
                lambda e: e.tensor_tensor(u, u, y2, ALU.mult),
                lambda e: e.tensor_scalar(u, u, 1.0 / 3.0, None, ALU.add),
                lambda e: e.tensor_tensor(u, u, y2, ALU.mult),
                lambda e: e.scalar_tensor_tensor(u, u, 1.0, y, ALU.add, ALU.mult),
                lambda e: e.tensor_scalar(r, r, 0.5, None, ALU.mult),
                lambda e: e.tensor_tensor(u, u, r, ALU.subtract),
                lambda e: e.tensor_scalar(y2, y, 0.05, None, ALU.is_lt),
                lambda e: e.tensor_tensor(u, u, y2, ALU.mult),
                lambda e: e.tensor_tensor(u, u, r, ALU.add),
                lambda e: e.reciprocal(fac, ss),
                lambda e: e.tensor_tensor(fac, fac, u, ALU.mult),
            ], tk)
            tfac = tk
            tk = V.chain([
                lambda e: e.tensor_tensor(nmr, nmr, fac, ALU.mult),
                lambda e: e.tensor_tensor(fac, fac, rstd, ALU.mult),
            ], tfac)
            yield
            rh = Ring(H0b)
            rb = Ring(bank[0:3])
            hs = {}

            def ball(t):
                ih, h0, fh = rh.take()
                hs[t] = (ih, h0, A.op(lambda e: e.activation(h0, X[:, t, :], ACT.Identity, bias=nmr[:, t:t + 1],
                                                             scale=fac[:, t:t + 1]), tk, fh))
            ball(0)
            prep = prepare()
            for t in range(NT):
                if t:
                    begun(t)
                if t + 1 < NT:
                    ball(t + 1)
                ih, h0, th = hs.pop(t)
                ib, b, fb = rb.take()
                for k in range(2):
                    tp = T.op(lambda e: e.transpose(b[:, k * P:(k + 1) * P], h0[:, 128 * k:128 * k + 128], ident[0:P, 0:P]),
                              th, fb)
                rh.free[ih] = tp
                rb.free[ib] = tHQ = V.op(lambda e: e.tensor_copy(HQ[:, :, P * t:P * t + P],
                                                                 b[:, 0:2 * P].rearrange("p (k n) -> p k n", k=2)), tp)
                yield
            for _ in prep:
                pass
            T.wait(tHQ)
            tn = [None] * 6
            for oc in range(6):
                tst = []
                for b, (l0, n) in enumerate(BLK):
                    i, ps, f = rb.take()
                    for q in range(2):
                        tm = T.op(lambda e: e.matmul(ps[:, 0:n], Wc[:, q, 128 * oc:128 * oc + 128],
                                                     HQ[:, q, l0:l0 + n], start=q == 0, stop=q == 1), f, c_w.now)
                    ta = A.op(lambda e: e.activation(TT[:, oc, l0:l0 + n], ps[:, 0:n], ACT.Copy), tm)
                    rb.free[i] = ta
                    tst.append(V.op(lambda e: e.bn_stats(bst[:, b, :], TT[:, oc, l0:l0 + n]), ta,
                                    tn[oc - 1] if oc else None))
                    yield
                tk = V.op(lambda e: e.bn_aggr(bmv[:, oc, :], bst), *tst)
                tn[oc] = tk
                c1, c2 = bsc[:, oc:oc + 1], bbi[:, oc:oc + 1]
                tk = V.op(lambda e: e.tensor_scalar(c1, bmv[:, oc, 1:2], 1e-5, None, ALU.add), tk)
                tk = A.op(lambda e: e.activation(c1, c1, ACT.Sqrt), tk)
                tbn = V.chain([
                    lambda e: e.reciprocal(c1, c1),
                    lambda e: e.tensor_tensor(c1, c1, bng[:, oc:oc + 1], ALU.mult),
                    lambda e: e.tensor_tensor(c2, c1, bmv[:, oc, 0:1], ALU.mult),
                    lambda e: e.tensor_tensor(c2, bnb[:, oc:oc + 1], c2, ALU.subtract),
                ], tk, c_w.now)
            tconv = T.now
            c_m.dma(A, wres, I["w_res"].rearrange("(k p) n -> p k n", p=128), tconv)
            c_m.dma(A, brB, rowb(I["b_res"], 0, D))
            tz = V.op(lambda e: e.memset(Wd, 0.0))
            for g in range(4):
                c_m.dma(A, Wd[32 * g:32 * g + 32, :, 32 * g:32 * g + 32], I["w_pw"][g], tz)
            for oc in range(6):
                twd = V.op(lambda e: e.tensor_scalar(Wd[:, oc, :], Wd[:, oc, :], wdwC[:, oc:oc + 1], None, ALU.mult),
                           c_m.now)
            yield
            rsq = Ring(sqb)
            rf = Ring([bank[4], bank[5]])

            def squares(ps, src, k, last, tok, mine):
                i, sq, f = rsq.take()
                n = src.shape[-1]
                ta = A.op(lambda e: e.activation(sq[:, 0:n], src, ACT.Square), f, tok)
                rsq.free[i] = mine[0] = T.op(lambda e: e.matmul(ps[:, 0:n], ones, sq[:, 0:n], start=k == 0, stop=k == last), ta)
                return ta

            def factor(ps, nb, n, mine, free):
                a = A.op(lambda e: e.activation(nb[0][:, 0:n], ps[:, 0:n], ACT.Sqrt), mine, free)
                t = V.chain([
                    lambda e: e.tensor_scalar(nb[0][:, 0:n], nb[0][:, 0:n], 1e-15, None, ALU.max),
                    lambda e: e.reciprocal(nb[1][:, 0:n], nb[0][:, 0:n]),
                    lambda e: e.scalar_tensor_tensor(nb[1][:, 0:n], nb[0][:, 0:n], T0, nb[1][:, 0:n], ALU.min, ALU.mult),
                ], a)
                return a, t

            def blocks(which, SB, RD, nb, psn):
                fnorm = fnb = fO = None
                mine = [None]
                for b in which:
                    l0, n = BLK[b]
                    tb = TT[:, :, l0:l0 + n]
                    T.wait(fnorm)
                    for oc in range(6):
                        ta = A.op(lambda e: e.activation(tb[:, oc, :], tb[:, oc, :], ACT.Relu, bias=bbi[:, oc:oc + 1],
                                                         scale=bsc[:, oc:oc + 1]), tbn)
                        squares(psn, tb[:, oc, :], oc, 5, ta, mine)
                        if oc == 2:
                            yield
                    fnorm, t = factor(psn, nb, n, mine, fnb)
                    yield
                    tT = V.op(lambda e: e.tensor_tensor(tb, tb, bc(nb[1][:, 0:n], 1, 6), ALU.mult), t)
                    T.wait(fnorm)
                    for oc in range(6):
                        i, ps, f = rb.take()
                        tm = T.op(lambda e: e.matmul(ps[:, 0:n], Wd[:, oc, :], tb[:, oc, :], start=True, stop=True), f, tT, twd)
                        if oc < 4:
                            tv = V.op(lambda e: e.tensor_scalar(SB[:, oc, 0:n], ps[:, 0:n], 0.0, None, ALU.max), tm, tconv, fO)
                        else:
                            tv = V.op(lambda e: e.tensor_copy(SB[:, oc, 0:n], ps[:, 0:n]), tm, tconv, fO)
                        squares(psn, tb[:, oc, :], 2 * oc, 11, tT, mine)
                        rb.free[i] = squares(psn, ps[:, 0:n], 2 * oc + 1, 11, tv, mine)
                        yield
                    fnorm, t = factor(psn, nb, n, mine, tT)
                    f2, g2 = nb[1][:, 0:n], nb[0][:, 0:n]
                    v1, v2 = tb[:, 4:6, :], SB[:, 4:6, 0:n]
                    r1_, r2_ = RD[:, 0:2, 0:n], RD[:, 2:4, 0:n]
                    V.op(lambda e: e.tensor_tensor(g2, f2, f2, ALU.mult), t)
                    for v, r, q in ((v1, r1_, tb[:, 0:2, :]), (v2, r2_, SB[:, 0:2, 0:n])):
                        for fn in (lambda e: e.tensor_tensor(v, v, bc(f2, 1, 2), ALU.mult),
                                   lambda e: e.tensor_scalar(r, v, 1e-15, None, ALU.add),
                                   lambda e: e.reciprocal(r[:, 0, :], r[:, 0, :]),
                                   lambda e: e.reciprocal(r[:, 1, :], r[:, 1, :]),
                                   lambda e: e.tensor_tensor(v, v, r, ALU.mult),
                                   lambda e: e.tensor_tensor(v, v, bc(g2, 1, 2), ALU.mult),
                                   lambda e: e.tensor_tensor(v, v, q, ALU.mult)):
                            t = V.op(fn, V.now, fO)
                            yield
                    fnb = t
                    tv = t
                    vs = [tb[:, 4, :], tb[:, 5, :], SB[:, 4, 0:n], SB[:, 5, 0:n]]
                    for q in range(4):
                        i, ps, f = rb.take()
                        kk = tb[:, 2 + q, :] if q < 2 else SB[:, q, 0:n]
                        tm = T.op(lambda e: e.matmul(ps[:, 0:n], blk, kk, start=True, stop=True), f, c_in.now, tv if q == 0 else None)
                        tv = rb.free[i] = V.op(lambda e: e.tensor_tensor(vs[q], vs[q], ps[:, 0:n], ALU.mult), tm, t)
                        ta = A.op(lambda e: e.activation(RD[:, q, 0:n], vs[q], ACT.Square), tv)
                        yield
                    for m0 in range(0, n, P):
                        tile = (l0 + m0) // P
                        i, ps, f = rf.take()
                        T.wait(f, ta, tv, c_m.now)
                        for q in range(4):
                            T.op(lambda e: e.matmul(ps[0:P, 0:D], vs[q][:, m0:m0 + P], wres[:, q, :], start=q == 0, stop=q == 3))
                        for q in range(4):
                            tm = T.op(lambda e: e.matmul(ps[0:P, D:D + 1], RD[:, q, m0:m0 + P], ones[:, 0:1], start=q == 0,
                                                         stop=q == 3))
                        V.op(lambda e: e.tensor_copy(FX[:, tile, :], ps[0:P, 0:D]), tm)
                        rf.free[i] = V.op(lambda e: e.tensor_copy(ss3[:, tile:tile + 1], ps[0:P, D:D + 1]))
                        yield
                    fO = tm
                    yield

            pair = [blocks((0, 2, 4, 6), SBs[0], RDs[0], nbs[0], bank[3]),
                    blocks((1, 3, 5), SBs[1], RDs[1], nbs[1], bank[6])]
            ahead = 13
            while pair:
                for g in list(pair) if ahead <= 0 else pair[:1]:
                    if next(g, pair) is pair:
                        pair.remove(g)
                    yield
                ahead -= 1
            tv2 = V.now
            XL = mem[0:P, BASE:BASE + NT * D].rearrange("p (t d) -> p t d", d=D)
            tx = c_x.dma125(A, XL, I["x"].rearrange("(t p) d -> p t d", p=P), A.now, V.now, T.now)
            a = A.op(lambda e: e.activation(ss3, ss3, ACT.Sqrt), tv2)
            t = V.chain([
                lambda e: e.tensor_scalar(ss3, ss3, 1e-15, None, ALU.max),
                lambda e: e.reciprocal(f3, ss3),
                lambda e: e.scalar_tensor_tensor(f3, ss3, T0, f3, ALU.min, ALU.mult),
            ], a)
            for m in range(NT):
                t1 = V.op(lambda e: e.scalar_tensor_tensor(FX[:, m, :], FX[:, m, :], f3[:, m:m + 1], brB[0:P, :],
                                                           ALU.mult, ALU.add), t, c_m.now)
                a = A.op(lambda e: e.activation(sqb[0][0:P, 0:D], FX[:, m, :], ACT.Square, accum_out=ss4[:, m:m + 1]),
                         t1, rsq.free, A.now)
            yield
            a = A.op(lambda e: e.activation(ss4, ss4, ACT.Sqrt), a)
            t = V.op(lambda e: e.tensor_scalar(n4, ss4, 1e-15, None, ALU.max), a)
            a = A.op(lambda e: e.activation(f4, n4, ACT.Tanh), t)
            t = V.chain([
                lambda e: e.reciprocal(n4, n4),
                lambda e: e.scalar_tensor_tensor(f4, f4, MX, n4, ALU.min, ALU.mult),
            ], a)
            for m in range(NT):
                V.op(lambda e: e.scalar_tensor_tensor(X[:, m, :], FX[:, m, :], f4[:, m:m + 1], XL[:, m, :],
                                                      ALU.mult, ALU.add), t, tx)
            yield

        def run(*gens):
            parts = [[g, n, 0] for g, n in gens]
            while parts:
                p = min(parts, key=lambda p: p[2] / p[1])
                cost = next(p[0], p)
                if cost is p:
                    parts.remove(p)
                else:
                    p[2] += cost or 1

        run((pass1(), 196), (edge_logits(), 98), (mixer0(), 290))
        barrier()

        def softmax(z, ex, dst, ar, heads, tok):
            same = ar.get(C)
            pf = ar.get(C)
            pb = ar.get(C)
            fw = ar.get(C)
            bw = ar.get(C)
            uu = ar.get(C)
            row = ar.get(8, 128)
            col = ar.get(8)
            cols = ar.get(2)
            tk = V.op(lambda e: e.tensor_tensor(same[:, 1:C], dst[:, 1:C], dst[:, 0:C - 1], ALU.not_equal), tok)
            V.op(lambda e: e.memset(pf[:, 0:1], -BIG))
            V.op(lambda e: e.memset(pb[:, C - 1:C], -BIG))
            V.op(lambda e: e.tensor_scalar(pf[:, 1:C], same[:, 1:C], -BIG, None, ALU.mult), tk)
            tpb = V.op(lambda e: e.tensor_scalar(pb[:, 0:C - 1], same[:, 1:C], -BIG, None, ALU.mult))
            cat = bank[0]
            T.op(lambda e: e.transpose(cat[0:1, 0:128], dst[:, 0:1], ident), tok)
            tt1 = T.op(lambda e: e.transpose(cat[0:1, 128:256], dst[:, C - 1:C], ident))
            fd, ld, df, db, ca, cb, wk = (row[0:1, i, :] for i in range(7))
            wide = lambda i: row[0:1, i, :]
            t = V.chain([
                lambda e: e.tensor_copy(fd, cat[0:1, 0:128]),
                lambda e: e.tensor_copy(ld, cat[0:1, 128:256]),
                lambda e: e.tensor_tensor(wk, fd, ld, ALU.not_equal),
                lambda e: e.tensor_tensor(ca[:, 1:128], fd[:, 1:128], ld[:, 0:127], ALU.not_equal),
                lambda e: e.memset(ca[:, 0:1], 1.0),
                lambda e: e.tensor_copy(cb[:, 0:127], ca[:, 1:128]),
                lambda e: e.memset(cb[:, 127:128], 1.0),
                lambda e: e.tensor_tensor(df, wk, ca, ALU.add),
                lambda e: e.tensor_tensor(db, wk, cb, ALU.add),
                lambda e: e.tensor_scalar(df, df, -BIG, None, ALU.mult),
                lambda e: e.tensor_scalar(db, db, -BIG, None, ALU.mult),
                lambda e: e.tensor_scalar(ca, ca, -BIG, None, ALU.mult),
                lambda e: e.tensor_scalar(cb, cb, -BIG, None, ALU.mult),
            ], tt1)
            tlast = None
            for h in range(heads):
                zh, eh = z(h), ex(h)
                t1 = V.op(lambda e, zh=zh: e.tensor_tensor_scan(fw, pf, zh, 0.0, ALU.add, ALU.max), t, tpb, tlast)
                t2 = V.op(lambda e, zh=zh: e.tensor_tensor_scan(bw[:, ::-1], pb[:, ::-1], zh[:, ::-1], 0.0, ALU.add,
                                                                ALU.max))
                T.op(lambda e: e.transpose(cat[0:1, 0:128], fw[:, C - 1:C], ident), t1, t)
                tp = T.op(lambda e: e.transpose(cat[0:1, 128:256], bw[:, 0:1], ident), t2)
                sf, sb_ = wide(6), wide(7)
                tv = V.chain([
                    lambda e: e.tensor_tensor_scan(sf, df, cat[0:1, 0:128], 0.0, ALU.add, ALU.max),
                    lambda e: e.tensor_tensor_scan(sb_[:, ::-1], db[:, ::-1], cat[0:1, 128:256][:, ::-1], 0.0, ALU.add,
                                                   ALU.max),
                    lambda e: e.tensor_tensor(fd[:, 1:128], sf[:, 0:127], ca[:, 1:128], ALU.add),
                    lambda e: e.memset(fd[:, 0:1], -BIG),
                    lambda e: e.tensor_tensor(ld[:, 0:127], sb_[:, 1:128], cb[:, 0:127], ALU.add),
                    lambda e: e.memset(ld[:, 127:128], -BIG),
                ], tp)
                T.op(lambda e: e.matmul(bank[1][:, 0:1], fd, ones[0:1, 0:1], start=True, stop=True), tv)
                tm = T.op(lambda e: e.matmul(bank[1][:, 1:2], ld, ones[0:1, 0:1], start=True, stop=True))
                tv = V.chain([
                    lambda e: e.tensor_copy(cols, bank[1][:, 0:2]),
                    lambda e: e.tensor_tensor(fw, fw, bw, ALU.max),
                    lambda e: e.tensor_scalar(uu, dst, dst[:, 0:1], -BIG, ALU.not_equal, ALU.mult),
                    lambda e: e.scalar_tensor_tensor(fw, uu, cols[:, 0:1], fw, ALU.add, ALU.max),
                    lambda e: e.tensor_scalar(uu, dst, dst[:, C - 1:C], -BIG, ALU.not_equal, ALU.mult),
                    lambda e: e.scalar_tensor_tensor(fw, uu, cols[:, 1:2], fw, ALU.add, ALU.max),
                    lambda e, zh=zh: e.tensor_tensor(fw, zh, fw, ALU.subtract),
                ], tm)
                tlast = A.op(lambda e, eh=eh: e.activation(eh, fw, ACT.Exp), tv)
            return tlast

        s3 = Arena(BASE + NT * D)
        zero = s3.get(D)
        chan().dma(A, xs_d.rearrange("(s p) d -> p s d", p=128), bc(zero, 1, MS // 128),
                   G.op(lambda e: e.memset(zero, 0.0)))
        rec0 = s3.get(C, 2)
        aa = s3.get(C)
        zz = s3.get(C)
        t = V.chain([
            lambda e: e.tensor_tensor(zz, Pt, tt, ALU.add),
            lambda e: e.tensor_scalar(zz, zz, wB[:, 128:129], None, ALU.add),
            lambda e: e.tensor_scalar(aa, zz, 0.01, None, ALU.mult),
            lambda e: e.tensor_tensor(aa, aa, zz, ALU.max),
            lambda e: e.tensor_copy(rec0[:, :, 0], dstF),
        ])
        tx = softmax(lambda h: aa, lambda h: rec0[:, :, 1], dstF, s3, 1, t)
        c_r = chan()
        trec = c_r.dma(S, rec0_d.rearrange("(p c) f -> p c f", p=128), rec0, tx, t)
        barrier()
        c_rid, c_rids = chan(), chan()
        rid_v = rid_d.rearrange("(p s) a -> p (s a)", p=128)
        G.wait(c_rid.dma(A, rid_v, rid))
        for t in range(NT):
            c_rids.n += 16
            G.do(lambda e: e.indirect_dma_start(
                out=rid_d, out_offset=bass.IndirectOffsetOnAxis(ap=tsrI[:, t:t + 1], axis=0),
                in_=nid[:, 0, t:t + 1], in_offset=None).then_inc(c_rids.sem, 16))
        c_rid.dma(A, rid, rid_v, c_rids.now)

        def steps(acc, rows, rec, width, nrec, make, ar, tz, by_step):
            nb = 4
            rbuf = [ar.get(4, width) for _ in range(nb)]
            qbuf = [ar.get(4, nrec) for _ in range(nb)]
            mbuf = [ar.get(4, P) for _ in range(3)]
            dl = [ar.get(4) for _ in range(3)]
            rr, rq, rm, rdl = Ring(rbuf), Ring(qbuf), Ring(mbuf), Ring(dl)
            rp = Ring(bank[0:4])
            cr = [chan() for _ in range(nb)]
            r_v = rows.rearrange("(t p i) d -> t p (i d)", p=128, i=4)
            q_v = rec.rearrange("(t p i) f -> t p (i f)", p=128, i=4)
            last = tz
            LAG = 2
            pend = {}

            def add(g):
                ps, w, tm, ip = pend.pop(g)
                reg = V.engine.value_load(REG[0:1, 0, g:g + 1], min_val=0, max_val=NT - 1)
                a = acc[:, bass.ds(reg, 1), 0:w].rearrange("p a c -> p (a c)")
                rp.free[ip] = V.op(lambda e: e.tensor_tensor(a, a, ps[0:P, 0:w], ALU.add), tm, last)
                return rp.free[ip]

            for g in range(NS):
                i, rb_, fr = rr.take()
                _, qb_, _ = rq.take()
                S.wait(fr)
                cr[i].n += 32

                def load(e, g=g, rb_=rb_, qb_=qb_, s=cr[i].sem):
                    t = e.value_load(REG[0:1, 1, g:g + 1], min_val=0, max_val=NTI - 1)
                    src = r_v[g] if by_step else r_v[bass.ds(t, 1), :, :].rearrange("a p c -> (a p) c")
                    e.dma_start(rb_.rearrange("p i d -> p (i d)"), src).then_inc(s, 16)
                    e.dma_start(qb_.rearrange("p i f -> p (i f)"),
                                q_v[bass.ds(t, 1), :, :].rearrange("a p c -> (a p) c")).then_inc(s, 16)
                S.do(load)
                tin = cr[i].now
                im, M, fm = rm.take()
                _, dd, _ = rdl.take()
                td = V.op(lambda e, g=g, dd=dd, qb_=qb_: e.tensor_scalar(dd, qb_[:, :, 0], JV[:, g:g + 1], None,
                                                                            ALU.subtract), tin, fm)
                lhs, rhs, tv = make(M, dd, rb_, qb_, td, tin)
                ip, ps, fp = rp.take()
                T.wait(tv, tin, fp)
                for k in range(4):
                    tm = T.op(lambda e, k=k, ps=ps, lhs=lhs, rhs=rhs: e.matmul(ps[0:P, 0:rhs(k).shape[-1]], lhs[:, k, :],
                                                                               rhs(k), start=k == 0, stop=k == 3))
                rm.free[im] = tm
                rr.free[i] = tm
                pend[g] = (ps, rhs(0).shape[-1], tm, ip)
                if g >= LAG:
                    last = add(g - LAG)
            for g in range(NS - LAG, NS):
                last = add(g)
            return last

        s3 = Arena(BASE)
        Y = s3.get(NT, D, parts=P)
        acc0 = s3.get(NT, RW, parts=P)
        tz = V.op(lambda e: e.memset(acc0, 0.0))

        def make0(M, dd, rb_, qb_, td, tin):
            for k in range(4):
                tv = V.op(lambda e, k=k: e.tensor_scalar(M[:, k, :], iota[:, 0:P], dd[:, k:k + 1], qb_[:, k, 1:2],
                                                         ALU.is_equal, ALU.mult), td)
            return M, (lambda k: rb_[:, k, 0:D + 1]), tv

        last = steps(acc0, hs_d, rec0_d, RW, 2, make0, s3, tz, False)
        den = s3.get(NT, parts=P)
        t = V.chain([
            lambda e: e.tensor_scalar(den, acc0[:, :, D], 1e-16, None, ALU.add),
            lambda e: e.reciprocal(den, den),
        ], last)

        def join(m):
            t1 = V.op(lambda e: e.tensor_scalar(acc0[:, m, 0:D], acc0[:, m, 0:D], den[:, m:m + 1], 0.0, ALU.mult, ALU.max), t)
            return V.op(lambda e: e.tensor_tensor(X[:, m, :], X[:, m, :], acc0[:, m, 0:D], ALU.add), t1)

        ty = ln_pipe(Y, X, 1e-5, join)

        def experts(ar, NE, y, ty, base, wall, b2, gw, gb, func, weighted, finish, between=None):
            nsl = (2 * N + NE * 127) // 128
            acc = ar.get(NT, D, parts=P)
            wb_ = [ar.get(WROW) for _ in range(4)]
            xb = [ar.get(2, D) for _ in range(4)]
            xTb = [ar.get(2, 128) for _ in range(2)]
            hTb = [ar.get(4, 128) for _ in range(2)]
            yb = [ar.get(D) for _ in range(16)]
            ride = ar.get(nsl, dt=I32)
            spare = ar.get(nsl)
            sr = ar.get(2, NT, parts=P)
            hf = ar.get(2, NT, parts=P)
            srI = ar.get(2, NT, parts=P, dt=I32)
            gb_ = [ar.get(2, D, parts=P) for _ in range(4)]
            yTb = [ar.get(2, P) for _ in range(3)]
            b2r = ar.get(D)
            gwc = ar.get(2, NE)
            gbB = ar.get(NE)
            lg = ar.get(NT, NE, parts=P)
            gate = ar.get(NT, NE, parts=P)
            oh1 = ar.get(NT, NE, parts=P)
            oh2 = ar.get(NT, NE, parts=P)
            cm = ar.get(NT, NE, parts=P)
            mx = ar.get(NT, 8, parts=P)
            mi = ar.get(NT, 8, parts=P, dt=U32)
            mf = ar.get(NT, 8, parts=P)
            wa = ar.get(NT, parts=P)
            wb = ar.get(NT, parts=P)
            sl = ar.get(2, NT, parts=P)
            slI = ar.get(2, NT, parts=P, dt=I32)
            esI = ar.get(nsl, parts=P, dt=I32)
            gTb = [ar.get(P) for _ in range(3)]
            cs = chan()
            cs.dma(A, b2r[0:NE, :], b2)
            cs.dma(A, gwc, gw.rearrange("(k p) n -> p k n", p=128))
            cs.dma(A, gbB, rowb(gb, 0, NE))
            tk = V.op(lambda e: e.tensor_scalar(spare, ones[:, 0:nsl], pid, float(nsl), ALU.mult, ALU.mult))
            tk = V.op(lambda e: e.tensor_tensor(spare, spare, iota[:, 0:nsl], ALU.add), tk)
            tk = V.op(lambda e: e.tensor_scalar(ride, spare, float(2 * N), None, ALU.add), tk)
            rie_v = rie_d[0:128 * nsl, :].rearrange("(p s) a -> p (s a)", p=128)
            cri, cris = chan(), chan()
            tri_ = cri.dma(A, rie_v, ride, tk)
            rt = Ring(bank[0:2])
            ry = Ring(yTb)
            yTs = {}

            def turn_y(t):
                i, b, f = rt.take()
                for k in range(2):
                    tp = T.op(lambda e: e.transpose(b[:, k * P:(k + 1) * P], y[:, t, 128 * k:128 * k + 128],
                                                    ident[0:P, 0:P]), f, ty[t])
                iy, yT, fy = ry.take()
                rt.free[i] = ta = A.op(lambda e: e.activation(
                    yT, b[:, 0:2 * P].rearrange("p (k n) -> p k n", k=2), ACT.Copy), tp, fy)
                yTs[t] = (iy, yT, ta)

            turn_y(0)
            for t in range(NT):
                if t + 1 < NT:
                    turn_y(t + 1)
                iy, yT, ta = yTs.pop(t)
                for k in range(2):
                    tm = T.op(lambda e: e.matmul(bank[2][0:P, NE * t:NE * t + NE], yT[:, k, :], gwc[:, k, :],
                                                 start=k == 0, stop=k == 1), ta, cs.now)
                ry.free[iy] = tm
            tk = V.op(lambda e: e.tensor_tensor(lg, bank[2][0:P, 0:NT * NE].rearrange("p (t n) -> p t n", n=NE),
                                                bc(gbB[0:P, :], 1, NT), ALU.add), tm, cs.now)
            for t in range(NT):
                tk1 = V.op(lambda e, t=t: e.max(mx[:, t, :], lg[:, t, :]), tk)
            for t in range(NT):
                tk1 = V.op(lambda e, t=t: e.max_index(mi[:, t, :], mx[:, t, :], lg[:, t, :]), tk1)
            io = bc(iota[0:P, 0:NE], 1, NT)
            tc = V.chain([
                lambda e: e.tensor_copy(mf, mi),
                lambda e: e.tensor_tensor(oh1, io, bc(mf[:, :, 0], 2, NE), ALU.is_equal),
                lambda e: e.tensor_tensor(oh2, io, bc(mf[:, :, 1], 2, NE), ALU.is_equal),
                lambda e: e.tensor_tensor(cm, oh1, oh2, ALU.add),
            ], tk1)
            slot, ts = slots(ar, cm.rearrange("p t e -> p e t"), NE, nsl, esI, tc)
            tl = V.chain([
                lambda e: e.tensor_tensor(cm, slot.rearrange("p e t -> p t e"), oh1, ALU.mult),
                lambda e: e.tensor_reduce(sl[:, 0, :], cm, X_AX, ALU.add),
                lambda e: e.tensor_tensor(cm, slot.rearrange("p e t -> p t e"), oh2, ALU.mult),
                lambda e: e.tensor_reduce(sl[:, 1, :], cm, X_AX, ALU.add),
                lambda e: e.tensor_copy(slI, sl),
            ], ts)
            tsr = V.chain([
                lambda e: e.tensor_scalar(srI, slI, 7, None, ALU.arith_shift_right),
                lambda e: e.tensor_copy(hf, srI),
                lambda e: e.scalar_tensor_tensor(sr, hf, -128.0, sl, ALU.mult, ALU.add),
                lambda e: e.scalar_tensor_tensor(sr, sr, float(nsl), hf, ALU.mult, ALU.add),
                lambda e: e.tensor_copy(srI, sr),
            ], tl)
            csc = chan()
            G.wait(tl, ty)
            for t in range(NT):
                for k in range(2):
                    csc.n += 16
                    G.do(lambda e, t=t, k=k: e.indirect_dma_start(
                        out=xs_d, out_offset=bass.IndirectOffsetOnAxis(ap=slI[:, k, t:t + 1], axis=0),
                        in_=y[:, t, :], in_offset=None).then_inc(csc.sem, 16))
            tsc = csc.now
            G.wait(tsr, tri_)
            for t in range(NT):
                for k in range(2):
                    cris.n += 16
                    G.do(lambda e: e.indirect_dma_start(
                        out=rie_d[0:128 * nsl, :], out_offset=bass.IndirectOffsetOnAxis(ap=srI[:, k, t:t + 1], axis=0),
                        in_=nid[:, k, t:t + 1], in_offset=None).then_inc(cris.sem, 16))
            tg = tl
            if weighted:
                tk = V.op(lambda e: e.tensor_tensor(wb, mx[:, :, 1], mx[:, :, 0], ALU.subtract), tl)
                tk = A.op(lambda e: e.activation(wb, wb, ACT.Exp), tk)
                tg = V.chain([
                    lambda e: e.tensor_scalar(wa, wb, 1.0, None, ALU.add),
                    lambda e: e.reciprocal(wa, wa),
                    lambda e: e.tensor_tensor(wb, wb, wa, ALU.mult),
                    lambda e: e.tensor_tensor(oh1, oh1, bc(wa, 2, NE), ALU.mult),
                    lambda e: e.tensor_tensor(oh2, oh2, bc(wb, 2, NE), ALU.mult),
                ], tk)
            tg = V.op(lambda e: e.tensor_tensor(gate, oh1, oh2, ALU.add), tg)
            rg2 = Ring(bank[5:8])
            rgt = Ring(gTb)
            gts = {}

            def turn_g(t):
                i, b, f = rg2.take()
                ig, gt, fg = rgt.take()
                tp = T.op(lambda e: e.transpose(b[0:NE, 0:P], gate[:, t, :], ident[0:P, 0:P]), tg, f)
                rg2.free[i] = A.op(lambda e: e.activation(gt[0:NE, :], b[0:NE, 0:P], ACT.Copy), tp, fg)
                gts[t] = (ig, gt, rg2.free[i])

            turn_g(0)
            for t in range(NT):
                if t + 1 < NT:
                    turn_g(t + 1)
                ig, gt, ta = gts.pop(t)
                i, b, f = rg2.take()
                rgt.free[ig] = tm = T.op(lambda e: e.matmul(b[0:P, 0:D], gt[0:NE, :], b2r[0:NE, :], start=True, stop=True),
                                         ta, f, cs.now)
                rg2.free[i] = tacc = V.op(lambda e: e.tensor_tensor(acc[:, t, :], b[0:P, 0:D], base[:, t, :], ALU.add), tm, ty)
            rw, rx, rxT, rh, ryb = Ring(wb_), Ring(xb), Ring(xTb), Ring(hTb), Ring(yb)
            cw = [chan() for _ in wb_]
            cx = [chan() for _ in xb]
            cy = [chan() for _ in yb]
            rbt, rb1, rb2 = Ring(bank[0:2]), Ring(bank[2:5]), Ring(bank[5:8])
            rbt.free = [T.now, T.now]
            rb1.free = [T.now, ts, tl]
            rb2.free = rg2.free
            xs_v = xs_d[0:128 * nsl, :].rearrange("(s p) d -> p s d", p=128)
            S.wait(ts)
            xt, wt, got, done = {}, {}, {}, {}

            def fetch(s):
                i, w, f = rw.take()
                S.wait(f)
                reg = S.engine.value_load(esI[0:1, s:s + 1], min_val=0, max_val=NE - 1)
                wt[s] = (i, w, cw[i].dma(S, w, wall[bass.ds(reg, 1), :, :].rearrange("a p c -> (a p) c")))

            def rows(s):
                i, x_, f = rx.take()
                n = min(2, nsl - s)
                got[s] = got[s + 1] = (i, x_, cx[i].dma(S, x_[:, 0:n, :], xs_v[:, s:s + n, :], f, tsc))

            def turn(s):
                i, x_, tin = got.pop(s)
                ib, b, f = rbt.take()
                for k in range(2):
                    tp = T.op(lambda e: e.transpose(b[:, 128 * k:128 * k + 128], x_[:, s % 2, 128 * k:128 * k + 128], ident),
                              tin, f)
                rx.free[i] = tp
                it, x_T, ft = rxT.take()
                rbt.free[ib] = tv = V.op(lambda e: e.tensor_copy(x_T, b[:, 0:256].rearrange("p (k n) -> p k n", k=2)), tp, ft)
                xt[s] = (it, x_T, tv)

            def first(s):
                it, x_T, tv = xt.pop(s)
                iw, w, tw = wt[s]
                ib, b, f = rb1.take()
                ih, h, fh = rh.take()
                for c in range(4):
                    for q in range(2):
                        tm = T.op(lambda e: e.matmul(b[:, 128 * c:128 * c + 128], w[:, 512 * q + 128 * c:512 * q + 128 * c + 128],
                                                     x_T[:, q, :], start=q == 0, stop=q == 1), tv, tw, f)
                rxT.free[it] = tm
                for c in range(4):
                    ta = A.op(lambda e: e.activation(h[:, c, :], b[:, 128 * c:128 * c + 128], func,
                                                     bias=w[:, 2048 + c:2049 + c]), tm, fh)
                rb1.free[ib] = ta
                return ih, h, ta

            def second(s, ih, h, ta):
                iw, w, tw = wt.pop(s)
                ib, b, f = rb2.take()
                for c in range(4):
                    tm = T.op(lambda e: e.matmul(b[:, 0:D], h[:, c, :], w[:, 1024 + D * c:1024 + D * c + D], start=c == 0,
                                                 stop=c == 3), ta, f)
                rh.free[ih] = rw.free[iw] = tm
                iy, o, fy = ryb.take()
                rb2.free[ib] = tv = V.op(lambda e: e.tensor_copy(o, b[:, 0:D]), tm, fy)
                done[s] = (iy, o, tv)

            def store(s):
                iy, o, tv = done.pop(s)
                G.wait(tv, trd)
                cy[iy].n += 16
                G.do(lambda e: e.indirect_dma_start(
                    out=ys_d, out_offset=bass.IndirectOffsetOnAxis(ap=ride[:, s:s + 1], axis=0),
                    in_=o, in_offset=None).then_inc(cy[iy].sem, 16))
                ryb.free[iy] = cy[iy].now

            for s in range(3):
                fetch(s)
            rows(0)
            rows(2)
            turn(0)
            late = None
            for s in range(nsl):
                if s == 13:
                    trd = cri.dma(S, ride, rie_v, cris.now)
                    for k in range(s - 2):
                        store(k)
                if s >= 13:
                    store(s - 2)
                if s % 2 == 0 and s + 4 < nsl:
                    rows(s + 4)
                if s + 1 < nsl:
                    turn(s + 1)
                now = first(s)
                if late:
                    second(s - 1, *late)
                if s + 3 < nsl:
                    fetch(s + 3)
                late = now
            second(nsl - 1, *late)
            store(nsl - 2)
            store(nsl - 1)
            if between:
                between()
            rg = Ring(gb_)
            cg = [chan() for _ in gb_]
            ys_v = ys_d[0:2 * N, :].rearrange("(k t p) d -> t p k d", k=2, p=P)
            S.wait(ryb.free)
            for t in range(NT):
                i, g, f = rg.take()
                cg[i].dma125(S, g, ys_v[t], f)
                tv = tacc
                for k, wk in ((0, wa), (1, wb)):
                    if weighted:
                        tv = V.op(lambda e: e.scalar_tensor_tensor(acc[:, t, :], g[:, k, :], wk[:, t:t + 1], acc[:, t, :],
                                                                   ALU.mult, ALU.add), cg[i].now, tv, tg)
                    else:
                        tv = V.op(lambda e: e.tensor_tensor(acc[:, t, :], acc[:, t, :], g[:, k, :], ALU.add), cg[i].now, tv)
                rg.free[i] = tv
                if t % 5 == 4:
                    finish(t // 5, acc, tv)

        barrier()
        f0 = Arena(BASE + NT * D)
        gam = f0.get(D)
        bet = f0.get(D)
        c_f = chan()
        c_f.dma(A, gam, rowb(I["f0_gamma"], 0, D))
        c_f.dma(A, bet, rowb(I["f0_beta"], 0, D))
        high = Arena(WIDE - 4160)
        RA = [high.get(2, 1024) for _ in range(2)]
        priB = high.get(32)
        c_l = chan()
        tz = [G.op(lambda e, m=m: e.memset(RA[m], 0.0)) for m in range(2)][-1]
        for m, name in enumerate(("att", "msg")):
            for h in range(4):
                hc, i = h // 2, h % 2
                c_l.dma(S, RA[m][64 * i:64 * i + 64, hc, :].rearrange("p (r o) -> p r o", r=8)[:, :, 64 * i:64 * i + 64],
                        I[name][h], tz)
        c_l.dma(S, priB, rowb(I["pri"], 0, 32))
        LWAT = BASE + NT * D + C + NT * 3 * D // 2
        LW = [mem[:, LWAT + 2048 * k:LWAT + 2048 * k + 2048].rearrange("p (k n) -> p k n", k=2) for k in range(3)]

        def early_weights():
            for m, name in enumerate(("k_lin", "q_lin", "v_lin")):
                for kc in range(2):
                    c_l.dma(S, LW[m][:, kc, :].rearrange("p (t n) -> p t n", t=4),
                            I[name][:, 128 * kc:128 * kc + 128, :].rearrange("t p n -> p t n"), T.now, A.now)

        first, second = {}, {}
        tyl = []

        def out0(k, acc):
            g, a, b = GRP[k], GRP[k][0], GRP[k][-1] + 1
            tk = V.op(lambda e: e.reciprocal(rstd[:, a:b], rstd[:, a:b]), first.pop(k))
            for t in g:
                t1 = V.op(lambda e: e.scalar_tensor_tensor(acc[:, t, :], acc[:, t, :], mv[:, t, 0:1], gam[0:P, :],
                                                           ALU.subtract, ALU.mult), tk, c_f.now)
                t1 = V.op(lambda e: e.scalar_tensor_tensor(acc[:, t, :], acc[:, t, :], rstd[:, t:t + 1], bet[0:P, :],
                                                           ALU.mult, ALU.add), t1)
                t1 = V.op(lambda e: e.tensor_tensor(X[:, t, :], X[:, t, :], acc[:, t, :], ALU.add), t1)
            second[k] = ln_begin(g, X, 1e-5, t1)

        def finish0(k, acc, tok):
            first[k] = ln_begin(GRP[k], acc, 1e-5, tok)
            if k >= 1:
                out0(k - 1, acc)
            if k >= 2:
                tyl.extend(ln_end(GRP[k - 2], Y, X, second.pop(k - 2)))
            if k == len(GRP) - 1:
                out0(k, acc)
                tyl.extend(ln_end(GRP[k - 1], Y, X, second.pop(k - 1)))
                tyl.extend(ln_end(GRP[k], Y, X, second.pop(k)))

        experts(f0, 16, Y, ty, Y, I["f0_w"], I["f0_b2"], I["f0_gw"], I["f0_gb"], ACT.Relu, True, finish0,
                early_weights)
        assert f0.at <= WIDE - 4160
        csc = chan()
        for t in range(NT):
            csc.n += 16
            G.wait(tyl[t])
            G.do(lambda e: e.indirect_dma_start(
                out=xs_d, out_offset=bass.IndirectOffsetOnAxis(ap=tslI[:, t:t + 1], axis=0),
                in_=Y[:, t, :], in_offset=None).then_inc(csc.sem, 16))
        tsc = csc.now
        barrier()

        g1 = Arena(BASE)
        XN = g1.get(NT, D, parts=P)
        dstF = g1.get(C)
        Q3 = g1.get(NT * 3 * D // 2, parts=P, dt=BF16).rearrange("p (t s d) -> p t s d", s=3, d=D)
        g1_own = g1.at
        s5 = Arena(LWAT + 3 * 2048)
        assert g1.at == LWAT
        etI = s5.get(C, dt=I32)
        kvI = etI
        dst2 = [s5.get(C // 2, dt=BF16) for _ in range(2)]
        rest = [s5.get(D) for _ in range(2)]
        KVo = [s5.get(8, 512) for _ in range(2)]
        early = Arena(s5.at - 4096)
        srcI = early.get(C, dt=I32)
        dstI = early.get(C, dt=I32)
        f1_, f2_ = early.get(C), early.get(C)
        c_5 = chan()
        c_5.dma(S, srcI, I["src"])
        c_5.dma(S, dstI, I["dst"])
        c_5.dma(S, etI, I["etype"])
        tk = V.op(lambda e: e.tensor_scalar(priB, priB, 0.125, None, ALU.mult), c_l.now)
        for hc in range(2):
            tk = V.op(lambda e, hc=hc: e.tensor_tensor(
                RA[0][:, hc, :].rearrange("p (r i d) -> p r i d", r=8, i=2),
                RA[0][:, hc, :].rearrange("p (r i d) -> p r i d", r=8, i=2),
                bc(priB.rearrange("p (r h i) -> p r h i", r=8, h=2)[:, :, hc, :], 3, 64), ALU.mult), tk)
        tra = tk
        V.chain([
            lambda e: e.tensor_copy(dstF, dstI),
            lambda e: e.tensor_copy(f1_, srcI),
            lambda e: e.tensor_copy(f2_, etI),
            lambda e: e.scalar_tensor_tensor(f2_, f1_, 8.0, f2_, ALU.mult, ALU.add),
            lambda e: e.tensor_copy(kvI, f2_),
            lambda e: e.tensor_scalar(dstI, dstI, 5, None, ALU.arith_shift_right),
            lambda e: e.tensor_copy(f1_, dstI),
            lambda e: e.tensor_scalar(f1_, f1_, 32.0, None, ALU.mult),
            lambda e: e.tensor_copy(dst2[0], f1_),
            lambda e: e.tensor_tensor(f1_, dstF, f1_, ALU.subtract),
            lambda e: e.tensor_copy(dst2[1], f1_),
        ], c_5.now)
        tmk = V.now
        c_i = chan()
        c_i.dma(S, kvi_d.rearrange("(p c) a -> p (c a)", p=128), kvI, tmk)
        for k in range(2):
            c_i.dma(S, dst_d[k].rearrange("(p c) -> p c", p=128), dst2[k], tmk)
        xb = [s5.get(2, D) for _ in range(3)]
        XTb = [s5.get(2, 128) for _ in range(2)]
        kvr = [s5.get(512) for _ in range(2)]
        qo = [s5.get(3 * D // 2, dt=BF16).rearrange("p (s d) -> p s d", s=3) for _ in range(2)]
        KTb = [s5.get(4, 128) for _ in range(2)]
        rxb, rx, rkv, rqo, rk, ro, rr = Ring(xb), Ring(XTb), Ring(kvr), Ring(qo), Ring(KTb), Ring(KVo), Ring(rest)
        ro_ps = Ring([b[:, :] for b in bank[4:8]])
        cx = [chan() for _ in xb]
        c_kv = [chan() for _ in KVo]
        c_q = [chan() for _ in qo]
        xs_v = xs_d[0:128 * NTS, :].rearrange("(s p) d -> p s d", p=128)
        kv_v = kv_d.rearrange("(n r) d -> n (r d)", r=8)
        LWv = [w.rearrange("p k (t n) -> p k t n", t=4) for w in LW]
        got, xts, kvs, kts = {}, {}, {}, {}
        ft = fkv = fq = fkt = None

        def rows(s):
            i, x_, f = rxb.take()
            n = min(2, NTS - s)
            got[s] = got[s + 1] = (i, x_, cx[i].dma(S, x_[:, 0:n, :], xs_v[:, s:s + n, :], f, tsc))

        def turn(s):
            nonlocal ft
            i, x_, tin = got.pop(s)
            for k in range(2):
                tp = T.op(lambda e: e.transpose(bank[0][:, 128 * k:128 * k + 128], x_[:, s % 2, 128 * k:128 * k + 128], ident),
                          tin, ft)
            rxb.free[i] = tp
            ix, xt, fx = rx.take()
            ft = A.op(lambda e: e.activation(xt, bank[0][:, 0:256].rearrange("p (k n) -> p k n", k=2), ACT.Copy), tp, fx)
            xts[s] = (ix, xt, ft)

        def typed(s):
            nonlocal fkv, fq
            ix, xt, ta = xts.pop(s)
            tau = T.engine.value_load(tauI[0:1, s:s + 1], min_val=0, max_val=3)
            for m, ps, f in ((0, bank[1][:, 0:D], fkv), (2, bank[1][:, D:2 * D], fkv), (1, bank[2][:, 0:D], fq)):
                for k in range(2):
                    tm = T.op(lambda e: e.matmul(ps, xt[:, k, :], LWv[m][:, k, bass.ds(tau, 1), :].rearrange("p a n -> p (a n)"),
                                                 start=k == 0, stop=k == 1), ta, f, c_l.now)
                if m == 2:
                    tkv = tm
            rx.free[ix] = tm
            ik, kv, fk = rkv.take()
            fkv = V.op(lambda e: e.tensor_copy(kv, bank[1][:, :]), tkv, fk)
            kvs[s] = (ik, kv, fkv)
            iq, o, fo = rqo.take()
            ir, r_, fr = rr.take()
            t1 = A.op(lambda e: e.activation(o[:, 0, :], bank[2][:, 0:D], ACT.Copy), tm, fo)
            fq = t1 = V.op(lambda e: e.tensor_tensor(r_, bank[2][:, 0:D], o[:, 0, :], ALU.subtract), t1, fr)
            t1 = A.op(lambda e: e.activation(o[:, 1, :], r_, ACT.Copy), t1)
            t1 = rr.free[ir] = V.op(lambda e: e.tensor_tensor(o[:, 2, :], r_, o[:, 1, :], ALU.subtract), t1)
            G.wait(t1)
            c_q[iq].n += 16
            G.do(lambda e: e.indirect_dma_start(
                out=q3_d, out_offset=bass.IndirectOffsetOnAxis(ap=rid[:, s:s + 1], axis=0),
                in_=o.rearrange("p s d -> p (s d)"), in_offset=None).then_inc(c_q[iq].sem, 16))
            rqo.free[iq] = c_q[iq].now

        def turn2(s):
            nonlocal fkt
            ik, kv, tkv = kvs.pop(s)
            for c in range(4):
                tp = T.op(lambda e: e.transpose(bank[3][:, 128 * c:128 * c + 128], kv[:, 128 * c:128 * c + 128], ident), tkv, fkt)
            rkv.free[ik] = tp
            it, kt, f = rk.take()
            fkt = A.op(lambda e: e.activation(kt, bank[3][:, :].rearrange("p (k n) -> p k n", k=4), ACT.Copy), tp, f)
            kts[s] = (it, kt, fkt)

        def relate(s):
            it, kt, ta = kts.pop(s)
            io, ko, fo = ro.take()
            tev = []
            for m in range(2):
                for hc in range(2):
                    for half in range(2):
                        im, ps, fm = ro_ps.take()
                        tm = T.op(lambda e: e.matmul(ps, kt[:, 2 * m + hc, :], RA[m][:, hc, 512 * half:512 * half + 512],
                                                     start=True, stop=True), ta, fm, tra)
                        dst_ = ko[:, 4 * half:4 * half + 4, 256 * m + 128 * hc:256 * m + 128 * hc + 128]
                        src_ = ps.rearrange("p (r d) -> p r d", r=4)
                        if half == 0:
                            te = A.op(lambda e: e.activation(dst_, src_, ACT.Copy), tm, fo)
                        else:
                            te = V.op(lambda e: e.tensor_copy(dst_, src_), tm, fo)
                        ro_ps.free[im] = te
                        tev.append(te)
            rk.free[it] = tm
            G.wait(tev)
            c_kv[io].n += 16
            G.do(lambda e: e.indirect_dma_start(
                out=kv_v, out_offset=bass.IndirectOffsetOnAxis(ap=rid[:, s:s + 1], axis=0),
                in_=ko.rearrange("p r d -> p (r d)"), in_offset=None).then_inc(c_kv[io].sem, 16))
            ro.free[io] = c_kv[io].now

        rows(0)
        rows(2)
        turn(0)
        typed(0)
        turn(1)
        turn2(0)
        for s in range(NTS):
            if s % 2 == 0 and s + 4 < NTS:
                rows(s + 4)
            if s + 1 < NTS:
                typed(s + 1)
            relate(s)
            if s + 2 < NTS:
                turn(s + 2)
            if s + 1 < NTS:
                turn2(s + 1)
        c_5.dma125(S, Q3, q3_d[0:N, :].rearrange("(t p) (s d) -> p t s d", p=P, s=3), rqo.free)
        barrier()

        s6 = Arena(g1_own)
        kvb = [s6.get(4, 512) for _ in range(4)]
        prod = [s6.get(1024)]
        red = [s6.get(16) for _ in range(2)]
        SCg = s6.get(NS, 16)
        JP = s6.get(NS)
        kib = [s6.get(4, dt=I32) for _ in range(8)]
        drb = [s6.get(256, dt=BF16) for _ in range(4)]
        one2 = s6.get(64, dt=BF16)
        MTb = [s6.get(256, dt=BF16) for _ in range(3)]

        def pass2():
            rk, rp, rr, ri, rd, rmt = Ring(kvb), Ring(prod), Ring(red), Ring(kib), Ring(drb), Ring(MTb)
            ci = [chan() for _ in kib]
            cg = [chan() for _ in kvb]
            cs = [chan() for _ in kvb]
            c_sc = chan()
            kvi_v = kvi_d.rearrange("(t p i) a -> t p (i a)", p=128, i=4)
            dst_v = dst_d.rearrange("k (t e) -> t k e", e=512)
            vs_v = vs_d.rearrange("(g p i) d -> g p i d", p=128, i=4)
            sc_v = sc_d.rearrange("(t p i) h -> t p (i h)", p=128, i=4)
            V.op(lambda e: e.memset(one2, 1.0))
            tjp = V.op(lambda e: e.tensor_scalar(JP, JV, pid, None, ALU.add))
            rbq = Ring(bank[3:7])
            tbs, exs = {}, {}
            fbc = None
            inp, kvs, mts, scs = {}, {}, {}, {}
            tsc = None

            def load(g):
                i, ki, f1 = ri.take()
                i2, dr, f2 = rd.take()
                S.wait(f1, f2)
                t = S.engine.value_load(REG[0:1, 1, g:g + 1], min_val=0, max_val=NTI - 1)
                ci[i].dma(S, ki, kvi_v[bass.ds(t, 1), :, :].rearrange("a p c -> (a p) c"))
                inp[g] = (i, ki, i2, dr, ci[i].dma(S, dr[0:2, :], dst_v[bass.ds(t, 1), :, :].rearrange("a k e -> (a k) e")))

            def spread(g):
                ii, ki, i2, dr, tin = inp[g]
                tbs[g] = rd.free[i2] = T.op(lambda e: e.matmul(bank[7][0:P, :], one2[0:2, 0:P], dr[0:2, :], start=True,
                                                               stop=True), tin, fbc, tjp)

            def expand(g):
                im, M, tM = mts.pop(g)
                j = T.engine.value_load(REG[0:1, 0, g:g + 1], min_val=0, max_val=NT - 1)
                q = [Q3[:, bass.ds(j, 1), x_, :].rearrange("p a d -> p (a d)") for x_ in range(3)]
                Mv = M.rearrange("p (e i) -> p i e", i=4)
                exs[g] = []
                for half in range(2):
                    ib, b, fb = rbq.take()
                    for k in range(2):
                        for x_ in range(3):
                            tm = T.op(lambda e: e.matmul(b[:, D * k:D * k + D], Mv[0:P, 2 * half + k, :], q[x_],
                                                         start=x_ == 0, stop=x_ == 2), tM, fb)
                    exs[g].append((ib, b, tm))
                rmt.free[im] = tm

            def score(g):
                nonlocal tsc
                i, kv, tg = kvs.pop(g)
                rk.free[i] = [cs[i].dma(S, vs_v[g], kv[:, :, D:2 * D], tg)]
                ip, pr, fp = rp.take()
                for half, (ib, b, tm) in enumerate(exs.pop(g)):
                    rbq.free[ib] = tv = V.op(lambda e: e.tensor_tensor(
                        pr[:, 512 * half:512 * half + 512].rearrange("p (c d) -> p c d", c=2), kv[:, 2 * half:2 * half + 2, 0:D],
                        b.rearrange("p (c d) -> p c d", c=2), ALU.mult), tm, tg, fp)
                rk.free[i].append(tv)
                prv = pr.rearrange("p (c d) -> p c d", c=16)
                if g == 0:
                    rp.free[ip] = tsc = V.op(lambda e: e.tensor_reduce(SCg[:, 0, :], prv, X_AX, ALU.add), V.now)
                else:
                    ir, r, fr = rr.take()
                    rp.free[ip] = t1 = V.op(lambda e: e.tensor_reduce(r, prv, X_AX, ALU.add), V.now, fr)
                    rr.free[ir] = tsc = V.op(lambda e: e.scalar_tensor_tensor(
                        SCg[:, g, :], SCg[:, g - 1, :], SAME[:, g:g + 1], r, ALU.mult, ALU.add), t1, tsc)
                scs[g] = tsc

            def store(g):
                t = S.engine.value_load(REG[0:1, 2, g:g + 1], min_val=0, max_val=NTI + NT - 1)
                c_sc.dma(S, sc_v[bass.ds(t, 1), :, :].rearrange("a p c -> (a p) c"), SCg[:, g, :], scs.pop(g))

            for g in range(3):
                load(g)
            spread(0)
            for g in range(NS):
                if g >= 1:
                    expand(g - 1)
                im, M, fm = rmt.take()
                fbc = V.op(lambda e: e.tensor_scalar(M[0:P, :], bank[7][0:P, :], JP[0:P, g:g + 1], None, ALU.is_equal),
                           tbs.pop(g), fm, tjp)
                mts[g] = (im, M, fbc)
                if g + 1 < NS:
                    spread(g + 1)
                ii, ki, i2, dr, tin = inp.pop(g)
                i, kv, f = rk.take()
                G.wait(f, tin)
                for c in range(4):
                    cg[i].n += 16
                    G.do(lambda e: e.indirect_dma_start(
                        out=kv[:, c, :], out_offset=None, in_=kv_d[0:8 * N, :],
                        in_offset=bass.IndirectOffsetOnAxis(ap=ki[:, c:c + 1], axis=0)).then_inc(cg[i].sem, 16))
                ri.free[ii] = cg[i].now
                kvs[g] = (i, kv, cg[i].now)
                if g >= 2:
                    score(g - 2)
                if g >= 4:
                    store(g - 4)
                if g + 3 < NS:
                    load(g + 3)
                yield
            expand(NS - 1)
            for g in range(NS - 2, NS):
                score(g)
            for g in range(NS - 4, NS):
                store(g)
            yield

        def mixer1():
            wq = s6.get(2, 768)
            wo = s6.get(2, D)
            boB = s6.get(D)
            wn1 = s6.get(2)
            wn2 = s6.get(D)
            qph = [s6.get(2, P) for _ in range(2)]
            HM = XN
            x1 = [s6.get(D, parts=P) for _ in range(2)]
            x1T = [s6.get(2, P) for _ in range(2)]
            kph = [s6.get(D, parts=P) for _ in range(2)]
            vv = [s6.get(2, 129, parts=P) for _ in range(2)]
            em = [s6.get(D) for _ in range(2)]
            em2 = [s6.get(D) for _ in range(2)]
            KVm = s6.get(2, 132)
            sso = s6.get(NT, parts=P)
            r1 = s6.get(NT, parts=P)
            zt = [s6.get(2, 4, parts=P) for _ in range(2)]
            oo = [s6.get(D, parts=P) for _ in range(2)]
            oT = [s6.get(2, P) for _ in range(2)]
            jk = s6.get(D, parts=P)
            c_7 = chan()
            c_7.dma(A, wq, I["m1_wqkv"].rearrange("(k p) n -> p k n", p=128))
            c_7.dma(A, wo, I["m1_wout"].rearrange("(k p) n -> p k n", p=128))
            c_7.dma(A, boB, rowb(I["m1_bout"], 0, D))
            c_7.dma(A, wn1, I["m1_wn1"])
            c_7.dma(A, wn2, rowb(I["m1_wn2"], 0, D))

            def rms(src, tok):
                for t in range(NT):
                    a = A.op(lambda e, t=t: e.activation(jk, src[:, t, :], ACT.Square, accum_out=sso[:, t:t + 1]), tok, A.now)
                t_ = V.op(lambda e: e.tensor_scalar(r1, sso, 1.0 / D, 1e-6, ALU.mult, ALU.add), a)
                a = A.op(lambda e: e.activation(r1, r1, ACT.Sqrt), t_)
                return V.op(lambda e: e.reciprocal(r1, r1), a)

            tr = rms(XN, None)
            yield
            tv1 = [V.op(lambda e, b=b: e.memset(b[:, :, 128:129], 1.0)) for b in vv][-1]
            rx, rxt, rkp, rv, re, re2 = Ring(x1), Ring(x1T), Ring(kph), Ring(vv), Ring(em), Ring(em2)
            rb = Ring(bank[0:1])
            fkv = fq = None

            def turned(t):
                ix, x_, fx = rx.take()
                t1 = V.op(lambda e: e.tensor_scalar(x_, XN[:, t, :], r1[:, t:t + 1], None, ALU.mult), tr, fx)
                ib, b, fb = rb.take()
                for k in range(2):
                    tp = T.op(lambda e: e.transpose(b[:, k * P:(k + 1) * P], x_[:, 128 * k:128 * k + 128], ident[0:P, 0:P]),
                              t1, fb)
                rx.free[ix] = tp
                yield
                it, xt, ft = rxt.take()
                for k in range(2):
                    ta = A.op(lambda e: e.activation(xt[:, k, :], b[:, k * P:(k + 1) * P], ACT.Identity,
                                                     scale=wn1[:, k:k + 1]), tp, ft, c_7.now)
                rb.free[ib] = ta
                return it, xt, ta

            for t in range(NT):
                it, xt, ta = yield from turned(t)
                for k in range(2):
                    tm = T.op(lambda e: e.matmul(bank[1][0:P, :], xt[:, k, :], wq[:, k, 256:768],
                                                 start=k == 0, stop=k == 1), ta, fkv, c_7.now)
                rxt.free[it] = tm
                yield
                ie, e1, fe = re.take()
                ta = V.op(lambda e: e.tensor_scalar(e1[0:P, :], bank[1][0:P, 0:D], 0.0, None, ALU.min), tm, fe)
                ta = A.op(lambda e: e.activation(e1[0:P, :], e1[0:P, :], ACT.Exp), ta)
                yield
                ik, kp, fk = rkp.take()
                tk_ = V.op(lambda e: e.scalar_tensor_tensor(kp, bank[1][0:P, 0:D], 0.0, e1[0:P, :], ALU.max, ALU.add), ta, fk)
                re.free[ie] = tk_
                iv, v_, fv = rv.take()
                tvv = A.op(lambda e: e.activation(v_[:, :, 0:128], bank[1][0:P, D:2 * D].rearrange("p (c d) -> p c d", c=2), ACT.Copy), tm, tk_, fv, tv1)
                fkv = [tk_, tvv]
                for c in range(2):
                    tkv = T.op(lambda e: e.matmul(bank[2][:, 129 * c:129 * c + 129], kp[:, 128 * c:128 * c + 128], v_[:, c, :],
                                                  start=t == 0 and c == 0, stop=t == NT - 1 and c == 1), fkv)
                rkp.free[ik] = tkv
                rv.free[iv] = tkv
                yield
            for c in range(2):
                V.op(lambda e: e.tensor_tensor(KVm[:, c, 0:128], bank[2][:, 129 * c:129 * c + 128], blk, ALU.mult), tkv)
                tm_ = V.op(lambda e: e.tensor_scalar(KVm[:, c, 128:132], hm4, bank[2][:, 129 * c + 128:129 * c + 129], None, ALU.mult))
            ro, rot, rz, rqp = Ring(oo), Ring(oT), Ring(zt), Ring(qph)
            fo = fo2 = None
            for t in range(NT):
                it, xt, ta = yield from turned(t)
                for c in range(2):
                    for k in range(2):
                        tm2 = T.op(lambda e: e.matmul(bank[1][:, c * P:(c + 1) * P], wq[:, k, 128 * c:128 * c + 128],
                                                      xt[:, k, :], start=k == 0, stop=k == 1), ta, fo2)
                rxt.free[it] = tm2
                yield
                ie, e2, fe = re2.take()
                ta = V.op(lambda e: e.tensor_scalar(e2[:, 0:2 * P], bank[1][:, 0:2 * P], 0.0, None, ALU.min), tm2, fe)
                ta = A.op(lambda e: e.activation(e2[:, 0:2 * P], e2[:, 0:2 * P], ACT.Exp), ta)
                yield
                iq, qp, fq_ = rqp.take()
                fq = V.op(lambda e: e.scalar_tensor_tensor(
                    qp, bank[1][:, 0:2 * P].rearrange("p (c n) -> p c n", c=2), 0.0,
                    e2[:, 0:2 * P].rearrange("p (c n) -> p c n", c=2), ALU.max, ALU.add), ta, fq_)
                re2.free[ie] = fq
                for c in range(2):
                    tm = T.op(lambda e: e.matmul(bank[2][0:P, 132 * c:132 * c + 132], qp[:, c, :], KVm[:, c, :], start=True,
                                                 stop=True), fq, tm_, fo, fkv)
                rqp.free[iq] = tm
                yield
                pv = bank[2][0:P, 0:264].rearrange("p (c w) -> p c w", c=2)
                iz, z, fz = rz.take()
                io_, o, fo_ = ro.take()
                t1 = V.op(lambda e: e.tensor_scalar(z, pv[:, :, 128:132], 1e-6, None, ALU.add), tm, fz)
                t1 = V.op(lambda e: e.reciprocal(z, z), t1)
                fo = V.op(lambda e: e.tensor_tensor(
                    o.rearrange("p (c h d) -> p c h d", c=2, h=4), pv[:, :, 0:128].rearrange("p c (h d) -> p c h d", h=4),
                    bc(z, 3, 32), ALU.mult), t1, fo_)
                rz.free[iz] = fo
                ib, b, fb = rb.take()
                for k in range(2):
                    tp = T.op(lambda e: e.transpose(b[:, k * P:(k + 1) * P], o[:, 128 * k:128 * k + 128], ident[0:P, 0:P]),
                              fo, fb)
                ro.free[io_] = tp
                yield
                it, ot, ft = rot.take()
                ta = A.op(lambda e: e.activation(ot, b[:, 0:2 * P].rearrange("p (k n) -> p k n", k=2), ACT.Copy), tp, ft)
                rb.free[ib] = ta
                for k in range(2):
                    tm = T.op(lambda e: e.matmul(bank[1][0:P, 256:256 + D], ot[:, k, :], wo[:, k, :], start=k == 0,
                                                 stop=k == 1), ta, fq)
                rot.free[it] = tm
                yield
                fo2 = V.op(lambda e: e.tensor_tensor(HM[:, t, :], HM[:, t, :], bank[1][0:P, 256:256 + D], ALU.add), tm)
                th = V.op(lambda e: e.tensor_tensor(HM[:, t, :], HM[:, t, :], boB[0:P, :], ALU.add), fo2)
                r, ssq = r1[:, t:t + 1], sso[:, t:t + 1]
                ta = A.op(lambda e: e.activation(jk, HM[:, t, :], ACT.Square, accum_out=ssq), th, A.now)
                t1 = V.op(lambda e: e.tensor_tensor(X[:, t, :], X[:, t, :], HM[:, t, :], ALU.add), th)
                yield
                t2 = V.op(lambda e: e.tensor_scalar(r, ssq, 1.0 / D, 1e-6, ALU.mult, ALU.add), ta)
                ta = A.op(lambda e: e.activation(r, r, ACT.Sqrt), t2)
                yield
                t2 = V.op(lambda e: e.reciprocal(r, r), ta)
                t2 = V.op(lambda e: e.scalar_tensor_tensor(HM[:, t, :], HM[:, t, :], r, wn2[0:P, :], ALU.mult, ALU.mult),
                          t1, t2)
                V.op(lambda e: e.tensor_tensor(X[:, t, :], X[:, t, :], HM[:, t, :], ALU.add), t2)
                yield

        run((pass2(), NS + 1), (mixer1(), 326))
        barrier()

        s7 = Arena(g1_own)
        rec1 = s7.get(C, 5)
        SC = s7.get(C, 4)
        tsc = c_r.dma(S, SC, sc_d[0:EP, :].rearrange("(p c) h -> p c h", p=128))
        tc = V.op(lambda e: e.tensor_copy(rec1[:, :, 0], dstF))
        tx = softmax(lambda h: SC[:, :, h], lambda h: rec1[:, :, 1 + h], dstF, s7, 4, [tc, tsc])
        trec = c_r.dma(S, rec1_d.rearrange("(p c) f -> p c f", p=128), rec1, tx, tc)
        barrier()
        s7 = Arena(g1_own)
        acc1 = s7.get(NT, RW, parts=P)
        tz = V.op(lambda e: e.memset(acc1, 0.0))
        vw = [s7.get(4, RW) for _ in range(3)]
        rvw = Ring(vw)

        def make1(M, dd, rb_, qb_, td, tin):
            i, w, f = rvw.take()
            t1 = V.op(lambda e: e.tensor_tensor(M, bc(iota[:, 0:P], 1, 4), bc(dd, 2, P), ALU.is_equal), td)
            t2 = A.op(lambda e: e.activation(w[:, :, D:RW], qb_[:, :, 1:5], ACT.Copy), tin, f)
            tv = [E_.op(lambda e: e.tensor_tensor(w[:, i0:i1, 0:D].rearrange("p i (h d) -> p i h d", h=4),
                                                  rb_[:, i0:i1, :].rearrange("p i (h d) -> p i h d", h=4),
                                                  bc(qb_[:, i0:i1, 1:5], 3, 64), ALU.mult), tin, f)
                  for E_, i0, i1 in ((G, 0, 3), (V, 3, 4))]
            rvw.free[i] = (T.sem, T.n + 4)
            return M, (lambda k: w[:, k, :]), [t1, t2, tv]

        last = steps(acc1, vs_d, rec1_d, D, 5, make1, s7, tz, True)
        den = s7.get(NT, 4, parts=P)
        AL = s7.get(2, 1024)
        skB = s7.get(4)
        ag = [s7.get(D, parts=P) for _ in range(3)]
        agT = [s7.get(2, P) for _ in range(3)]
        c_a = chan()
        for kc in range(2):
            c_a.dma(A, AL[:, kc, :].rearrange("p (t n) -> p t n", t=4),
                    I["a_lin"][:, 128 * kc:128 * kc + 128, :].rearrange("t p n -> p t n"))
        c_a.dma(A, skB, rowb(I["skip"], 0, 4))
        ts = A.op(lambda e: e.activation(skB, skB, ACT.Sigmoid), c_a.now)
        for a in range(4):
            tsk = V.op(lambda e, a=a: e.tensor_scalar(mk[:, a, :], mk[:, a, :], skB[0:P, a:a + 1], None, ALU.mult), ts)
        t = V.chain([
            lambda e: e.tensor_scalar(den, acc1[:, :, D:RW], 1e-30, None, ALU.max),
            lambda e: e.reciprocal(den, den),
        ], last)
        rg, rt = Ring(ag), Ring(agT)
        rb = Ring(bank[4:6])
        rm = Ring(bank[0:4])
        T.wait(last)
        ats = {}

        def pre(m):
            i, a_, f = rg.take()
            t1 = V.op(lambda e: e.tensor_tensor(
                a_.rearrange("p (h d) -> p h d", h=4), acc1[:, m, 0:D].rearrange("p (h d) -> p h d", h=4),
                bc(den[:, m, :], 2, 64), ALU.mult), t, f)
            return i, a_, t1

        def turn_a(m, i, a_, t1):
            ib, b, fb = rb.take()
            for k in range(2):
                tp = T.op(lambda e: e.transpose(b[:, k * P:(k + 1) * P], a_[:, 128 * k:128 * k + 128], ident[0:P, 0:P]),
                          t1, fb)
            rg.free[i] = tp
            it, at, ft = rt.take()
            ta = A.op(lambda e: e.activation(at, b[:, 0:2 * P].rearrange("p (k n) -> p k n", k=2), ACT.Copy), tp, ft)
            rb.free[ib] = ta
            ats[m] = (it, at, ta)

        def post(m):
            it, at, ta = ats.pop(m)
            tv = None
            for half in range(2):
                im, ps, fm = rm.take()
                for k in range(2):
                    tm = T.op(lambda e: e.matmul(ps[0:P, :], at[:, k, :], AL[:, k, 512 * half:512 * half + 512],
                                                 start=k == 0, stop=k == 1), ta, fm, c_a.now)
                for a in range(2):
                    tv = V.op(lambda e: e.scalar_tensor_tensor(
                        X[:, m, :], ps[0:P, D * a:D * a + D], mk[:, 2 * half + a, m:m + 1], X[:, m, :], ALU.mult, ALU.add),
                        tm, tsk, tv)
                rm.free[im] = tv
            rt.free[it] = tm
            return tv

        def both(m):
            nxt = pre(m + 2) if m + 2 < NT else None
            tv = post(m)
            if nxt:
                turn_a(m + 2, *nxt)
            return tv

        turn_a(0, *pre(0))
        turn_a(1, *pre(1))
        Y = mem[0:P, BASE:BASE + NT * D].rearrange("p (t d) -> p t d", d=D)
        ty = ln_pipe(Y, X, 1e-5, both)
        barrier()

        f1 = Arena(BASE + NT * D)
        c_o = chan()
        out_v = out.rearrange("(t p) d -> p t d", p=P)

        def finish1(k, acc, tok):
            a, b = GRP[k][0], GRP[k][-1] + 1
            c_o.dma125(S, out_v[:, a:b, :], acc[:, a:b, :], tok)

        experts(f1, 8, Y, ty, X, I["f1_w"], I["f1_b2"], I["f1_gw"], I["f1_gb"], ACT.Gelu, False, finish1)
        S.wait(c_o.now)
        barrier()


def kernel(**a):
    import concourse.bacc as bacc
    from concourse.bass_utils import run_bass_kernel_spmd

    def arr(v):
        return np.ascontiguousarray(np.asarray(v))

    a = {k: np.asarray(v) for k, v in a.items()}

    def edges(v, fill):
        w = np.full(EP, fill, v.dtype)
        w[:E] = v
        return w.reshape(128, C)

    def experts(w1, b1, w2):
        n = len(w1)
        return np.concatenate([w1.reshape(n, 2, 128, 512).transpose(0, 2, 1, 3).reshape(n, 128, 1024),
                               w2.reshape(n, 4, 128, D).transpose(0, 2, 1, 3).reshape(n, 128, 1024),
                               b1.reshape(n, 4, 128).transpose(0, 2, 1)], 2)

    perm = np.array([96 * (b % 8) + 32 * (b // 8) + i for b in range(24) for i in range(32)])
    p = np.arange(128)
    feeds = {
        "x": a["x"], "src": edges(a["src"], 0), "dst": edges(a["dst"], PADN), "etype": edges(a["edge_type_8"], 0),
        "edge_attr": a["edge_attr_128"], "ntype": a["node_type_4"].reshape(NT, P).T,
        "c_ident": np.eye(128, dtype=np.float32),
        "c_nid": np.arange(2 * N, dtype=np.int32).reshape(2, NT, P).transpose(2, 0, 1),
        "c_pid": p[:, None].astype(np.float32), "c_tri": (p[:, None] < p[None, :]).astype(np.float32),
        "c_iota": np.tile(np.arange(128, dtype=np.float32), (128, 1)),
        "c_blk": (p[:, None] // 32 == p[None, :] // 32).astype(np.float32),
        "c_hm4": (p[:, None] // 32 == np.arange(4)[None, :]).astype(np.float32),
        "c_steps": np.tile(np.arange(NS, dtype=np.float32), (128, 1)),
        "WnT": a["L0_gnn_Wn"].T, "bn": a["L0_gnn_bn"],
        "WeB": np.concatenate([a["L0_gnn_We"], a["L0_gnn_be"][:, None]], 1),
        "attn": a["L0_gnn_attn"].reshape(D), "attnC": a["L0_gnn_attn"].reshape(2, 128).T,
        "w_qkv": a["L0_mix_w_qkv"][perm][:, :, 2].T,
        "bn_gamma": a["L0_mix_bn_gamma"][perm].reshape(6, 128).T, "bn_beta": a["L0_mix_bn_beta"][perm].reshape(6, 128).T,
        "w_dw": a["L0_mix_w_dw"][perm][:, 0, 2].reshape(6, 128).T,
        "w_pw": a["L0_mix_w_pw"][perm].reshape(6, 4, 32, 32).transpose(1, 3, 0, 2),
        "w_res": a["L0_mix_w_res"][:, :, 0].T, "b_res": a["L0_mix_b_res"],
        "f0_gw": a["L0_ffn_gate_w"], "f0_gb": a["L0_ffn_gate_b"], "f0_w": experts(a["L0_ffn_w1"], a["L0_ffn_b1"], a["L0_ffn_w2"]),
        "f0_b2": a["L0_ffn_b2"],
        "f0_gamma": a["L0_ffn_gamma"], "f0_beta": a["L0_ffn_beta"],
        "k_lin": a["L1_gnn_k_linears"], "q_lin": a["L1_gnn_q_linears"], "v_lin": a["L1_gnn_v_linears"],
        "a_lin": a["L1_gnn_a_linears"], "pri": a["L1_gnn_relation_pri"].reshape(32), "skip": a["L1_gnn_skip"],
        "att": a["L1_gnn_relation_att"].transpose(1, 3, 0, 2), "msg": a["L1_gnn_relation_msg"].transpose(1, 2, 0, 3),
        "m1_wqkv": a["L1_mix_w_qkv"], "m1_wout": a["L1_mix_w_out"], "m1_bout": a["L1_mix_b_out"],
        "m1_wn1": a["L1_mix_w_norm1"].reshape(2, 128).T, "m1_wn2": a["L1_mix_w_norm2"],
        "f1_gw": a["L1_ffn_Wg"], "f1_gb": a["L1_ffn_bg"], "f1_w": experts(a["L1_ffn_W1"], a["L1_ffn_b1"], a["L1_ffn_W2"]),
        "f1_b2": a["L1_ffn_b2"],
    }
    nc = bacc.Bacc("TRN2", target_bir_lowering=False, num_devices=1)
    arrays, ins = {}, {}
    for name, v in feeds.items():
        v = arr(v)
        arrays["in_" + name] = v
        ins[name] = nc.dram_tensor("in_" + name, v.shape, mybir.dt.from_np(v.dtype), kind="ExternalInput").ap()
    out = nc.dram_tensor("out_0", (N, D), F32, kind="ExternalOutput").ap()
    build(nc, ins, out)
    r = run_bass_kernel_spmd(nc, [arrays], core_ids=[0])
    return r.results[0]["out_0"]
```
